# Optimizing a Trainium2 kernel written in Bass

```python
import numpy as np
import jax
import jax.numpy as jnp

def _softmax(x, axis=-1):
    return jax.nn.softmax(x, axis=axis)

def _gelu(x):
    return jax.nn.gelu(x, approximate=True)

def _silu(x):
    return jax.nn.silu(x)

def _sigmoid(x):
    return jax.nn.sigmoid(x)

def _layernorm(x, axis=-1, eps=1e-05):
    m = jnp.mean(x, axis=axis, keepdims=True)
    v = jnp.var(x, axis=axis, keepdims=True)
    return (x - m) / jnp.sqrt(v + eps)

def _scatter_add(tgt, idx, src, axis=0):
    return tgt.at[idx].add(src)

def _segment_sum(src, seg, n):
    return jax.ops.segment_sum(src, seg, n)
kernel_name = 'mk_recurrent_d2_jaxref_r8_6f845b'

def setup_inputs(seed: int=0):
    np.random.seed(seed)
    _w = jnp.asarray

    def _L0_attn_setup():
        import jax, jax.numpy as jnp
        import numpy as np
        B, T, D, H = (2, 256, 256, 16)
        HD = D // H
        key = jax.random.key(seed)
        ks = jax.random.split(key, 6)
        s = 1.0 / np.sqrt(D)
        return {'x': jax.random.normal(ks[0], (B, T, D), dtype=jnp.float32), 'Wq': jax.random.normal(ks[1], (D, D), dtype=jnp.float32) * s, 'Wk': jax.random.normal(ks[2], (D, D), dtype=jnp.float32) * s, 'Wv': jax.random.normal(ks[3], (D, D), dtype=jnp.float32) * s, 'Wo': jax.random.normal(ks[4], (D, D), dtype=jnp.float32) * s, 'bo': jnp.zeros((D,), dtype=jnp.float32)}
    _L0_attn_in = _L0_attn_setup()

    def _L0_ffn_setup():
        import jax, jax.numpy as jnp
        import numpy as np
        BLOCK_SIZE = 32
        HIDDEN_SIZE = 256
        MLP_DIM = 2048
        NVFP4_LUT = jnp.array([0.0, 0.5, 1.0, 1.5, 2.0, 3.0, 4.0, 6.0, 0.0, -0.5, -1.0, -1.5, -2.0, -3.0, -4.0, -6.0], dtype=jnp.float32)

        def dequant_nvfp4(W_packed, scales, block=BLOCK_SIZE):
            N = W_packed.shape[0]
            low = W_packed & 15
            high = W_packed >> 4 & 15
            idx = jnp.stack([low, high], axis=-1).reshape(N, -1)
            vals = NVFP4_LUT[idx]
            K = vals.shape[1]
            vals = vals.reshape(N, K // block, block) * scales[:, :, None]
            return vals.reshape(N, K)
        key = jax.random.key(seed)
        ks = jax.random.split(key, 7)
        x = jax.random.normal(ks[0], (4, 32, HIDDEN_SIZE), dtype=jnp.float32)
        gate_W_packed = jax.random.randint(ks[1], (MLP_DIM, HIDDEN_SIZE // 2), 0, 32, dtype=jnp.int32)
        gate_scales = jax.random.uniform(ks[2], (MLP_DIM, HIDDEN_SIZE // BLOCK_SIZE), dtype=jnp.float32) * 0.1 + 0.001
        up_W_packed = jax.random.randint(ks[3], (MLP_DIM, HIDDEN_SIZE // 2), 0, 32, dtype=jnp.int32)
        up_scales = jax.random.uniform(ks[4], (MLP_DIM, HIDDEN_SIZE // BLOCK_SIZE), dtype=jnp.float32) * 0.1 + 0.001
        down_W_packed = jax.random.randint(ks[5], (HIDDEN_SIZE, MLP_DIM // 2), 0, 32, dtype=jnp.int32)
        down_scales = jax.random.uniform(ks[6], (HIDDEN_SIZE, MLP_DIM // BLOCK_SIZE), dtype=jnp.float32) * 0.1 + 0.001
        return {'x': x, 'gate_W_packed': gate_W_packed, 'gate_scales': gate_scales, 'up_W_packed': up_W_packed, 'up_scales': up_scales, 'down_W_packed': down_W_packed, 'down_scales': down_scales}
    _L0_ffn_in = _L0_ffn_setup()

    def _L1_attn_setup():
        import jax, jax.numpy as jnp
        import numpy as np
        B, T, D_MODEL = (4, 256, 256)
        NUM_HEADS, HEAD_SIZE = (16, 128)
        MODEL_SIZE = 256
        key = jax.random.key(seed)
        ks = jax.random.split(key, 9)
        s = 0.02 / np.sqrt(D_MODEL)
        so = 0.02 / np.sqrt(NUM_HEADS * HEAD_SIZE)
        return {'query': jax.random.normal(ks[0], (B, T, D_MODEL), jnp.float32), 'w_q': jax.random.normal(ks[1], (D_MODEL, NUM_HEADS * HEAD_SIZE), jnp.float32) * s, 'b_q': jnp.zeros((NUM_HEADS * HEAD_SIZE,), jnp.float32), 'w_k': jax.random.normal(ks[2], (D_MODEL, NUM_HEADS * HEAD_SIZE), jnp.float32) * s, 'b_k': jnp.zeros((NUM_HEADS * HEAD_SIZE,), jnp.float32), 'w_v': jax.random.normal(ks[3], (D_MODEL, NUM_HEADS * HEAD_SIZE), jnp.float32) * s, 'b_v': jnp.zeros((NUM_HEADS * HEAD_SIZE,), jnp.float32), 'w_o': jax.random.normal(ks[4], (NUM_HEADS * HEAD_SIZE, MODEL_SIZE), jnp.float32) * so, 'b_o': jnp.zeros((MODEL_SIZE,), jnp.float32)}
    _L1_attn_in = _L1_attn_setup()

    def _L1_ffn_setup():
        import jax, jax.numpy as jnp
        import numpy as np
        DIM = 256
        INTER = 176
        E = 16
        TOPK = 4
        G = 4
        TOPK_G = 2
        N_SHARED = 2
        ROUTE_SCALE = 1.0
        INIT_STD = 0.02
        B, S = (1, 256)
        key = jax.random.key(seed)
        ks = jax.random.split(key, 9)
        std = INIT_STD
        x = jax.random.normal(ks[0], (B, S, DIM), jnp.float32)
        gate_w = jax.random.normal(ks[1], (E, DIM), jnp.float32) * std
        expert_bias = jnp.zeros((E,), jnp.float32)
        w1 = jax.random.normal(ks[2], (E, DIM, INTER), jnp.float32) * std
        w3 = jax.random.normal(ks[3], (E, DIM, INTER), jnp.float32) * std
        w2 = jax.random.normal(ks[4], (E, INTER, DIM), jnp.float32) * std
        sh = N_SHARED * INTER
        sw1 = jax.random.normal(ks[5], (DIM, sh), jnp.float32) * std
        sw3 = jax.random.normal(ks[6], (DIM, sh), jnp.float32) * std
        sw2 = jax.random.normal(ks[7], (sh, DIM), jnp.float32) * std
        return {'x': x, 'gate_w': gate_w, 'expert_bias': expert_bias, 'w1': w1, 'w2': w2, 'w3': w3, 'sw1': sw1, 'sw2': sw2, 'sw3': sw3}
    _L1_ffn_in = _L1_ffn_setup()
    _d = {'L0_attn_x': _L0_attn_in['x'], 'L0_attn_Wq': _L0_attn_in['Wq'], 'L0_attn_Wk': _L0_attn_in['Wk'], 'L0_attn_Wv': _L0_attn_in['Wv'], 'L0_attn_Wo': _L0_attn_in['Wo'], 'L0_attn_bo': _L0_attn_in['bo'], 'L0_ffn_gate_W_packed': _L0_ffn_in['gate_W_packed'], 'L0_ffn_gate_scales': _L0_ffn_in['gate_scales'], 'L0_ffn_up_W_packed': _L0_ffn_in['up_W_packed'], 'L0_ffn_up_scales': _L0_ffn_in['up_scales'], 'L0_ffn_down_W_packed': _L0_ffn_in['down_W_packed'], 'L0_ffn_down_scales': _L0_ffn_in['down_scales'], 'L1_attn_w_q': _L1_attn_in['w_q'], 'L1_attn_b_q': _L1_attn_in['b_q'], 'L1_attn_w_k': _L1_attn_in['w_k'], 'L1_attn_b_k': _L1_attn_in['b_k'], 'L1_attn_w_v': _L1_attn_in['w_v'], 'L1_attn_b_v': _L1_attn_in['b_v'], 'L1_attn_w_o': _L1_attn_in['w_o'], 'L1_attn_b_o': _L1_attn_in['b_o'], 'L1_ffn_gate_w': _L1_ffn_in['gate_w'], 'L1_ffn_expert_bias': _L1_ffn_in['expert_bias'], 'L1_ffn_w1': _L1_ffn_in['w1'], 'L1_ffn_w2': _L1_ffn_in['w2'], 'L1_ffn_w3': _L1_ffn_in['w3'], 'L1_ffn_sw1': _L1_ffn_in['sw1'], 'L1_ffn_sw2': _L1_ffn_in['sw2'], 'L1_ffn_sw3': _L1_ffn_in['sw3']}
    _x0 = _d['L0_attn_x']
    _d['L0_attn_x'] = jax.random.normal(jax.random.fold_in(jax.random.key(seed), 1), (4, 512, 256), dtype=_x0.dtype)
    del _x0
    return _d

def reference(L0_attn_x, L0_attn_Wq, L0_attn_Wk, L0_attn_Wv, L0_attn_Wo, L0_attn_bo, L0_ffn_gate_W_packed, L0_ffn_gate_scales, L0_ffn_up_W_packed, L0_ffn_up_scales, L0_ffn_down_W_packed, L0_ffn_down_scales, L1_attn_w_q, L1_attn_b_q, L1_attn_w_k, L1_attn_b_k, L1_attn_w_v, L1_attn_b_v, L1_attn_w_o, L1_attn_b_o, L1_ffn_gate_w, L1_ffn_expert_bias, L1_ffn_w1, L1_ffn_w2, L1_ffn_w3, L1_ffn_sw1, L1_ffn_sw2, L1_ffn_sw3):

    def _L0_attn_ref(x, Wq, Wk, Wv, Wo, bo):
        import jax, jax.numpy as jnp
        import numpy as np
        B, T, D, H = (2, 256, 256, 16)
        HD = D // H
        b, t, d = x.shape
        q = (x @ Wq.T).reshape(b, t, H, HD).transpose(0, 2, 1, 3)
        k = (x @ Wk.T).reshape(b, t, H, HD).transpose(0, 2, 1, 3)
        v = (x @ Wv.T).reshape(b, t, H, HD).transpose(0, 2, 1, 3)
        scores = jnp.einsum('bhid,bhjd->bhij', q, k) / np.sqrt(HD)
        causal = jnp.tril(jnp.ones((t, t), dtype=bool))
        scores = jnp.where(causal[None, None], scores, -jnp.inf)
        attn = jax.nn.softmax(scores, axis=-1)
        out = jnp.einsum('bhij,bhjd->bhid', attn, v)
        out = out.transpose(0, 2, 1, 3).reshape(b, t, d)
        return out @ Wo.T + bo

    def _L0_ffn_ref(x, gate_W_packed, gate_scales, up_W_packed, up_scales, down_W_packed, down_scales):
        import jax, jax.numpy as jnp
        import numpy as np
        BLOCK_SIZE = 32
        HIDDEN_SIZE = 256
        MLP_DIM = 2048
        NVFP4_LUT = jnp.array([0.0, 0.5, 1.0, 1.5, 2.0, 3.0, 4.0, 6.0, 0.0, -0.5, -1.0, -1.5, -2.0, -3.0, -4.0, -6.0], dtype=jnp.float32)

        def dequant_nvfp4(W_packed, scales, block=BLOCK_SIZE):
            N = W_packed.shape[0]
            low = W_packed & 15
            high = W_packed >> 4 & 15
            idx = jnp.stack([low, high], axis=-1).reshape(N, -1)
            vals = NVFP4_LUT[idx]
            K = vals.shape[1]
            vals = vals.reshape(N, K // block, block) * scales[:, :, None]
            return vals.reshape(N, K)
        B, S, H = x.shape
        xt = x.reshape(B * S, H)
        Wg = dequant_nvfp4(gate_W_packed, gate_scales)
        Wu = dequant_nvfp4(up_W_packed, up_scales)
        Wd = dequant_nvfp4(down_W_packed, down_scales)
        gate = jnp.einsum('th,nh->tn', xt, Wg)
        up = jnp.einsum('th,nh->tn', xt, Wu)
        gelu = jnp.tanh(0.7978845608028654 * (gate + 0.044715 * gate ** 3)) * gate * 0.5 + gate * 0.5
        inter = gelu * up
        out = jnp.einsum('tn,hn->th', inter, Wd)
        return out.reshape(B, S, H)

    def _L1_attn_ref(query, w_q, b_q, w_k, b_k, w_v, b_v, w_o, b_o):
        import jax, jax.numpy as jnp
        import numpy as np
        B, T, D_MODEL = (4, 256, 256)
        NUM_HEADS, HEAD_SIZE = (16, 128)
        MODEL_SIZE = 256
        B_, T_, _ = query.shape
        q = (query @ w_q + b_q).reshape(B_, T_, NUM_HEADS, HEAD_SIZE)
        k = (query @ w_k + b_k).reshape(B_, T_, NUM_HEADS, HEAD_SIZE)
        v = (query @ w_v + b_v).reshape(B_, T_, NUM_HEADS, HEAD_SIZE)
        logits = jnp.einsum('bthd,bThd->bhtT', q, k) * jax.lax.rsqrt(jnp.float32(HEAD_SIZE))
        i = jnp.arange(T_, dtype=jnp.int32)[:, None]
        j = jnp.arange(T_, dtype=jnp.int32)
        mask = (i >= j).astype(logits.dtype)
        logits = logits - 10000000000.0 * (1.0 - mask)
        weights = jax.nn.softmax(logits, axis=-1)
        attn = jnp.einsum('bhtT,bThd->bthd', weights, v).reshape(B_, T_, NUM_HEADS * HEAD_SIZE)
        out = attn @ w_o + b_o
        return out

    def _L1_ffn_ref(x, gate_w, expert_bias, w1, w2, w3, sw1, sw2, sw3):
        import jax, jax.numpy as jnp
        import numpy as np
        DIM = 256
        INTER = 176
        E = 16
        TOPK = 4
        G = 4
        TOPK_G = 2
        N_SHARED = 2
        ROUTE_SCALE = 1.0
        INIT_STD = 0.02
        B, S = (1, 256)
        b, s, d = x.shape
        T = b * s
        xf = x.reshape(T, d)
        scores = jax.nn.sigmoid(xf @ gate_w.T)
        original_scores = scores
        scores = scores + expert_bias
        sg = scores.reshape(T, G, E // G)
        group_scores = sg.max(axis=-1)
        _, gidx = jax.lax.top_k(group_scores, TOPK_G)
        gmask = jnp.zeros((T, G), bool).at[jnp.arange(T)[:, None], gidx].set(True)
        masked = jnp.where(gmask[:, :, None], sg, -jnp.inf).reshape(T, E)
        _, idx = jax.lax.top_k(masked, TOPK)
        w = jnp.take_along_axis(original_scores, idx, axis=1)
        w = w / jnp.sum(w, axis=-1, keepdims=True)
        w = w * ROUTE_SCALE
        cw = jnp.zeros((T, E), x.dtype).at[jnp.arange(T)[:, None], idx].add(w)
        h = jax.nn.silu(jnp.einsum('td,edh->teh', xf, w1)) * jnp.einsum('td,edh->teh', xf, w3)
        y = jnp.einsum('teh,ehd,te->td', h, w2, cw)
        z = jax.nn.silu(xf @ sw1) * (xf @ sw3) @ sw2
        return (y + z).reshape(b, s, d)
    x = L0_attn_x
    xn = _layernorm(x, axis=-1)
    s = _L0_attn_ref(xn, L0_attn_Wq, L0_attn_Wk, L0_attn_Wv, L0_attn_Wo, L0_attn_bo)
    g = _silu(_L0_ffn_ref(xn, L0_ffn_gate_W_packed, L0_ffn_gate_scales, L0_ffn_up_W_packed, L0_ffn_up_scales, L0_ffn_down_W_packed, L0_ffn_down_scales))
    x = x + s * g
    xn = _layernorm(x, axis=-1)
    s = _L1_attn_ref(xn, L1_attn_w_q, L1_attn_b_q, L1_attn_w_k, L1_attn_b_k, L1_attn_w_v, L1_attn_b_v, L1_attn_w_o, L1_attn_b_o)
    g = _silu(_L1_ffn_ref(xn, L1_ffn_gate_w, L1_ffn_expert_bias, L1_ffn_w1, L1_ffn_w2, L1_ffn_w3, L1_ffn_sw1, L1_ffn_sw2, L1_ffn_sw3))
    x = x + s * g
    return x

_drawn_inputs = setup_inputs


def setup_inputs(seed=0):
    import zlib

    import numpy as np

    out = dict(_drawn_inputs(seed))
    spreads = {'L0_attn_bo': (0.0, 0.1),
     'L1_attn_b_q': (0.0, 2.0),
     'L1_attn_b_k': (0.0, 0.8),
     'L1_attn_b_v': (0.0, 0.8),
     'L1_attn_b_o': (0.0, 0.8),
     'L1_ffn_expert_bias': (0.0, 0.8)}
    factors = {'L1_attn_w_q': 64.0,
     'L1_attn_w_k': 64.0,
     'L1_attn_w_v': 47.669,
     'L1_attn_w_o': 8.0,
     'L1_ffn_gate_w': 8.0,
     'L1_ffn_w1': 8.0,
     'L1_ffn_w2': 8.0,
     'L1_ffn_w3': 8.0,
     'L1_ffn_sw1': 8.0,
     'L1_ffn_sw2': 8.0,
     'L1_ffn_sw3': 8.0}
    for name, (base, spread) in spreads.items():
        noise = np.random.default_rng([zlib.crc32(name.encode()), seed]).standard_normal(out[name].shape)
        drawn = base * np.exp(spread * noise) if base else spread * noise
        out[name] = jnp.asarray(drawn.astype(out[name].dtype))
    for name, factor in factors.items():
        out[name] = (out[name] * factor).astype(out[name].dtype)
    return out
```

```python
from contextlib import ExitStack

import concourse.bass as bass
import numpy as np
from concourse import mybir

F32 = mybir.dt.float32
F16 = mybir.dt.float16
BF16 = mybir.dt.bfloat16
I32 = mybir.dt.int32
FP8 = mybir.dt.float8e3
ALU = mybir.AluOpType
ACT = mybir.ActivationFunctionType
AX = mybir.AxisListType
ds = bass.ds

P = 128
B, T, D = 4, 512, 256
TOK = B * T
NT = TOK // P
TPB = T // P
DC = D // P
H0, HD0 = 16, 16
H1, HD1 = 16, 128
MLP = 2048
NCH0 = MLP // P
E, TOPK, G, TOPK_G = 16, 4, 4, 2
EG = E // G
INTER, SHARED = 176, 352
HID1 = 3200
NCH1 = HID1 // P
EPS = 1e-5
MASKED = -1e30
GELU_C, GELU_K = 0.044715, 0.7978845608028654
HEADS = 4
VG = 640
SMAX = [(3, 0), (2, 512), (1, 896), (0, 1152)]
PW = 1280
TFILLS = [([0], 0, 1024), ([1], 1024, 768), ([2, 3], 1792, 768)]


def key_columns():
    where, at = {}, 0
    for blocks, _, _ in TFILLS:
        for kb in blocks:
            w = (TPB - kb) * P
            where[kb] = (at, at + w, w)
            at += 2 * w
    return where


KEYCOL = key_columns()
PCOL = dict(SMAX)


class Count:

    def __init__(self, sem):
        self.sem, self.n = sem, 0

    def __call__(self, ins, by=1):
        ins.then_inc(self.sem, by)
        self.n += by
        return ins

    def wait(self, engine):
        engine.wait_ge(self.sem, self.n)


def split_product(pe, out, lhs, rhs, start, stop):
    mm = None
    n = len(lhs)
    for c in range(n):
        for i, (a, b) in enumerate(((0, 0), (0, 1), (1, 0))):
            mm = pe.matmul(out, lhs[c][a], rhs[c][b], start=start and c == 0 and i == 0,
                           stop=stop and c == n - 1 and i == 2, skip_group_check=True)
    return mm


def layer_norm(nc, ctx, tag, x, xT, ident, eps_tile, psum, interleaved):
    sb = lambda n, s, d: ctx.enter_context(nc.sbuf_tensor(f"{n}_{tag}", s, d))
    sem = lambda n: ctx.enter_context(nc.semaphore(f"{n}_{tag}"))
    stats = sb("stats", [P, NT, 6], F32)
    mv = sb("mv", [P, NT, 2], F32)
    std = sb("std", [P, NT], F32)
    rstd = sb("rstd", [P, NT], F32)
    xn = sb("xn", [P, 2, D], F32)
    parts = sb("xn_parts", [P, 2, 2, DC, P], F16)
    stats_done, std_done, rstd_done = sem("stats_done"), sem("std_done"), sem("rstd_done")
    xn_ready, hi_ready, lo_ready = sem("xn_ready"), sem("xn_hi_ready"), sem("xn_lo_ready")
    turned, copied = sem("xn_turned"), sem("xn_copied")
    xT4 = xT.rearrange("p a c t -> p (a c) t")

    def as_parts(ap):
        return ap.rearrange("p (j c) -> p c j", c=DC) if interleaved else ap.rearrange("p (c j) -> p c j", c=DC)

    with nc.Block() as block:
        @block.scalar
        def _(act):
            act.wait_ge(stats_done, 2 * NT)
            act.activation(std[:, :], mv[:, :, 1], ACT.Sqrt, bias=eps_tile[:, 0:1]).then_inc(std_done, 1)
            with act.Fori(0, NT // 2) as i:
                for k in range(2):
                    act.wait_ge(xn_ready, i * 2 + k + 1)
                    act.wait_ge(turned, i * 2 + k + 1)
                    act.activation(parts[:, k, 0, :, :], as_parts(xn[:, k, :]), ACT.Copy).then_inc(hi_ready, 1)

        @block.vector
        def _(dve):
            for t in range(NT):
                dve.bn_stats(stats[:, t, :], x[:, t, :]).then_inc(stats_done, 1)
            dve.wait_ge(stats_done, NT)
            for t in range(NT):
                dve.bn_aggr(mv[:, t, :], stats[:, t, :]).then_inc(stats_done, 1)
            dve.wait_ge(std_done, 1)
            dve.reciprocal(rstd[:, :], std[:, :]).then_inc(rstd_done, 1)
            dve.wait_ge(rstd_done, 1)
            dve.wait_ge(stats_done, 2 * NT)

            def normalise(tile, k):
                dve.tensor_scalar(xn[:, k, :], x[:, ds(tile, 1), :].rearrange("p a d -> p (a d)"),
                                  mv[:, ds(tile, 1), 0], rstd[:, ds(tile, 1)],
                                  ALU.subtract, ALU.mult).then_inc(xn_ready, 1)

            with dve.Fori(0, NT // 2) as i:
                for k in range(2):
                    normalise(i * 2 + k, k)
                    dve.wait_ge(hi_ready, i * 2 + k + 1)
                    dve.wait_ge(xn_ready, i * 2 + k + 1)
                    dve.tensor_tensor(parts[:, k, 1, :, :], as_parts(xn[:, k, :]), parts[:, k, 0, :, :],
                                      ALU.subtract).then_inc(lo_ready, 1)
                for k in range(2):
                    dve.wait_ge(turned, i * 2 + k + 3)
                    dve.tensor_copy(xT4[:, :, ds((i * 2 + k) * P, P)],
                                    psum[k][:, :].bitcast(F16)[:, 0:4 * P].rearrange("p (a t) -> p a t", a=4)
                                    ).then_inc(copied, 1)

        @block.tensor
        def _(pe):
            pe.sem_inc(turned, 2)
            with pe.Fori(0, NT // 2) as i:
                for k in range(2):
                    pe.wait_ge(lo_ready, i * 2 + k + 1)
                    pe.wait_ge(hi_ready, i * 2 + k + 1)
                    for a in range(2):
                        for c in range(DC):
                            q = (a * DC + c) * P
                            mm = pe.transpose(psum[k][:, :].bitcast(F16)[:, q:q + P], parts[:, k, a, c, :], ident[:, :])
                    mm.then_inc(turned, 1)


def network(nc, A):
    ctx = ExitStack()
    with ctx:
        def sbp(name, shape, dt, c=ctx):
            return c.enter_context(nc.sbuf_tensor("s_" + name, shape, dt))

        x = sbp("x", [P, NT, D], F32)
        xT = sbp("xT", [P, 2, DC, TOK], F16)
        ident = sbp("ident", [P, P], F16)
        ident_b = sbp("ident_b", [P, P], BF16)
        causal = sbp("causal", [P, P], BF16)
        zeros = sbp("zeros", [P, P], F16)
        eps_tile = sbp("eps", [P, 1], F32)
        psum = [ctx.enter_context(nc.psum_tensor(f"bank{i}", [P, 512], F32)) for i in range(8)]

        ffn_ctx = ExitStack()
        ctx.enter_context(ffn_ctx)
        wffn = [sbp(f"wffn{m}", [P, 2, DC, MLP], F16, ffn_ctx) for m in range(2)]
        wdown = sbp("wdown", [P, 2, NCH0, D], F16, ffn_ctx)
        wqkv = sbp("wqkv", [P, 2, DC, 3 * D], F16, ffn_ctx)
        wo = sbp("wo", [P, 2, HEADS, D], F16, ffn_ctx)
        bo = sbp("bo", [P, D], F32, ffn_ctx)
        prepare_block0(nc, A, x, ident, ident_b, causal, zeros, eps_tile, wffn, wdown, wqkv, wo, bo)
        with ExitStack() as c:
            layer_norm(nc, c, "ln0", x, xT, ident, eps_tile, psum, True)
        block0(nc, A, x, xT, ident, ident_b, causal, zeros, wffn, wdown, wqkv, wo, bo, psum)
        ffn_ctx.close()
        with ExitStack() as c:
            layer_norm(nc, c, "ln1", x, xT, ident, eps_tile, psum, False)
        gate = sbp("gate", [P, NT, D], F32)
        experts(nc, A, xT, ident, zeros, gate, psum)
        attention1(nc, A, x, xT, ident, ident_b, causal, zeros, gate, psum)


def split_weights(nc, jobs, tag, extra=()):
    with ExitStack() as c:
        n = len(jobs)
        loaded = [c.enter_context(nc.semaphore(f"w_loaded{i}_{tag}")) for i in range(n)]
        hi_done = c.enter_context(nc.semaphore(f"w_hi_{tag}"))
        other = c.enter_context(nc.semaphore(f"w_other_{tag}"))
        with nc.Block() as block:
            @block.sync
            def _(sp):
                for i, (src, st, _, _) in enumerate(jobs):
                    sp.dma_start(st, src).then_inc(loaded[i], 16)
                for dst, src in extra:
                    sp.dma_start(dst, src).then_inc(other, 16)
                if extra:
                    sp.wait_ge(other, 16 * len(extra))

            @block.scalar
            def _(act):
                for i, (_, st, hi, _) in enumerate(jobs):
                    act.wait_ge(loaded[i], 16)
                    act.activation(hi, st, ACT.Copy).then_inc(hi_done, 1)

            def low(eng, mine):
                for i in mine:
                    _, st, hi, lo = jobs[i]
                    eng.wait_ge(loaded[i], 16)
                    eng.wait_ge(hi_done, i + 1)
                    eng.tensor_tensor(lo, st, hi, ALU.subtract)

            @block.vector
            def _(dve):
                low(dve, [i for i in range(n) if i % 3 != 2])

            @block.gpsimd
            def _(pool):
                low(pool, [i for i in range(n) if i % 3 == 2])


def prepare_block0(nc, A, x, ident, ident_b, causal, zeros, eps_tile, wffn, wdown, wqkv, wo, bo):
    with ExitStack() as c:
        sb = lambda n, s, d: c.enter_context(nc.sbuf_tensor("p0_" + n, s, d))
        sem = lambda n: c.enter_context(nc.semaphore("p0_" + n))
        codes = [sb(f"codes{m}", [P, MLP], I32) for m in range(3)]
        scales = [sb(f"scales{m}", [P, MLP], F32) for m in range(3)]
        mag = sb("mag", [P, MLP], I32)
        sign = sb("sign", [P, MLP], I32)
        byte = sb("byte", [P, 2, MLP], I32)
        w32 = sb("w32", [P, 2, MLP], F32)
        qst = sb("qst", [P, DC, 3 * D], F32)
        ost = sb("ost", [P, HEADS, D], F32)
        loaded = [sem(f"fp4_loaded{m}") for m in range(3)]
        loaded_q, other, made = sem("qkvo_loaded"), sem("other_loaded"), sem("constants_made")
        bits, w_ready, hi_ready, lo_ready = sem("bits"), sem("w_ready"), sem("w_hi_ready"), sem("w_lo_ready")
        lo_q = sem("q_lo")

        def target(m, nib):
            if m < 2:
                return wffn[m][:, 0, nib, :], wffn[m][:, 1, nib, :]
            v = wdown[:, :, :, :].rearrange("p a (j n) d -> p a n j d", n=2)
            return v[:, 0, nib, :, :], v[:, 1, nib, :, :]

        def shaped(m, ap):
            return ap if m < 2 else ap.rearrange("p (j d) -> p j d", d=D)

        with nc.Block() as block:
            @block.sync
            def _(sp):
                for m in range(3):
                    sp.dma_start(codes[m][:, :], A[f"codes{m}"]).then_inc(loaded[m], 16)
                    sp.dma_start(scales[m][:, :], A[f"scales{m}"]).then_inc(loaded[m], 16)
                sp.dma_start(x[:, :, :], A["x"].rearrange("(t p) d -> p t d", p=P)).then_inc(other, 16)
                sp.dma_start(bo[:, :], A["bo0"].broadcast_to([P, D])).then_inc(other, 16)
                sp.wait_ge(other, 2 * 16)

            @block.scalar
            def _(act):
                act.dma_start(qst[:, :, :], A["wqkv0"].rearrange("(c p) n -> p c n", p=P)).then_inc(loaded_q, 16)
                act.dma_start(ost[:, :, :], A["wo0"].rearrange("g p n -> p g n")).then_inc(loaded_q, 16)
                act.wait_ge(loaded_q, 32)
                act.activation(wqkv[:, 0, :, :], qst[:, :, :], ACT.Copy).then_inc(hi_ready, 1)
                act.activation(wo[:, 0, :, :], ost[:, :, :], ACT.Copy).then_inc(hi_ready, 1)
                for m in range(3):
                    for nib in range(2):
                        act.wait_ge(w_ready, 2 * m + nib + 1)
                        act.activation(target(m, nib)[0], shaped(m, w32[:, nib, :]), ACT.Copy).then_inc(hi_ready, 1)

            @block.gpsimd
            def _(pool):
                pool.memset(zeros[:, :], 0.0)
                pool.memset(eps_tile[:, :], EPS)
                for m in (ident, ident_b, causal):
                    pool.memset(m[:, :], 0.0).then_inc(made, 1)
                pool.wait_ge(made, 3)
                for m in (ident, ident_b):
                    pool.affine_select(out=m[:, :], in_=m[:, :], compare_op=ALU.not_equal, fill=1.0, base=0,
                                       pattern=[[-1, P]], channel_multiplier=1)
                pool.affine_select(out=causal[:, :], in_=causal[:, :], compare_op=ALU.is_ge, fill=MASKED, base=0,
                                   pattern=[[-1, P]], channel_multiplier=1)
                pool.wait_ge(loaded_q, 32)
                pool.wait_ge(hi_ready, 2)
                pool.tensor_tensor(wqkv[:, 1, :, :], qst[:, :, :], wqkv[:, 0, :, :], ALU.subtract)
                pool.tensor_tensor(wo[:, 1, :, :], ost[:, :, :], wo[:, 0, :, :], ALU.subtract)
                for m in range(3):
                    for nib in range(2):
                        pool.wait_ge(w_ready, 2 * m + nib + 1)
                        pool.wait_ge(hi_ready, 2 * m + nib + 3)
                        hi, lo = target(m, nib)
                        pool.tensor_tensor(lo, shaped(m, w32[:, nib, :]), hi, ALU.subtract).then_inc(lo_ready, 1)

            @block.vector
            def _(dve):
                done = Count(bits)
                for m in range(3):
                    cd = codes[m][:, :]
                    dve.wait_ge(loaded[m], 32)
                    done(dve.tensor_scalar(mag[:, :], cd, 7, 3, ALU.bitwise_and, ALU.logical_shift_left))
                    done(dve.tensor_scalar(sign[:, :], cd, 4, 128, ALU.logical_shift_left, ALU.bitwise_and))
                    done.wait(dve)
                    done(dve.tensor_tensor(byte[:, 0, :], mag[:, :], sign[:, :], ALU.bitwise_or))
                    done.wait(dve)
                    done(dve.tensor_scalar(mag[:, :], cd, 1, 56, ALU.logical_shift_right, ALU.bitwise_and))
                    done(dve.tensor_scalar(sign[:, :], cd, 128, None, ALU.bitwise_and))
                    done.wait(dve)
                    done(dve.tensor_tensor(byte[:, 1, :], mag[:, :], sign[:, :], ALU.bitwise_or))
                    done.wait(dve)
                    for nib in range(2):
                        if m:
                            dve.wait_ge(lo_ready, 2 * (m - 1) + nib + 1)
                        dve.scalar_tensor_tensor(out=w32[:, nib, :],
                                                 in0=byte[:, nib, :].bitcast(FP8)[:, 0:4 * MLP:4], scalar=4.0,
                                                 in1=scales[m][:, :], op0=ALU.mult, op1=ALU.mult).then_inc(w_ready, 1)
                    dve.wait_ge(w_ready, 2 * m + 2)


def block0(nc, A, x, xT, ident, ident_b, causal, zeros, wffn, wdown, wqkv, wo, bo, psum):
    SC = HD0 ** -0.5
    STK = 48
    with ExitStack() as c:
        sb = lambda n, s, d: c.enter_context(nc.sbuf_tensor("b0_" + n, s, d))
        sem = lambda n: c.enter_context(nc.semaphore("b0_" + n))
        raw = sb("raw", [P, 2, 4, T], F16)
        qs = sb("qs", [P, H0, T], F16)
        ks = sb("ks", [P, H0, T], F16)
        vm = sb("vm", [P, TPB, HEADS, VG], F16)
        ex = sb("ex", [P, PW], F32)
        pn = sb("pn", [P, 2, PW], F16)
        pt = sb("pt", [P, 2, 2 * PW], F16)
        nmax, nbias = sb("nmax", [P, TPB], F32), sb("nbias", [P, TPB], F32)
        rsum, rinv = sb("rsum", [P, TPB], F32), sb("rinv", [P, TPB], F32)
        at = sb("at", [P, 2, HEADS, T], F16)
        gsq, ga, gt, gb, gp = (sb(n, [P, T], F32) for n in ("gsq", "ga", "gt", "gb", "gp"))
        hT = sb("hT", [P, 2, 2, T], F16)
        et, eb = sb("et", [P, 2, T], F32), sb("eb", [P, 2, T], F32)
        scr = nc.dram_tensor("qk_parts", [2, 4, P, T], F16, kind="Internal").ap()

        SB, TB, GB, UB, AO, FB = psum[0:2], psum[2], psum[3], psum[4], psum[5], psum[6:8]
        TB16 = TB[:, :].bitcast(F16)

        raw_hi, raw_lo, raw_out = sem("raw_hi"), sem("raw_lo"), sem("raw_out")
        qk_mm, v_mm, v_hi, v_lo = sem("qk_mm"), sem("v_mm"), sem("v_hi"), sem("v_lo")
        stacked = [sem("stacked0"), sem("stacked1")]
        stack_zero, vm_zero = sem("stack_zero"), sem("vm_zero")
        s_mm, bias_n, biased, exp_done = sem("s_mm"), sem("nmax_done"), sem("bias_ready"), sem("exp_done")
        recip, pn_hi, pn_lo = sem("recip"), sem("pn_hi"), sem("pn_lo")
        t_mm, t_ev, av_mm = sem("t_mm"), sem("t_evacuated"), sem("av_mm")
        ao_hi, ao_lo = sem("ao_hi"), sem("ao_lo")
        g_mm, u_mm, sq_r, ga_r, gt_r, gb_r, gp_r, h_hi, h_lo, d_mm = (
            sem(n) for n in ("g_mm", "u_mm", "sq", "ga", "gt", "gb", "gp", "h_hi", "h_lo", "d_mm"))
        wo_mm, e_t, e_b, e_s, e_q, e_x = (sem(n) for n in ("wo_mm", "e_tanh", "e_b", "e_s", "e_q", "e_x"))

        def per_batch(eng, body):
            with eng.Fori(0, B - 1) as b:
                body(b, False)
            body(B - 1, True)

        def per_group(eng, b, item, mid):
            with eng.Fori(0, 2) as g:
                for k in range(HEADS):
                    item(g, k, True)
            mid()
            for g in (2, 3):
                for k in range(HEADS):
                    item(g, k, None if (g, k) == (3, 3) else True)

        def item_no(b, g, k):
            return b * 16 + g * 4 + k

        with nc.Block() as block:
            @block.sync
            def _(sp):
                def spill(n):
                    for ch in range(4):
                        sp.wait_ge(raw_hi, n * 4 + ch + 1)
                        sp.wait_ge(raw_lo, n * 4 + ch + 1)
                        for a in range(2):
                            sp.dma_start(scr[a, ch], raw[:, a, ch, :]).then_inc(raw_out, 16)
                    sp.wait_ge(raw_out, n * 128 + 128)

                def stack(half):
                    h = slice(half * 8, half * 8 + 8)
                    for row, a in enumerate((0, 1, 0)):
                        sp.dma_start(qs[16 * row:16 * row + 16, h, :],
                                     scr[a, half].rearrange("(h d) t -> d h t", d=HD0)).then_inc(stacked[half], 16)
                    for row, a in enumerate((0, 0, 1)):
                        sp.dma_start(ks[16 * row:16 * row + 16, h, :],
                                     scr[a, 2 + half].rearrange("(h d) t -> d h t", d=HD0)).then_inc(stacked[half], 16)

                sp.wait_ge(stack_zero, 2)
                spill(0)
                stack(0)
                stack(1)
                with sp.Fori(0, B - 1) as b:
                    for half in range(2):
                        sp.wait_ge(stacked[half], b * 96 + 96)
                    spill(b + 1)
                    sp.wait_ge(s_mm, b * 48 + 24)
                    stack(0)
                    sp.wait_ge(s_mm, b * 48 + 48)
                    stack(1)
                sp.wait_ge(stacked[0], 96 * B)
                sp.wait_ge(stacked[1], 96 * B)

            @block.gpsimd
            def _(pool):
                for s, credit in ((exp_done, 1), (pn_lo, 1), (t_mm, 3), (t_ev, 1), (av_mm, 2), (ao_lo, 1), (gb_r, 1),
                                  (gp_r, 1), (h_lo, 1), (d_mm, 2), (wo_mm, 2), (e_s, 2), (e_b, 2), (e_x, 2)):
                    pool.sem_inc(s, credit)
                pool.memset(qs[:, :, :], 0.0).then_inc(stack_zero, 1)
                pool.memset(ks[:, :, :], 0.0).then_inc(stack_zero, 1)
                pool.memset(vm[:, :, :, :], 0.0).then_inc(vm_zero, 1)

                def item(b, g, k):
                    n = item_no(b, g, k)
                    pool.wait_ge(gp_r, n + 2)
                    pool.wait_ge(h_hi, n + 1)
                    pool.tensor_tensor(hT[:, k % 2, 1, :], gp[:, :], hT[:, k % 2, 0, :], ALU.subtract).then_inc(h_lo, 1)

                def body(b, last):
                    with pool.Fori(0, 4) as g:
                        for k in range(HEADS):
                            item(b, g, k)
                    for i in range(2):
                        pool.wait_ge(e_q, b * 2 + i + 1)
                        xv = x[:, ds(b * TPB + 2 * i, 2), :].rearrange("p t d -> p (t d)")
                        pool.tensor_tensor(xv, xv, eb[:, i, :], ALU.add).then_inc(e_x, 1)

                with pool.Fori(0, B) as b:
                    body(b, False)

            @block.tensor
            def _(pe):
                def project_qk(b, n):
                    for ch in range(4):
                        bank = (GB, UB)[ch % 2]
                        if ch >= 2:
                            pe.wait_ge(raw_lo, n * 4 + ch - 1)
                        col = (ch // 2) * D + (ch % 2) * P
                        split_product(pe, bank[:, :],
                                      [[wqkv[:, a, c2, col:col + P] for a in range(2)] for c2 in range(DC)],
                                      [[xT[:, a, c2, ds(b * T, T)] for a in range(2)] for c2 in range(DC)],
                                      True, True).then_inc(qk_mm, 1)

                def project_v(b):
                    for t in range(TPB):
                        bank = (GB, UB)[t % 2]
                        if t >= 2:
                            pe.wait_ge(v_lo, b * 4 + t - 1)
                        split_product(pe, bank[:, 0:D],
                                      [[xT[:, a, c2, ds(b * T + t * P, P)] for a in range(2)] for c2 in range(DC)],
                                      [[wqkv[:, a, c2, 2 * D:3 * D] for a in range(2)] for c2 in range(DC)],
                                      True, True).then_inc(v_mm, 1)

                def scores(n, j, h, par, first=False):
                    bank = SB[(par + j) % 2]
                    if not (first and j < 2):
                        pe.wait_ge(exp_done, n * 3 + j)
                    at_col = 0
                    for i in ((3,), (2,), (1, 0))[j]:
                        w = (i + 1) * P
                        o = bank[:, at_col:at_col + w]
                        pe.matmul(o, qs[:, ds(h, 1), i * P:(i + 1) * P].rearrange("p a t -> p (a t)"),
                                  ks[:, ds(h, 1), 0:w].rearrange("p a t -> p (a t)"), start=True, stop=False,
                                  skip_group_check=True)
                        mm = pe.matmul(bank[:, at_col + i * P:at_col + w], ident_b[:, :], causal[:, :], start=False,
                                       stop=True, skip_group_check=True)
                        at_col += w
                    mm.then_inc(s_mm, 1)

                def turn(n, j):
                    pe.wait_ge(t_ev, n * 3 + j + 1)
                    blocks, _, _ = TFILLS[j]
                    col = 0
                    for kb in blocks:
                        for a in range(2):
                            for i in range(kb, TPB):
                                src = PCOL[i] + kb * P
                                mm = pe.transpose(TB16[:, col:col + P], pn[:, a, src:src + P], ident[:, :])
                                col += P
                    mm.then_inc(t_mm, 1)

                def weighted(n, b, g, k):
                    if k == 0:
                        pe.wait_ge(ao_lo, b * 4 + g + 1)
                    for kb in range(TPB):
                        if kb < 3:
                            pe.wait_ge(t_ev, n * 3 + min(kb, 2) + 2)
                        for a in range(2):
                            c0, c1, w = KEYCOL[kb]
                            col = (c0, c1)[a]
                            mm = pe.matmul(AO[:, kb * P:T],
                                           vm[:, kb, ds(g, 1), k * P:(k + 1) * P].rearrange("p a t -> p (a t)"),
                                           pt[:, k % 2, col:col + w],
                                           start=(k == 0 and kb == 0 and a == 0), stop=(k == 3 and kb == 3 and a == 1),
                                           skip_group_check=True)
                    mm.then_inc(av_mm, 1)

                def down(n, g, k):
                    pe.wait_ge(h_lo, n + 2)
                    for t in range(TPB):
                        mm = split_product(pe, FB[t // 2][:, (t % 2) * D:(t % 2 + 1) * D],
                                           [[hT[:, k % 2, a, t * P:(t + 1) * P] for a in range(2)]],
                                           [[wdown[:, a, ds(g * 4 + k, 1), :].rearrange("p a t -> p (a t)")
                                             for a in range(2)]], False, False)
                    mm.then_inc(d_mm, 1)

                pe.wait_ge(vm_zero, 1)
                project_qk(0, 0)
                pe.wait_ge(raw_lo, 4)
                for half in range(2):
                    pe.wait_ge(stacked[half], 96)
                for j in range(3):
                    scores(0, j, 0, 0, first=True)

                def batch(b, last):
                    pe.wait_ge(e_s, b * 2 + 2)
                    pe.wait_ge(e_b, b * 2 + 2)
                    project_v(b)
                    pe.wait_ge(v_lo, b * 4 + 4)
                    for f in range(2):
                        pe.matmul(FB[f][:, :], zeros[:, :], xT[:, 0, 0, 0:T], start=True, stop=False,
                                  skip_group_check=True)

                    def item(g, k, nxt):
                        n = item_no(b, g, k)
                        for m, (bank, s) in enumerate(((GB, g_mm), (UB, u_mm))):
                            pe.wait_ge((gb_r, gp_r)[m], n + 1)
                            split_product(pe, bank[:, :],
                                          [[wffn[m][:, a, c2, ds(g * 512 + k * P, P)] for a in range(2)] for c2 in range(DC)],
                                          [[xT[:, a, c2, ds(b * T, T)] for a in range(2)] for c2 in range(DC)],
                                          True, True).then_inc(s, 1)
                        if nxt is None:
                            if not last:
                                pe.wait_ge(stacked[0], b * 96 + 192)
                            h, have = 0, not last
                        else:
                            h, have = g * 4 + k + 1, True
                            if k == 3:
                                pe.wait_ge(stacked[1], b * 96 + 96)
                        par = (k + 1) % 2
                        if have:
                            scores(n + 1, 0, h, par)
                            scores(n + 1, 1, h, par)
                        pe.wait_ge(pn_lo, n + 2)
                        pe.wait_ge(pn_hi, n + 1)
                        turn(n, 0)
                        if have:
                            scores(n + 1, 2, h, par)
                        turn(n, 1)
                        turn(n, 2)
                        if k:
                            down(n - 1, g, k - 1)
                        weighted(n, b, g, k)
                        if k == 3:
                            down(n, g, 3)

                    def mid():
                        if not last:
                            pe.wait_ge(gb_r, b * 16 + 9)
                            pe.wait_ge(gp_r, b * 16 + 9)
                            pe.wait_ge(raw_out, b * 128 + 128)
                            project_qk(b + 1, b + 1)
                            pe.wait_ge(raw_lo, b * 4 + 8)

                    per_group(pe, b, item, mid)
                    pe.wait_ge(gb_r, b * 16 + 17)
                    pe.wait_ge(gp_r, b * 16 + 17)
                    pe.wait_ge(ao_lo, b * 4 + 5)
                    for t in range(TPB):
                        mm = split_product(pe, (GB, UB)[t // 2][:, (t % 2) * D:(t % 2 + 1) * D],
                                           [[at[:, a, gg, t * P:(t + 1) * P] for a in range(2)] for gg in range(4)],
                                           [[wo[:, a, gg, :] for a in range(2)] for gg in range(4)], True, True)
                        if t % 2:
                            mm.then_inc(wo_mm, 1)

                per_batch(pe, batch)

            @block.scalar
            def _(act):
                def raw_parts(n):
                    for ch in range(4):
                        act.wait_ge(qk_mm, n * 4 + ch + 1)
                        act.activation(raw[:, 0, ch, :], (GB, UB)[ch % 2][:, :], ACT.Copy).then_inc(raw_hi, 1)

                def softmax_exp(n, par, js):
                    for j in js:
                        blocks = ((3,), (2,), (1, 0))[j]
                        col = 0
                        act.wait_ge(biased, n * 3 + j + 1)
                        if j == 0:
                            act.wait_ge(pn_lo, n + 1)
                        for i in blocks:
                            w = (i + 1) * P
                            ins = act.activation(ex[:, PCOL[i]:PCOL[i] + w], SB[(par + j) % 2][:, col:col + w], ACT.Exp,
                                                 bias=nbias[:, i:i + 1], scale=SC, accum_out=rsum[:, i:i + 1])
                            col += w
                        ins.then_inc(exp_done, 1)

                def probs_hi(n):
                    act.wait_ge(recip, n + 1)
                    act.wait_ge(exp_done, n * 3 + 4)
                    act.wait_ge(t_mm, n * 3 + 3)
                    for i in range(TPB):
                        ins = act.activation(pn[:, 0, PCOL[i]:PCOL[i] + (i + 1) * P],
                                             ex[:, PCOL[i]:PCOL[i] + (i + 1) * P], ACT.Copy, scale=rinv[:, i:i + 1])
                    ins.then_inc(pn_hi, 1)

                raw_parts(0)
                softmax_exp(0, 0, (0, 1, 2))
                probs_hi(0)

                def batch(b, last):
                    for t in range(TPB):
                        act.wait_ge(v_mm, b * 4 + t + 1)
                        if t == 0:
                            act.wait_ge(av_mm, b * 16 + 2)
                            act.wait_ge(vm_zero, 1)
                        v4 = vm[:, t, :, :].rearrange("p g (k e) -> p g k e", e=160)
                        act.activation(v4[:, :, :, 0:16], (GB, UB)[t % 2][:, 0:D].rearrange("p (g k d) -> p g k d", g=4, k=4),
                                       ACT.Copy).then_inc(v_hi, 1)

                    def item(g, k, nxt):
                        n = item_no(b, g, k)
                        act.wait_ge(g_mm, n + 1)
                        act.activation(gsq[:, :], GB[:, :], ACT.Square).then_inc(sq_r, 1)
                        act.wait_ge(ga_r, n + 1)
                        act.activation(gt[:, :], ga[:, :], ACT.Tanh, scale=GELU_K * GELU_C).then_inc(gt_r, 1)
                        have = not (nxt is None and last)
                        if have:
                            softmax_exp(n + 1, (k + 1) % 2, (0, 1))
                        act.wait_ge(gp_r, n + 2)
                        act.wait_ge(d_mm, n + 1)
                        act.activation(hT[:, k % 2, 0, :], gp[:, :], ACT.Copy).then_inc(h_hi, 1)
                        if have:
                            softmax_exp(n + 1, (k + 1) % 2, (2,))
                            probs_hi(n + 1)
                        if k == 3:
                            act.wait_ge(av_mm, n + 3)
                            act.wait_ge(wo_mm, b * 2 + 2)
                            act.activation(at[:, 0, ds(g, 1), :].rearrange("p a t -> p (a t)"), AO[:, :],
                                           ACT.Copy).then_inc(ao_hi, 1)

                    def mid():
                        if not last:
                            raw_parts(b + 1)

                    per_group(act, b, item, mid)
                    for i in range(2):
                        act.wait_ge(d_mm, b * 16 + 18)
                        act.activation(et[:, i, :], FB[i][:, :], ACT.Tanh, scale=0.5).then_inc(e_t, 1)

                per_batch(act, batch)

            @block.vector
            def _(dve):
                def raw_parts(n):
                    for ch in range(4):
                        dve.wait_ge(raw_hi, n * 4 + ch + 1)
                        dve.tensor_tensor(raw[:, 1, ch, :], (GB, UB)[ch % 2][:, :], raw[:, 0, ch, :],
                                          ALU.subtract).then_inc(raw_lo, 1)

                def maxima(n, par, j):
                    dve.wait_ge(s_mm, n * 3 + j + 1)
                    if j == 0:
                        dve.wait_ge(exp_done, n * 3 + 1)
                    blocks = ((3,), (2,), (1, 0))[j]
                    col = 0
                    for i in blocks:
                        w = (i + 1) * P
                        ins = dve.tensor_reduce(nmax[:, i:i + 1], SB[(par + j) % 2][:, col:col + w], axis=AX.X,
                                                op=ALU.max, negate=True)
                        col += w
                    ins.then_inc(bias_n, 1)
                    dve.wait_ge(bias_n, n * 3 + j + 1)
                    lo, hi = blocks[-1], blocks[0] + 1
                    dve.tensor_scalar(nbias[:, lo:hi], nmax[:, lo:hi], SC, None, ALU.mult).then_inc(biased, 1)

                def turned(n, par, j):
                    _, col, w = TFILLS[j]
                    dve.wait_ge(t_mm, n * 3 + j + 4)
                    if j == 0:
                        dve.wait_ge(av_mm, n + 1)
                    dve.tensor_copy(pt[:, par, col:col + w], TB16[:, 0:w]).then_inc(t_ev, 1)

                def probs_lo(n):
                    dve.wait_ge(exp_done, n * 3 + 4)
                    dve.reciprocal(rinv[:, :], rsum[:, :]).then_inc(recip, 1)
                    dve.wait_ge(pn_hi, n + 1)
                    dve.wait_ge(recip, n + 1)
                    for i in range(TPB):
                        s = slice(PCOL[i], PCOL[i] + (i + 1) * P)
                        ins = dve.scalar_tensor_tensor(out=pn[:, 1, s], in0=ex[:, s], scalar=rinv[:, i:i + 1],
                                                       in1=pn[:, 0, s], op0=ALU.mult, op1=ALU.subtract)
                    ins.then_inc(pn_lo, 1)

                raw_parts(0)
                for j in range(3):
                    maxima(0, 0, j)
                probs_lo(0)

                def batch(b, last):
                    for t in range(TPB):
                        dve.wait_ge(v_hi, b * 4 + t + 1)
                        v4 = vm[:, t, :, :].rearrange("p g (k e) -> p g k e", e=160)
                        dve.tensor_tensor(v4[:, :, :, 16:32], (GB, UB)[t % 2][:, 0:D].rearrange("p (g k d) -> p g k d", g=4, k=4),
                                          v4[:, :, :, 0:16], ALU.subtract).then_inc(v_lo, 1)

                    def item(g, k, nxt):
                        n = item_no(b, g, k)
                        dve.wait_ge(sq_r, n + 1)
                        dve.scalar_tensor_tensor(out=ga[:, :], in0=gsq[:, :], scalar=1.0 / GELU_C, in1=GB[:, :],
                                                 op0=ALU.add, op1=ALU.mult).then_inc(ga_r, 1)
                        have = not (nxt is None and last)
                        par = (k + 1) % 2
                        if have:
                            maxima(n + 1, par, 0)
                        dve.wait_ge(gt_r, n + 1)
                        dve.scalar_tensor_tensor(out=gb[:, :], in0=gt[:, :], scalar=1.0, in1=GB[:, :],
                                                 op0=ALU.add, op1=ALU.mult).then_inc(gb_r, 1)
                        dve.wait_ge(u_mm, n + 1)
                        dve.wait_ge(gb_r, n + 2)
                        dve.wait_ge(h_lo, n + 1)
                        dve.scalar_tensor_tensor(out=gp[:, :], in0=gb[:, :], scalar=0.5, in1=UB[:, :],
                                                 op0=ALU.mult, op1=ALU.mult).then_inc(gp_r, 1)
                        if have:
                            maxima(n + 1, par, 1)
                        turned(n, k % 2, 0)
                        if have:
                            maxima(n + 1, par, 2)
                        turned(n, k % 2, 1)
                        turned(n, k % 2, 2)
                        if have:
                            probs_lo(n + 1)
                        if k == 3:
                            dve.wait_ge(ao_hi, b * 4 + g + 1)
                            dve.tensor_tensor(at[:, 1, ds(g, 1), :].rearrange("p a t -> p (a t)"), AO[:, :],
                                              at[:, 0, ds(g, 1), :].rearrange("p a t -> p (a t)"),
                                              ALU.subtract).then_inc(ao_lo, 1)

                    def mid():
                        if not last:
                            raw_parts(b + 1)

                    per_group(dve, b, item, mid)
                    bo2 = bo[:, :].rearrange("p (a d) -> p a d", a=1).broadcast_to([P, 2, D])
                    for i in range(2):
                        dve.wait_ge(e_t, b * 2 + i + 1)
                        dve.wait_ge(e_x, b * 2 + i + 1)
                        dve.scalar_tensor_tensor(out=eb[:, i, :], in0=et[:, i, :], scalar=1.0, in1=FB[i][:, :],
                                                 op0=ALU.add, op1=ALU.mult).then_inc(e_b, 1)
                        dve.wait_ge(wo_mm, b * 2 + i + 3)
                        dve.wait_ge(e_b, b * 2 + i + 3)
                        dve.tensor_tensor(et[:, i, :].rearrange("p (a d) -> p a d", a=2),
                                          (GB, UB)[i][:, :].rearrange("p (a d) -> p a d", a=2), bo2,
                                          ALU.add).then_inc(e_s, 1)
                        dve.wait_ge(e_s, b * 2 + i + 3)
                        dve.scalar_tensor_tensor(out=eb[:, i, :], in0=et[:, i, :], scalar=0.5, in1=eb[:, i, :],
                                                 op0=ALU.mult, op1=ALU.mult).then_inc(e_q, 1)

                per_batch(dve, batch)


def experts(nc, A, xT, ident, zeros, gate, psum):
    with ExitStack() as c:
        sb = lambda n, s, d: c.enter_context(nc.sbuf_tensor("m_" + n, s, d))
        sem = lambda n: c.enter_context(nc.semaphore("m_" + n))
        w13 = [sb(f"w{m}", [P, 2, DC, HID1], F16) for m in range(2)]
        w2 = sb("w2", [P, 2, NCH1, D], F16)
        wg = sb("wg", [P, 2, DC, E], F16)
        sel = sb("sel", [E + 1, HID1], F16)
        share = sb("share", [E + 1, 2, TOK], F16)
        bias = sb("bias", [P, E], F32)
        with ExitStack() as c2:
            st = [c2.enter_context(nc.sbuf_tensor(f"m_stage{i}", [P, HID1], F32)) for i in range(2)]
            st2 = c2.enter_context(nc.sbuf_tensor("m_stage_w2", [P, 5, D], F32))
            stg = c2.enter_context(nc.sbuf_tensor("m_stage_gate", [P, DC, E], F32))
            extra = [(sel[:, :], A["sel"]), (bias[:, :], A["expert_bias"].broadcast_to([P, E]))]
            for m in range(2):
                split_weights(nc, [(A[f"w{m}"][cc * P:(cc + 1) * P, :], st[cc][:, :], w13[m][:, 0, cc, :],
                                    w13[m][:, 1, cc, :]) for cc in range(2)], f"moe{m}")
            for q in range(NCH1 // 5):
                jobs = [(A["w2"][q * 5 * P:(q + 1) * 5 * P, :].rearrange("(c p) d -> p c d", p=P), st2[:, :, :],
                         w2[:, 0, q * 5:(q + 1) * 5, :], w2[:, 1, q * 5:(q + 1) * 5, :])]
                if q == 0:
                    jobs.append((A["gate_w"].rearrange("(c p) e -> p c e", p=P), stg[:, :, :], wg[:, 0, :, :],
                                 wg[:, 1, :, :]))
                split_weights(nc, jobs, f"moe2{q}", extra if q == 0 else ())
        route(nc, xT, wg, bias, ident, share, psum)

        gt, gb, gp = (sb(n, [P, 2, T], F32) for n in ("gt", "gb", "gp"))
        hT = sb("hT", [P, 2, 2, T], F16)
        et, eb = sb("et", [P, 2, T], F32), sb("eb", [P, 2, T], F32)
        GB, UB, CB, FB = psum[0:2], psum[2:4], psum[4:6], psum[6:8]
        g_mm, u_mm, c_mm, gt_r, gb_r, gu_r, gp_r, h_hi, h_lo, d_mm, e_t, e_b, e_g = (
            sem(n) for n in ("g_mm", "u_mm", "c_mm", "tanh", "gb", "gu", "gp", "h_hi", "h_lo", "d_mm", "e_tanh",
                             "e_b", "e_gate"))

        def chunks(eng, b, item, tail=lambda: None):
            item(0, b * NCH1, 0, True)
            with eng.Fori(0, NCH1 // 2) as i:
                for k in range(2):
                    item(i * 2 + k + 1, b * NCH1 + i * 2 + k + 1, (k + 1) % 2, False)

        with nc.Block() as block:
            @block.tensor
            def _(pe):
                def down(ch, n, par):
                    pe.wait_ge(h_lo, n + 3)
                    for t in range(TPB):
                        mm = split_product(pe, FB[t // 2][:, (t % 2) * D:(t % 2 + 1) * D],
                                           [[hT[:, par, a, t * P:(t + 1) * P] for a in range(2)]],
                                           [[w2[:, a, ds(ch, 1), :].rearrange("p a t -> p (a t)")
                                             for a in range(2)]], False, False)
                    mm.then_inc(d_mm, 1)

                with pe.Fori(0, B) as b:
                    pe.wait_ge(e_b, b * 2 + 2)
                    for f in range(2):
                        pe.matmul(FB[f][:, :], zeros[:, :], xT[:, 0, 0, 0:T], start=True, stop=False,
                                  skip_group_check=True)

                    def item(ch, n, par, first):
                        pe.wait_ge(gp_r, n + 1)
                        for m, (banks, s) in enumerate(((GB, g_mm), (UB, u_mm))):
                            split_product(pe, banks[par][:, :],
                                          [[w13[m][:, a, c2, ds(ch * P, P)] for a in range(2)] for c2 in range(DC)],
                                          [[xT[:, a, c2, ds(b * T, T)] for a in range(2)] for c2 in range(DC)],
                                          True, True).then_inc(s, 1)
                        for a in range(2):
                            mm = pe.matmul(CB[par][:, :], sel[:, ds(ch * P, P)], share[:, a, ds(b * T, T)],
                                           start=a == 0, stop=a == 1, skip_group_check=True)
                        mm.then_inc(c_mm, 1)
                        if not first:
                            down(ch - 1, n - 1, 1 - par)

                    chunks(pe, b, item)
                    down(NCH1 - 1, b * NCH1 + NCH1 - 1, 0)

            @block.scalar
            def _(act):
                with act.Fori(0, B) as b:
                    def item(ch, n, par, first):
                        act.wait_ge(g_mm, n + 1)
                        act.activation(gt[:, par, :], GB[par][:, :], ACT.Tanh, scale=0.5).then_inc(gt_r, 1)
                        act.wait_ge(gp_r, n + 3)
                        act.wait_ge(d_mm, n + 1)
                        act.activation(hT[:, par, 0, :], gp[:, par, :], ACT.Copy).then_inc(h_hi, 1)

                    chunks(act, b, item)
                    act.wait_ge(d_mm, b * NCH1 + NCH1 + 2)
                    for i in range(2):
                        act.activation(et[:, i, :], FB[i][:, :], ACT.Tanh, scale=0.5).then_inc(e_t, 1)

            @block.gpsimd
            def _(pool):
                for s, credit in ((gp_r, 2), (h_lo, 2), (d_mm, 2), (e_b, 2)):
                    pool.sem_inc(s, credit)
                with pool.Fori(0, B) as b:
                    def item(ch, n, par, first):
                        pool.wait_ge(gp_r, n + 3)
                        pool.wait_ge(h_hi, n + 1)
                        pool.tensor_tensor(hT[:, par, 1, :], gp[:, par, :], hT[:, par, 0, :],
                                           ALU.subtract).then_inc(h_lo, 1)

                    chunks(pool, b, item)

            @block.vector
            def _(dve):
                with dve.Fori(0, B) as b:
                    def item(ch, n, par, first):
                        dve.wait_ge(gt_r, n + 1)
                        dve.scalar_tensor_tensor(out=gb[:, par, :], in0=gt[:, par, :], scalar=1.0, in1=GB[par][:, :],
                                                 op0=ALU.add, op1=ALU.mult).then_inc(gb_r, 1)
                        dve.wait_ge(u_mm, n + 1)
                        dve.wait_ge(gb_r, n + 1)
                        dve.scalar_tensor_tensor(out=gt[:, par, :], in0=gb[:, par, :], scalar=0.5, in1=UB[par][:, :],
                                                 op0=ALU.mult, op1=ALU.mult).then_inc(gu_r, 1)
                        dve.wait_ge(c_mm, n + 1)
                        dve.wait_ge(gu_r, n + 1)
                        dve.wait_ge(h_lo, n + 1)
                        dve.tensor_tensor(gp[:, par, :], gt[:, par, :], CB[par][:, :], ALU.mult).then_inc(gp_r, 1)

                    chunks(dve, b, item)
                    for i in range(2):
                        dve.wait_ge(e_t, b * 2 + i + 1)
                        dve.scalar_tensor_tensor(out=eb[:, i, :], in0=et[:, i, :], scalar=1.0, in1=FB[i][:, :],
                                                 op0=ALU.add, op1=ALU.mult).then_inc(e_b, 1)
                        dve.wait_ge(e_b, b * 2 + i + 3)
                        dve.tensor_scalar(gate[:, ds(b * TPB + 2 * i, 2), :].rearrange("p t d -> p (t d)"), eb[:, i, :],
                                          0.5, None, ALU.mult).then_inc(e_g, 1)


def route(nc, xT, wg, bias, ident, share, psum):
    with ExitStack() as c:
        sb = lambda n, s, d: c.enter_context(nc.sbuf_tensor("r_" + n, s, d))
        sem = lambda n: c.enter_context(nc.semaphore("r_" + n))
        score, biased, masked = sb("score", [P, NT, E], F32), sb("biased", [P, NT, E], F32), sb("masked", [P, NT, E], F32)
        gmax, grank, gsel = (sb(n, [P, NT, G], F32) for n in ("gmax", "grank", "gsel"))
        gcmp, geq = sb("gcmp", [P, NT, G, G], F32), sb("geq", [P, NT, G, G], F32)
        cmp_, eq = sb("cmp", [P, NT, E, E], F32), sb("eq", [P, NT, E, E], F32)
        lower_g, lower_e = sb("lower_g", [P, G, G], F32), sb("lower_e", [P, E, E], F32)
        rank, total = sb("rank", [P, NT, E], F32), sb("total", [P, NT], F32)
        parts = sb("parts", [P, 2, NT, E], F16)
        logits_done, tanh_done, low_made, chain = sem("logits"), sem("tanh"), sem("lower"), sem("chain")
        turned, hi_done, copied = sem("turned"), sem("hi"), sem("copied")
        LOG = psum[0]
        TQ = psum[1:5]

        with nc.Block() as block:
            @block.tensor
            def _(pe):
                for t in range(NT):
                    mm = split_product(pe, LOG[:, t * E:(t + 1) * E],
                                       [[xT[:, a, c2, t * P:(t + 1) * P] for a in range(2)] for c2 in range(DC)],
                                       [[wg[:, a, c2, :] for a in range(2)] for c2 in range(DC)], True, True)
                mm.then_inc(logits_done, 1)
                pe.wait_ge(copied, 1)
                for a in range(2):
                    for t in range(NT):
                        mm = pe.transpose(TQ[a * 2 + t // 8][:, :].bitcast(F16)[0:E, (t % 8) * P:(t % 8 + 1) * P],
                                          parts[:, a, t, :], ident[:, :])
                    mm.then_inc(turned, 1)

            @block.scalar
            def _(act):
                act.wait_ge(logits_done, 1)
                act.activation(score[:, :, :].rearrange("p t e -> p (t e)"), LOG[:, 0:NT * E], ACT.Tanh,
                               scale=0.5).then_inc(tanh_done, 1)

            @block.gpsimd
            def _(pool):
                for m, n in ((lower_g, G), (lower_e, E)):
                    pool.memset(m[:, :, :], 1.0).then_inc(low_made, 1)
                pool.wait_ge(low_made, 2)
                for m, n in ((lower_g, G), (lower_e, E)):
                    pool.affine_select(out=m[:, :, :], in_=m[:, :, :], compare_op=ALU.is_gt, fill=0.0, base=0,
                                       pattern=[[1, n], [-1, n]], channel_multiplier=0).then_inc(low_made, 1)
                pool.memset(share[:, 0, :], 1.0).then_inc(low_made, 1)
                pool.memset(share[:, 1, :], 0.0).then_inc(low_made, 1)

            @block.vector
            def _(dve):
                step = Count(chain)

                def do(ins):
                    step(ins)
                    step.wait(dve)

                dve.wait_ge(tanh_done, 1)
                dve.wait_ge(low_made, 6)
                do(dve.tensor_scalar(score[:, :, :], score[:, :, :], 1.0, 0.5, ALU.add, ALU.mult))
                bias_t = bias[:, :].rearrange("p (a e) -> p a e", a=1).broadcast_to([P, NT, E])
                do(dve.tensor_tensor(biased[:, :, :], score[:, :, :], bias_t, ALU.add))
                do(dve.tensor_reduce(gmax[:, :, :], biased[:, :, :].rearrange("p t (g e) -> p t g e", g=G),
                                     axis=AX.X, op=ALU.max))

                def ranks(value, n, lower, cmp_, eq, rank):
                    mine = value.rearrange("p t (e a) -> p t e a", a=1).broadcast_to([P, NT, n, n])
                    other = value.rearrange("p t (a e) -> p t a e", a=1).broadcast_to([P, NT, n, n])
                    low = lower[:, :, :].rearrange("p (a i) j -> p a i j", a=1).broadcast_to([P, NT, n, n])
                    do(dve.tensor_tensor(cmp_[:, :, :, :], other, mine, ALU.is_gt))
                    do(dve.tensor_tensor(eq[:, :, :, :], other, mine, ALU.is_equal))
                    do(dve.tensor_tensor(eq[:, :, :, :], eq[:, :, :, :], low, ALU.mult))
                    do(dve.tensor_tensor(cmp_[:, :, :, :], cmp_[:, :, :, :], eq[:, :, :, :], ALU.add))
                    do(dve.tensor_reduce(rank, cmp_[:, :, :, :], axis=AX.X, op=ALU.add))

                ranks(gmax[:, :, :], G, lower_g, gcmp, geq, grank[:, :, :])
                do(dve.tensor_scalar(gsel[:, :, :], grank[:, :, :], TOPK_G - 0.5, None, ALU.is_lt))
                sel_e = gsel[:, :, :].rearrange("p t (g a) -> p t g a", a=1).broadcast_to([P, NT, G, EG])
                as_groups = lambda ap: ap.rearrange("p t (g e) -> p t g e", g=G)
                do(dve.tensor_tensor(as_groups(masked[:, :, :]), as_groups(biased[:, :, :]), sel_e, ALU.mult))
                do(dve.tensor_scalar(gsel[:, :, :], gsel[:, :, :], 1.0, -MASKED, ALU.subtract, ALU.mult))
                do(dve.tensor_tensor(as_groups(masked[:, :, :]), as_groups(masked[:, :, :]), sel_e, ALU.add))
                ranks(masked[:, :, :], E, lower_e, cmp_, eq, rank[:, :, :])
                do(dve.tensor_scalar(rank[:, :, :], rank[:, :, :], TOPK - 0.5, None, ALU.is_lt))
                do(dve.tensor_tensor(score[:, :, :], score[:, :, :], rank[:, :, :], ALU.mult))
                do(dve.tensor_reduce(total[:, :], score[:, :, :], axis=AX.X, op=ALU.add))
                do(dve.reciprocal(total[:, :], total[:, :]))
                tot = total[:, :].rearrange("p (t a) -> p t a", a=1).broadcast_to([P, NT, E])
                do(dve.tensor_tensor(score[:, :, :], score[:, :, :], tot, ALU.mult))
                do(dve.tensor_copy(parts[:, 0, :, :], score[:, :, :]))
                dve.tensor_tensor(parts[:, 1, :, :], score[:, :, :], parts[:, 0, :, :], ALU.subtract).then_inc(copied, 1)
                for a in range(2):
                    dve.wait_ge(turned, a + 1)
                    for half in range(2):
                        dve.tensor_copy(share[0:E, a, half * 1024:(half + 1) * 1024],
                                        TQ[a * 2 + half][:, :].bitcast(F16)[0:E, :])


def attention1(nc, A, x, xT, ident, ident_b, causal, zeros, gate, psum):
    SC = HD1 ** -0.5
    NI = H1
    with ExitStack() as c:
        sb = lambda n, s, d: c.enter_context(nc.sbuf_tensor("a_" + n, s, d))
        sem = lambda n: c.enter_context(nc.semaphore("a_" + n))
        wq, wk, wv = (sb(n, [P, 2, DC, H1 * HD1], F16) for n in ("wq", "wk", "wv"))
        wo = sb("wo", [P, 2, H1, D], F16)
        bq, bk, bv = (sb(n, [P, H1], F32) for n in ("bq", "bk", "bv"))
        bo = sb("bo", [P, D], F32)
        with ExitStack() as c2:
            st = [c2.enter_context(nc.sbuf_tensor(f"a_stage{i}", [P, H1 * HD1], F32)) for i in range(2)]
            for m, (w, name) in enumerate(((wq, "wq1"), (wk, "wk1"), (wv, "wv1"))):
                split_weights(nc, [(A[name][cc * P:(cc + 1) * P, :], st[cc][:, :], w[:, 0, cc, :], w[:, 1, cc, :])
                                   for cc in range(2)], f"att{m}",
                              ((bq[:, :], A["bq1"]), (bk[:, :], A["bk1"]), (bv[:, :], A["bv1"]),
                               (bo[:, :], A["bo1"].broadcast_to([P, D]))) if m == 0 else ())
            split_weights(nc, [(A["wo1"][hh * 1024:(hh + 1) * 1024, :].rearrange("(h p) d -> p h d", p=P),
                                st[hh][:, :].rearrange("p (h d) -> p h d", d=D), wo[:, 0, hh * 8:hh * 8 + 8, :],
                                wo[:, 1, hh * 8:hh * 8 + 8, :]) for hh in range(2)], "att3")

        qk = sb("qk", [P, 2, 2, 2, T], F16)
        vv = sb("vv", [P, 2, 2, TPB * P], F16)
        ex = sb("ex", [P, PW], F32)
        pn = sb("pn", [P, 2, PW], F16)
        pt = sb("pt", [P, 2, 2 * PW], F16)
        nmax, nbias = sb("nmax", [P, TPB], F32), sb("nbias", [P, TPB], F32)
        rsum, rinv = sb("rsum", [P, TPB], F32), sb("rinv", [P, TPB], F32)
        at = sb("at", [P, 2, 2, T], F16)
        fo = sb("fo", [P, 2, T], F32)
        SB, TB, JB, AO, FB = psum[0:2], psum[2], psum[3:5], psum[5], psum[6:8]
        TB16 = TB[:, :].bitcast(F16)
        p_mm, p_hi, p_lo = sem("proj_mm"), sem("proj_hi"), sem("proj_lo")
        s_mm, bias_n, biased, exp_done = sem("s_mm"), sem("nmax_done"), sem("bias_ready"), sem("exp_done")
        recip, pn_hi, pn_lo = sem("recip"), sem("pn_hi"), sem("pn_lo")
        t_mm, t_ev, av_mm = sem("t_mm"), sem("t_evacuated"), sem("av_mm")
        ao_hi, ao_lo, wo_mm = sem("ao_hi"), sem("ao_lo"), sem("wo_mm")
        o_b, o_g, o_x, o_dma = sem("o_bias"), sem("o_gate"), sem("o_x"), sem("o_dma")

        def items(eng, item, prologue):
            prologue()

            def batch(b, last):
                with eng.Fori(0, NI // 2 - 1) as i:
                    for k in range(2):
                        item(b, i * 2 + k, b * NI + i * 2 + k, k, i * 2 + k + 1, b)
                item(b, NI - 2, b * NI + NI - 2, 0, NI - 1, b)
                item(b, NI - 1, b * NI + NI - 1, 1, None if last else 0, b if last else b + 1)
                return b

            return batch

        def per_batch(eng, body):
            with eng.Fori(0, B - 1) as b:
                body(b, False)
            body(B - 1, True)

        with nc.Block() as block:
            @block.gpsimd
            def _(pool):
                for s, credit in ((p_lo, 2), (exp_done, 1), (pn_lo, 1), (t_mm, 3), (t_ev, 1), (av_mm, 2), (ao_lo, 1),
                                  (wo_mm, 2), (o_b, 2), (o_x, 2)):
                    pool.sem_inc(s, credit)
                with pool.Fori(0, B) as b:
                    for i in range(2):
                        pool.wait_ge(o_g, b * 2 + i + 1)
                        xv = x[:, ds(b * TPB + 2 * i, 2), :].rearrange("p t d -> p (t d)")
                        pool.tensor_tensor(xv, xv, fo[:, i, :], ALU.add).then_inc(o_x, 1)

            @block.sync
            def _(sp):
                with sp.Fori(0, B) as b:
                    for i in range(2):
                        sp.wait_ge(o_x, b * 2 + i + 3)
                        sp.dma_start(A["out"].rearrange("(t p) d -> p t d", p=P)[:, ds(b * TPB + 2 * i, 2), :],
                                     x[:, ds(b * TPB + 2 * i, 2), :]).then_inc(o_dma, 16)
                sp.wait_ge(o_dma, B * 2 * 16)

            @block.tensor
            def _(pe):
                def project(n, b, h, j, bank, par):
                    pe.wait_ge(p_lo, n * 3 + j + 1)
                    if j < 2:
                        w = (wq, wk)[j]
                        mm = split_product(pe, bank[:, :],
                                           [[w[:, a, c2, ds(h * P, P)] for a in range(2)] for c2 in range(DC)],
                                           [[xT[:, a, c2, ds(b * T, T)] for a in range(2)] for c2 in range(DC)],
                                           True, True)
                    else:
                        for t in range(TPB):
                            mm = split_product(pe, bank[:, t * P:(t + 1) * P],
                                               [[xT[:, a, c2, ds(b * T + t * P, P)] for a in range(2)] for c2 in range(DC)],
                                               [[wv[:, a, c2, ds(h * P, P)] for a in range(2)] for c2 in range(DC)],
                                               True, True)
                    mm.then_inc(p_mm, 1)

                def scores(n, j, par, first=False):
                    bank = SB[(par + j) % 2]
                    if not (first and j < 2):
                        pe.wait_ge(exp_done, n * 3 + j)
                    if j == 0:
                        pe.wait_ge(p_lo, n * 3 + 4)
                    at_col = 0
                    for i in ((3,), (2,), (1, 0))[j]:
                        w = (i + 1) * P
                        split_product(pe, bank[:, at_col:at_col + w],
                                      [[qk[:, par, 0, a, i * P:(i + 1) * P] for a in range(2)]],
                                      [[qk[:, par, 1, a, 0:w] for a in range(2)]], True, False)
                        mm = pe.matmul(bank[:, at_col + i * P:at_col + w], ident_b[:, :], causal[:, :], start=False,
                                       stop=True, skip_group_check=True)
                        at_col += w
                    mm.then_inc(s_mm, 1)

                def turn(n, j):
                    pe.wait_ge(t_ev, n * 3 + j + 1)
                    col = 0
                    for kb in TFILLS[j][0]:
                        for a in range(2):
                            for i in range(kb, TPB):
                                src = PCOL[i] + kb * P
                                mm = pe.transpose(TB16[:, col:col + P], pn[:, a, src:src + P], ident[:, :])
                                col += P
                    mm.then_inc(t_mm, 1)

                def weighted(n, par):
                    pe.wait_ge(ao_lo, n + 1)
                    pe.wait_ge(p_lo, n * 3 + 5)
                    for kb in range(TPB):
                        if kb < 3:
                            pe.wait_ge(t_ev, n * 3 + kb + 2)
                        c0, c1, w = KEYCOL[kb]
                        mm = split_product(pe, AO[:, kb * P:T], [[vv[:, par, a, kb * P:(kb + 1) * P] for a in range(2)]],
                                           [[pt[:, par, col:col + w] for col in (c0, c1)]], kb == 0, kb == 3)
                    mm.then_inc(av_mm, 1)

                def out_product(n, h, par):
                    pe.wait_ge(ao_lo, n + 2)
                    for t in range(TPB):
                        mm = split_product(pe, FB[t // 2][:, (t % 2) * D:(t % 2 + 1) * D],
                                           [[at[:, par, a, t * P:(t + 1) * P] for a in range(2)]],
                                           [[wo[:, a, ds(h, 1), :].rearrange("p a t -> p (a t)") for a in range(2)]],
                                           False, False)
                    mm.then_inc(wo_mm, 1)

                def item(b, h, n, par, h2, b2):
                    q = 1 - par
                    if h2 is not None:
                        project(n + 1, b2, h2, 0, JB[q], q)
                        project(n + 1, b2, h2, 1, JB[1 - q], q)
                    pe.wait_ge(pn_lo, n + 2)
                    pe.wait_ge(pn_hi, n + 1)
                    turn(n, 0)
                    turn(n, 1)
                    if h2 is not None:
                        project(n + 1, b2, h2, 2, JB[q], q)
                    turn(n, 2)
                    weighted(n, par)
                    if h2 is not None:
                        for j in range(3):
                            scores(n + 1, j, q)
                    out_product(n, h, par)

                def batch(b, last):
                    pe.wait_ge(o_b, b * 2 + 2)
                    for f in range(2):
                        pe.matmul(FB[f][:, :], zeros[:, :], xT[:, 0, 0, 0:T], start=True, stop=False,
                                  skip_group_check=True)
                    items(pe, item, lambda: None)(b, last)

                for j in range(3):
                    project(0, 0, 0, j, JB[j % 2], 0)
                for j in range(3):
                    scores(0, j, 0, first=True)
                per_batch(pe, batch)

            def softmax_exp(act, n, par):
                for j in range(3):
                    col = 0
                    act.wait_ge(biased, n * 3 + j + 1)
                    if j == 0:
                        act.wait_ge(pn_lo, n + 1)
                    for i in ((3,), (2,), (1, 0))[j]:
                        w = (i + 1) * P
                        ins = act.activation(ex[:, PCOL[i]:PCOL[i] + w], SB[(par + j) % 2][:, col:col + w], ACT.Exp,
                                             bias=nbias[:, i:i + 1], scale=SC, accum_out=rsum[:, i:i + 1])
                        col += w
                    ins.then_inc(exp_done, 1)

            @block.scalar
            def _(act):
                def high(n, h, j, bank, par):
                    act.wait_ge(p_mm, n * 3 + j + 1)
                    if j < 2:
                        act.activation(qk[:, par, j, 0, :], bank[:, :], ACT.Identity,
                                       bias=(bq, bk)[j][:, ds(h, 1)]).then_inc(p_hi, 1)
                    else:
                        act.wait_ge(av_mm, n + 1)
                        act.activation(vv[:, par, 0, :], bank[:, :], ACT.Copy).then_inc(p_hi, 1)

                def probs_hi(n):
                    act.wait_ge(recip, n + 1)
                    act.wait_ge(exp_done, n * 3 + 4)
                    act.wait_ge(t_mm, n * 3 + 3)
                    for i in range(TPB):
                        ins = act.activation(pn[:, 0, PCOL[i]:PCOL[i] + (i + 1) * P],
                                             ex[:, PCOL[i]:PCOL[i] + (i + 1) * P], ACT.Copy, scale=rinv[:, i:i + 1])
                    ins.then_inc(pn_hi, 1)

                def item(b, h, n, par, h2, b2):
                    q = 1 - par
                    if h2 is not None:
                        high(n + 1, h2, 0, JB[q], q)
                        high(n + 1, h2, 1, JB[1 - q], q)
                        high(n + 1, h2, 2, JB[q], q)
                    act.wait_ge(av_mm, n + 3)
                    act.wait_ge(wo_mm, n + 1)
                    act.activation(at[:, par, 0, :], AO[:, :], ACT.Identity, bias=bv[:, ds(h, 1)]).then_inc(ao_hi, 1)
                    if h2 is not None:
                        softmax_exp(act, n + 1, q)
                        probs_hi(n + 1)

                for j in range(3):
                    high(0, 0, j, JB[j % 2], 0)
                softmax_exp(act, 0, 0)
                probs_hi(0)
                per_batch(act, lambda b, last: items(act, item, lambda: None)(b, last))

            @block.vector
            def _(dve):
                def low(n, h, j, bank, par):
                    dve.wait_ge(p_hi, n * 3 + j + 1)
                    if j < 2:
                        dve.scalar_tensor_tensor(out=qk[:, par, j, 1, :], in0=bank[:, :], scalar=(bq, bk)[j][:, ds(h, 1)],
                                                 in1=qk[:, par, j, 0, :], op0=ALU.add, op1=ALU.subtract).then_inc(p_lo, 1)
                    else:
                        dve.tensor_tensor(vv[:, par, 1, :], bank[:, :], vv[:, par, 0, :], ALU.subtract).then_inc(p_lo, 1)

                def maxima(n, par, j):
                    dve.wait_ge(s_mm, n * 3 + j + 1)
                    if j == 0:
                        dve.wait_ge(exp_done, n * 3 + 1)
                    blocks = ((3,), (2,), (1, 0))[j]
                    col = 0
                    for i in blocks:
                        w = (i + 1) * P
                        ins = dve.tensor_reduce(nmax[:, i:i + 1], SB[(par + j) % 2][:, col:col + w], axis=AX.X,
                                                op=ALU.max, negate=True)
                        col += w
                    ins.then_inc(bias_n, 1)
                    dve.wait_ge(bias_n, n * 3 + j + 1)
                    lo, hi = blocks[-1], blocks[0] + 1
                    dve.tensor_scalar(nbias[:, lo:hi], nmax[:, lo:hi], SC, None, ALU.mult).then_inc(biased, 1)

                def turned(n, par, j):
                    _, col, w = TFILLS[j]
                    dve.wait_ge(t_mm, n * 3 + j + 4)
                    if j == 0:
                        dve.wait_ge(av_mm, n + 1)
                    dve.tensor_copy(pt[:, par, col:col + w], TB16[:, 0:w]).then_inc(t_ev, 1)

                def probs_lo(n):
                    dve.wait_ge(exp_done, n * 3 + 4)
                    dve.reciprocal(rinv[:, :], rsum[:, :]).then_inc(recip, 1)
                    dve.wait_ge(pn_hi, n + 1)
                    dve.wait_ge(recip, n + 1)
                    for i in range(TPB):
                        s = slice(PCOL[i], PCOL[i] + (i + 1) * P)
                        ins = dve.scalar_tensor_tensor(out=pn[:, 1, s], in0=ex[:, s], scalar=rinv[:, i:i + 1],
                                                       in1=pn[:, 0, s], op0=ALU.mult, op1=ALU.subtract)
                    ins.then_inc(pn_lo, 1)

                def item(b, h, n, par, h2, b2):
                    q = 1 - par
                    if h2 is not None:
                        low(n + 1, h2, 0, JB[q], q)
                        low(n + 1, h2, 1, JB[1 - q], q)
                    turned(n, par, 0)
                    turned(n, par, 1)
                    if h2 is not None:
                        low(n + 1, h2, 2, JB[q], q)
                    turned(n, par, 2)
                    dve.wait_ge(ao_hi, n + 1)
                    dve.scalar_tensor_tensor(out=at[:, par, 1, :], in0=AO[:, :], scalar=bv[:, ds(h, 1)],
                                             in1=at[:, par, 0, :], op0=ALU.add, op1=ALU.subtract).then_inc(ao_lo, 1)
                    if h2 is not None:
                        for j in range(3):
                            maxima(n + 1, q, j)
                        probs_lo(n + 1)

                def batch(b, last):
                    items(dve, item, lambda: None)(b, last)
                    bo2 = bo[:, :].rearrange("p (a d) -> p a d", a=1).broadcast_to([P, 2, D])
                    dve.wait_ge(wo_mm, b * NI + NI + 2)
                    for i in range(2):
                        f3 = fo[:, i, :].rearrange("p (a d) -> p a d", a=2)
                        dve.wait_ge(o_x, b * 2 + i + 1)
                        dve.tensor_tensor(f3, FB[i][:, :].rearrange("p (a d) -> p a d", a=2), bo2, ALU.add).then_inc(o_b, 1)
                        dve.wait_ge(o_b, b * 2 + i + 3)
                        dve.tensor_tensor(fo[:, i, :], fo[:, i, :],
                                          gate[:, ds(b * TPB + 2 * i, 2), :].rearrange("p t d -> p (t d)"),
                                          ALU.mult).then_inc(o_g, 1)

                for j in range(3):
                    low(0, 0, j, JB[j % 2], 0)
                for j in range(3):
                    maxima(0, 0, j)
                probs_lo(0)
                per_batch(dve, batch)


_OUT = (B, T, D)


def kernel(**inputs):
    import concourse.bacc as bacc
    from concourse.bass_utils import run_bass_kernel_spmd

    i = {k: np.asarray(v) for k, v in inputs.items()}

    def halves(w):
        return np.concatenate([w[0::2], w[1::2]], axis=0)

    def fp4(name):
        codes, scales = i[f"L0_ffn_{name}_W_packed"], i[f"L0_ffn_{name}_scales"]
        if name == "down":
            c = codes.T.reshape(8, P, D).transpose(1, 0, 2)
            s = np.repeat(scales.T.reshape(8, 8, D), 16, axis=1).transpose(1, 0, 2)
        else:
            order = np.arange(MLP).reshape(8, P, 2).transpose(0, 2, 1).reshape(-1)
            c = codes.T[:, order]
            s = np.repeat(scales.T[:, order], 16, axis=0)
        return c.reshape(P, MLP), s.reshape(P, MLP)

    host = {"x": i["L0_attn_x"].reshape(TOK, D)}
    host["wqkv0"] = halves(np.concatenate([i[f"L0_attn_W{n}"].T for n in "qkv"], axis=1))
    host["wo0"] = np.repeat(i["L0_attn_Wo"].T.reshape(4, 4, 1, HD0, D), 2, axis=2).reshape(4, P, D)
    host["bo0"] = i["L0_attn_bo"].reshape(1, D)
    for m, name in enumerate(("gate", "up", "down")):
        host[f"codes{m}"], host[f"scales{m}"] = fp4(name)
    for n in "qkv":
        host[f"w{n}1"] = i[f"L1_attn_w_{n}"]
        host[f"b{n}1"] = i[f"L1_attn_b_{n}"].reshape(H1, HD1).T
    host["wo1"] = i["L1_attn_w_o"]
    host["bo1"] = i["L1_attn_b_o"].reshape(1, D)
    host["gate_w"] = i["L1_ffn_gate_w"].T
    host["expert_bias"] = i["L1_ffn_expert_bias"].reshape(1, E)
    pad = HID1 - E * INTER - SHARED
    for m, (w, s) in enumerate((("w1", "sw1"), ("w3", "sw3"))):
        host[f"w{m}"] = np.concatenate([i[f"L1_ffn_{w}"].transpose(1, 0, 2).reshape(D, E * INTER), i[f"L1_ffn_{s}"],
                                        np.zeros((D, pad), np.float32)], axis=1)
    host["w2"] = np.concatenate([i["L1_ffn_w2"].reshape(E * INTER, D), i["L1_ffn_sw2"], np.zeros((pad, D), np.float32)])
    owner = np.minimum(np.arange(HID1) // INTER, E)
    host["sel"] = (owner[None, :] == np.arange(E + 1)[:, None]).astype(np.float16)

    nc = bacc.Bacc("TRN2", target_bir_lowering=False, num_devices=1)
    arrays, aps = {}, {}
    for name, a in host.items():
        arrays[f"in_{name}"] = np.ascontiguousarray(a)
        aps[name] = nc.dram_tensor(f"in_{name}", a.shape, mybir.dt.from_np(a.dtype), kind="ExternalInput").ap()
    aps["out"] = nc.dram_tensor("out_x", (TOK, D), F32, kind="ExternalOutput").ap()
    network(nc, aps)
    r = run_bass_kernel_spmd(nc, [arrays], core_ids=[0])
    return r.results[0]["out_x"].reshape(_OUT)
```

```python
from contextlib import ExitStack

import concourse.bass as bass
import numpy as np
from concourse import mybir

F32 = mybir.dt.float32
F16 = mybir.dt.float16
BF16 = mybir.dt.bfloat16
I32 = mybir.dt.int32
FP8 = mybir.dt.float8e3
ALU = mybir.AluOpType
ACT = mybir.ActivationFunctionType
AX = mybir.AxisListType
ds = bass.ds

P = 128
B, T, D = 4, 512, 256
TOK = B * T
NT = TOK // P
TPB = T // P
DC = D // P
H0, HD0 = 16, 16
H1, HD1 = 16, 128
MLP = 2048
NCH0 = MLP // P
E, TOPK, G, TOPK_G = 16, 4, 4, 2
EG = E // G
INTER, SHARED = 176, 352
HID1 = 3200
NCH1 = HID1 // P
EPS = 1e-5
MASKED = -1e30
GELU_C, GELU_K = 0.044715, 0.7978845608028654
HEADS = 4
VG = 640
SMAX = [(3, 0), (2, 512), (1, 896), (0, 1152)]
PW = 1280
TFILLS = [([0], 0, 1024), ([1], 1024, 768), ([2, 3], 1792, 768)]


def key_columns():
    where, at = {}, 0
    for blocks, _, _ in TFILLS:
        for kb in blocks:
            w = (TPB - kb) * P
            where[kb] = (at, at + w, w)
            at += 2 * w
    return where


KEYCOL = key_columns()
PCOL = dict(SMAX)


class Count:

    def __init__(self, sem):
        self.sem, self.n = sem, 0

    def __call__(self, ins, by=1):
        ins.then_inc(self.sem, by)
        self.n += by
        return ins

    def wait(self, engine):
        engine.wait_ge(self.sem, self.n)


def split_product(pe, out, lhs, rhs, start, stop):
    mm = None
    n = len(lhs)
    for c in range(n):
        for i, (a, b) in enumerate(((0, 0), (0, 1), (1, 0))):
            mm = pe.matmul(out, lhs[c][a], rhs[c][b], start=start and c == 0 and i == 0,
                           stop=stop and c == n - 1 and i == 2, skip_group_check=True)
    return mm


def layer_norm(nc, ctx, tag, x, xT, ident, eps_tile, psum, interleaved):
    sb = lambda n, s, d: ctx.enter_context(nc.sbuf_tensor(f"{n}_{tag}", s, d))
    sem = lambda n: ctx.enter_context(nc.semaphore(f"{n}_{tag}"))
    stats = sb("stats", [P, NT, 6], F32)
    mv = sb("mv", [P, NT, 2], F32)
    std = sb("std", [P, NT], F32)
    rstd = sb("rstd", [P, NT], F32)
    xn = sb("xn", [P, 2, 2, D], F32)
    parts = sb("xn_parts", [P, 2, 2, 2, DC, P], F16)
    stats_done, std_done, rstd_done = sem("stats_done"), sem("std_done"), sem("rstd_done")
    xn_ready, hi_ready, lo_ready = sem("xn_ready"), sem("xn_hi_ready"), sem("xn_lo_ready")
    turned, copied = sem("xn_turned"), sem("xn_copied")
    xT4 = xT.rearrange("p a c t -> p (a c) t")
    NP = NT // 2

    def as_parts(k):
        v = xn[:, k, :, :].rearrange("p t d -> p (t d)")
        return (v.rearrange("p (t j c) -> p t c j", t=2, c=DC) if interleaved
                else v.rearrange("p (t c j) -> p t c j", t=2, c=DC))

    def pairs(eng, pair):
        pair(0, 0, True, False)
        with eng.Fori(0, NP // 2 - 1) as i:
            pair(i * 2 + 1, 1, False, False)
            pair(i * 2 + 2, 0, False, False)
        pair(NP - 1, 1, False, True)

    with nc.Block() as block:
        @block.scalar
        def _(act):
            act.wait_ge(stats_done, 2 * NT)
            act.activation(std[:, :], mv[:, :, 1], ACT.Sqrt, bias=eps_tile[:, 0:1]).then_inc(std_done, 1)

            def pair(n, k, first, last):
                act.wait_ge(xn_ready, n * 2 + 2)
                act.wait_ge(turned, n + 1)
                act.activation(parts[:, k, 0], as_parts(k), ACT.Copy).then_inc(hi_ready, 1)

            pairs(act, pair)

        @block.vector
        def _(dve):
            for t in range(NT):
                dve.bn_stats(stats[:, t, :], x[:, t, :]).then_inc(stats_done, 1)
            dve.wait_ge(stats_done, NT)
            for t in range(NT):
                dve.bn_aggr(mv[:, t, :], stats[:, t, :]).then_inc(stats_done, 1)
            dve.wait_ge(std_done, 1)
            dve.reciprocal(rstd[:, :], std[:, :]).then_inc(rstd_done, 1)
            dve.wait_ge(rstd_done, 1)
            dve.wait_ge(stats_done, 2 * NT)

            def normalise(n, k):
                for t in range(2):
                    tile = n * 2 + t
                    dve.tensor_scalar(xn[:, k, t, :], x[:, ds(tile, 1), :].rearrange("p a d -> p (a d)"),
                                      mv[:, ds(tile, 1), 0], rstd[:, ds(tile, 1)],
                                      ALU.subtract, ALU.mult).then_inc(xn_ready, 1)

            def copy_out(n, k):
                for t in range(2):
                    dve.wait_ge(turned, n + 3)
                    dve.tensor_copy(xT4[:, :, ds((n * 2 + t) * P, P)],
                                    psum[k * 2 + t][:, :].bitcast(F16)[:, 0:4 * P].rearrange("p (a t) -> p a t", a=4)
                                    ).then_inc(copied, 1)

            def pair(n, k, first, last):
                if not last:
                    if not first:
                        dve.wait_ge(lo_ready, n)
                    normalise(n + 1, 1 - k)
                dve.wait_ge(hi_ready, n + 1)
                dve.wait_ge(xn_ready, n * 2 + 2)
                dve.tensor_tensor(parts[:, k, 1], as_parts(k), parts[:, k, 0], ALU.subtract).then_inc(lo_ready, 1)
                if not first:
                    copy_out(n - 1, 1 - k)

            normalise(0, 0)
            pairs(dve, pair)
            copy_out(NP - 1, 1)

        @block.tensor
        def _(pe):
            pe.sem_inc(turned, 2)
            pe.sem_inc(copied, 4)

            def pair(n, k, first, last):
                pe.wait_ge(lo_ready, n + 1)
                pe.wait_ge(copied, n * 2 + 2)
                for t in range(2):
                    for a in range(2):
                        for c in range(DC):
                            q = (a * DC + c) * P
                            mm = pe.transpose(psum[k * 2 + t][:, :].bitcast(F16)[:, q:q + P], parts[:, k, a, t, c, :],
                                              ident[:, :])
                mm.then_inc(turned, 1)

            pairs(pe, pair)


def network(nc, A):
    ctx = ExitStack()
    with ctx:
        def sbp(name, shape, dt, c=ctx):
            return c.enter_context(nc.sbuf_tensor("s_" + name, shape, dt))

        x = sbp("x", [P, NT, D], F32)
        xT = sbp("xT", [P, 2, DC, TOK], F16)
        ident = sbp("ident", [P, P], F16)
        ident_b = sbp("ident_b", [P, P], BF16)
        causal = sbp("causal", [P, P], BF16)
        zeros = sbp("zeros", [P, P], F16)
        eps_tile = sbp("eps", [P, 1], F32)
        psum = [ctx.enter_context(nc.psum_tensor(f"bank{i}", [P, 512], F32)) for i in range(8)]

        ffn_ctx = ExitStack()
        ctx.enter_context(ffn_ctx)
        wffn = [sbp(f"wffn{m}", [P, 2, DC, MLP], F16, ffn_ctx) for m in range(2)]
        wdown = sbp("wdown", [P, 2, NCH0, D], F16, ffn_ctx)
        wqkv = sbp("wqkv", [P, 2, DC, 3 * D], F16, ffn_ctx)
        wo = sbp("wo", [P, 2, HEADS, D], F16, ffn_ctx)
        bo = sbp("bo", [P, D], F32, ffn_ctx)
        prepare_block0(nc, A, x, ident, ident_b, causal, zeros, eps_tile, wffn, wdown, wqkv, wo, bo)
        with ExitStack() as c:
            layer_norm(nc, c, "ln0", x, xT, ident, eps_tile, psum, True)
        block0(nc, A, x, xT, ident, ident_b, causal, zeros, wffn, wdown, wqkv, wo, bo, psum)
        ffn_ctx.close()
        with ExitStack() as c:
            layer_norm(nc, c, "ln1", x, xT, ident, eps_tile, psum, False)
        gate = sbp("gate", [P, NT, D], F32)
        experts(nc, A, xT, ident, zeros, gate, psum)
        attention1(nc, A, x, xT, ident, ident_b, causal, zeros, gate, psum)


def split_weights(nc, jobs, tag, extra=()):
    with ExitStack() as c:
        n = len(jobs)
        loaded = [c.enter_context(nc.semaphore(f"w_loaded{i}_{tag}")) for i in range(n)]
        hi_done = c.enter_context(nc.semaphore(f"w_hi_{tag}"))
        other = c.enter_context(nc.semaphore(f"w_other_{tag}"))
        with nc.Block() as block:
            @block.sync
            def _(sp):
                for i, (src, st, _, _) in enumerate(jobs):
                    sp.dma_start(st, src).then_inc(loaded[i], 16)
                for dst, src in extra:
                    sp.dma_start(dst, src).then_inc(other, 16)
                if extra:
                    sp.wait_ge(other, 16 * len(extra))

            @block.scalar
            def _(act):
                for i, (_, st, hi, _) in enumerate(jobs):
                    act.wait_ge(loaded[i], 16)
                    act.activation(hi, st, ACT.Copy).then_inc(hi_done, 1)

            def low(eng, mine):
                for i in mine:
                    _, st, hi, lo = jobs[i]
                    eng.wait_ge(loaded[i], 16)
                    eng.wait_ge(hi_done, i + 1)
                    eng.tensor_tensor(lo, st, hi, ALU.subtract)

            @block.vector
            def _(dve):
                low(dve, [i for i in range(n) if i % 3 != 2])

            @block.gpsimd
            def _(pool):
                low(pool, [i for i in range(n) if i % 3 == 2])


def prepare_block0(nc, A, x, ident, ident_b, causal, zeros, eps_tile, wffn, wdown, wqkv, wo, bo):
    with ExitStack() as c:
        sb = lambda n, s, d: c.enter_context(nc.sbuf_tensor("p0_" + n, s, d))
        sem = lambda n: c.enter_context(nc.semaphore("p0_" + n))
        codes = [sb(f"codes{m}", [P, MLP], I32) for m in range(3)]
        scales = [sb(f"scales{m}", [P, MLP], F32) for m in range(3)]
        mag = sb("mag", [P, MLP], I32)
        sign = sb("sign", [P, MLP], I32)
        byte = sb("byte", [P, 2, MLP], I32)
        w32 = sb("w32", [P, 2, MLP], F32)
        qst = sb("qst", [P, DC, 3 * D], F32)
        ost = sb("ost", [P, HEADS, D], F32)
        loaded = [sem(f"fp4_loaded{m}") for m in range(3)]
        loaded_q, other, made = sem("qkvo_loaded"), sem("other_loaded"), sem("constants_made")
        bits, w_ready, hi_ready, lo_ready = sem("bits"), sem("w_ready"), sem("w_hi_ready"), sem("w_lo_ready")
        lo_q = sem("q_lo")

        def target(m, nib):
            if m < 2:
                return wffn[m][:, 0, nib, :], wffn[m][:, 1, nib, :]
            v = wdown[:, :, :, :].rearrange("p a (j n) d -> p a n j d", n=2)
            return v[:, 0, nib, :, :], v[:, 1, nib, :, :]

        def shaped(m, ap):
            return ap if m < 2 else ap.rearrange("p (j d) -> p j d", d=D)

        with nc.Block() as block:
            @block.sync
            def _(sp):
                for m in range(3):
                    sp.dma_start(codes[m][:, :], A[f"codes{m}"]).then_inc(loaded[m], 16)
                    sp.dma_start(scales[m][:, :], A[f"scales{m}"]).then_inc(loaded[m], 16)
                sp.dma_start(x[:, :, :], A["x"].rearrange("(t p) d -> p t d", p=P)).then_inc(other, 16)
                sp.dma_start(bo[:, :], A["bo0"].broadcast_to([P, D])).then_inc(other, 16)
                sp.wait_ge(other, 2 * 16)

            @block.scalar
            def _(act):
                act.dma_start(qst[:, :, :], A["wqkv0"].rearrange("(c p) n -> p c n", p=P)).then_inc(loaded_q, 16)
                act.dma_start(ost[:, :, :], A["wo0"].rearrange("g p n -> p g n")).then_inc(loaded_q, 16)
                act.wait_ge(loaded_q, 32)
                act.activation(wqkv[:, 0, :, :], qst[:, :, :], ACT.Copy).then_inc(hi_ready, 1)
                act.activation(wo[:, 0, :, :], ost[:, :, :], ACT.Copy).then_inc(hi_ready, 1)
                for m in range(3):
                    for nib in range(2):
                        act.wait_ge(w_ready, 2 * m + nib + 1)
                        act.activation(target(m, nib)[0], shaped(m, w32[:, nib, :]), ACT.Copy).then_inc(hi_ready, 1)

            @block.gpsimd
            def _(pool):
                pool.memset(zeros[:, :], 0.0)
                pool.memset(eps_tile[:, :], EPS)
                for m in (ident, ident_b, causal):
                    pool.memset(m[:, :], 0.0).then_inc(made, 1)
                pool.wait_ge(made, 3)
                for m in (ident, ident_b):
                    pool.affine_select(out=m[:, :], in_=m[:, :], compare_op=ALU.not_equal, fill=1.0, base=0,
                                       pattern=[[-1, P]], channel_multiplier=1)
                pool.affine_select(out=causal[:, :], in_=causal[:, :], compare_op=ALU.is_ge, fill=MASKED, base=0,
                                   pattern=[[-1, P]], channel_multiplier=1)
                pool.wait_ge(loaded_q, 32)
                pool.wait_ge(hi_ready, 2)
                pool.tensor_tensor(wqkv[:, 1, :, :], qst[:, :, :], wqkv[:, 0, :, :], ALU.subtract)
                pool.tensor_tensor(wo[:, 1, :, :], ost[:, :, :], wo[:, 0, :, :], ALU.subtract)
                for m in range(3):
                    for nib in range(2):
                        pool.wait_ge(w_ready, 2 * m + nib + 1)
                        pool.wait_ge(hi_ready, 2 * m + nib + 3)
                        hi, lo = target(m, nib)
                        pool.tensor_tensor(lo, shaped(m, w32[:, nib, :]), hi, ALU.subtract).then_inc(lo_ready, 1)

            @block.vector
            def _(dve):
                done = Count(bits)
                for m in range(3):
                    cd = codes[m][:, :]
                    dve.wait_ge(loaded[m], 32)
                    done(dve.tensor_scalar(mag[:, :], cd, 7, 3, ALU.bitwise_and, ALU.logical_shift_left))
                    done(dve.tensor_scalar(sign[:, :], cd, 4, 128, ALU.logical_shift_left, ALU.bitwise_and))
                    done.wait(dve)
                    done(dve.tensor_tensor(byte[:, 0, :], mag[:, :], sign[:, :], ALU.bitwise_or))
                    done.wait(dve)
                    done(dve.tensor_scalar(mag[:, :], cd, 1, 56, ALU.logical_shift_right, ALU.bitwise_and))
                    done(dve.tensor_scalar(sign[:, :], cd, 128, None, ALU.bitwise_and))
                    done.wait(dve)
                    done(dve.tensor_tensor(byte[:, 1, :], mag[:, :], sign[:, :], ALU.bitwise_or))
                    done.wait(dve)
                    for nib in range(2):
                        if m:
                            dve.wait_ge(lo_ready, 2 * (m - 1) + nib + 1)
                        dve.scalar_tensor_tensor(out=w32[:, nib, :],
                                                 in0=byte[:, nib, :].bitcast(FP8)[:, 0:4 * MLP:4], scalar=4.0,
                                                 in1=scales[m][:, :], op0=ALU.mult, op1=ALU.mult).then_inc(w_ready, 1)
                    dve.wait_ge(w_ready, 2 * m + 2)


def block0(nc, A, x, xT, ident, ident_b, causal, zeros, wffn, wdown, wqkv, wo, bo, psum):
    SC = HD0 ** -0.5
    STK = 48
    with ExitStack() as c:
        sb = lambda n, s, d: c.enter_context(nc.sbuf_tensor("b0_" + n, s, d))
        sem = lambda n: c.enter_context(nc.semaphore("b0_" + n))
        raw = sb("raw", [P, 2, 4, T], F16)
        qs = sb("qs", [P, H0, T], F16)
        ks = sb("ks", [P, H0, T], F16)
        vm = sb("vm", [P, TPB, HEADS, VG], F16)
        ex = sb("ex", [P, PW], F32)
        pn = sb("pn", [P, 2, 2, PW], F16)
        pt = sb("pt", [P, 2, 2 * PW], F16)
        nmax = sb("nmax", [P, TPB], F32)
        rsum, rinv = sb("rsum", [P, TPB], F32), sb("rinv", [P, TPB], F32)
        at = sb("at", [P, 2, HEADS, T], F16)
        g4 = sb("g4", [P, 4, T], F32)
        gsq, ga, gt, gb = (g4[:, i, :] for i in range(4))
        et, eb = g4[:, 0:2, :], g4[:, 2:4, :]
        gp = sb("gp", [P, T], F32)
        hT = sb("hT", [P, 2, 2, T], F16)
        scr = nc.dram_tensor("qk_parts", [2, 4, P, T], F16, kind="Internal").ap()

        SB, TB, GB, UB, AO, FB = psum[0:2], psum[2], psum[3], psum[4], psum[5], psum[6:8]
        TB16 = TB[:, :].bitcast(F16)

        raw_hi, raw_lo, raw_out = sem("raw_hi"), sem("raw_lo"), sem("raw_out")
        qk_mm, v_mm, v_hi, v_lo = sem("qk_mm"), sem("v_mm"), sem("v_hi"), sem("v_lo")
        stacked = [sem("stacked0"), sem("stacked1")]
        stack_zero, vm_zero = sem("stack_zero"), sem("vm_zero")
        s_mm, nmax_done, exp_done = sem("s_mm"), sem("nmax_done"), sem("exp_done")
        recip, pn_hi, pn_lo = sem("recip"), sem("pn_hi"), sem("pn_lo")
        t_mm, t_ev, av_mm = sem("t_mm"), sem("t_evacuated"), sem("av_mm")
        ao_hi, ao_lo = sem("ao_hi"), sem("ao_lo")
        g_mm, u_mm, sq_r, ga_r, gt_r, gb_r, gp_r, h_hi, h_lo, d_mm = (
            sem(n) for n in ("g_mm", "u_mm", "sq", "ga", "gt", "gb", "gp", "h_hi", "h_lo", "d_mm"))
        wo_mm, e_t, e_b, e_s, e_q, e_x = (sem(n) for n in ("wo_mm", "e_tanh", "e_b", "e_s", "e_q", "e_x"))

        def per_batch(eng, body):
            with eng.Fori(0, B - 1) as b:
                body(b, False)
            body(B - 1, True)

        def per_group(eng, b, last, item):
            for k in range(HEADS):
                item(0, k, "first" if k == 0 else "inner")
            with eng.Fori(1, 3) as g:
                for k in range(HEADS):
                    item(g, k, "inner")
            for k in range(HEADS):
                item(3, k, "inner" if k < 3 else "end" if last else "last")

        def item_no(b, g, k):
            return b * 16 + g * 4 + k

        def turned(eng, n, par, j):
            _, col, w = TFILLS[j]
            eng.wait_ge(t_mm, n * 3 + j + 5)
            eng.wait_ge(av_mm, n + 1)
            if j < 2:
                eng.tensor_copy(pt[:, par, col:col + w], TB16[:, 0:w]).then_inc(t_ev, 1)
            else:
                eng.activation(pt[:, par, col:col + w], TB16[:, 0:w], ACT.Copy).then_inc(t_ev, 1)

        with nc.Block() as block:
            @block.sync
            def _(sp):
                def spill(n):
                    for ch in range(4):
                        sp.wait_ge(raw_hi, n * 4 + ch + 1)
                        sp.wait_ge(raw_lo, n * 4 + ch + 1)
                        for a in range(2):
                            sp.dma_start(scr[a, ch], raw[:, a, ch, :]).then_inc(raw_out, 16)
                    sp.wait_ge(raw_out, n * 128 + 128)

                def stack(half):
                    h = slice(half * 8, half * 8 + 8)
                    for row, a in enumerate((0, 1, 0)):
                        sp.dma_start(qs[16 * row:16 * row + 16, h, :],
                                     scr[a, half].rearrange("(h d) t -> d h t", d=HD0)).then_inc(stacked[half], 16)
                    for row, a in enumerate((0, 0, 1)):
                        sp.dma_start(ks[16 * row:16 * row + 16, h, :],
                                     scr[a, 2 + half].rearrange("(h d) t -> d h t", d=HD0)).then_inc(stacked[half], 16)

                sp.wait_ge(stack_zero, 2)
                spill(0)
                stack(0)
                stack(1)
                with sp.Fori(0, B - 1) as b:
                    for half in range(2):
                        sp.wait_ge(stacked[half], b * 96 + 96)
                    spill(b + 1)
                    sp.wait_ge(s_mm, b * 48 + 24)
                    stack(0)
                    sp.wait_ge(s_mm, b * 48 + 48)
                    stack(1)
                sp.wait_ge(stacked[0], 96 * B)
                sp.wait_ge(stacked[1], 96 * B)

            @block.gpsimd
            def _(pool):
                for s, credit in ((exp_done, 1), (pn_lo, TPB), (t_mm, 4), (t_ev, 1), (av_mm, 2), (ao_lo, 1), (gb_r, 1),
                                  (gp_r, 1), (h_lo, 1), (d_mm, 2), (wo_mm, 2), (e_s, 2), (e_b, 2), (e_x, 2)):
                    pool.sem_inc(s, credit)
                pool.memset(qs[:, :, :], 0.0).then_inc(stack_zero, 1)

                def item(b, g, k):
                    n = item_no(b, g, k)
                    pool.wait_ge(gp_r, n + 2)
                    pool.wait_ge(h_hi, n + 1)
                    pool.tensor_tensor(hT[:, k % 2, 1, :], gp[:, :], hT[:, k % 2, 0, :], ALU.subtract).then_inc(h_lo, 1)

                def body(b, last):
                    with pool.Fori(0, 4) as g:
                        for k in range(HEADS):
                            item(b, g, k)
                    for i in range(2):
                        pool.wait_ge(e_q, b * 2 + i + 1)
                        xv = x[:, ds(b * TPB + 2 * i, 2), :].rearrange("p t d -> p (t d)")
                        pool.tensor_tensor(xv, xv, eb[:, i, :], ALU.add).then_inc(e_x, 1)

                with pool.Fori(0, B) as b:
                    body(b, False)

            @block.tensor
            def _(pe):
                def project_qk(b, n, after_v=None):
                    for ch in range(4):
                        if ch == 1 and after_v is not None:
                            pe.wait_ge(v_lo, after_v)
                        bank = (GB, UB)[ch % 2]
                        if ch >= 2:
                            pe.wait_ge(raw_lo, n * 4 + ch - 1)
                        col = (ch // 2) * D + (ch % 2) * P
                        split_product(pe, bank[:, :],
                                      [[wqkv[:, a, c2, col:col + P] for a in range(2)] for c2 in range(DC)],
                                      [[xT[:, a, c2, ds(b * T, T)] for a in range(2)] for c2 in range(DC)],
                                      True, True).then_inc(qk_mm, 1)

                def project_v(b):
                    for t in range(TPB):
                        bank = (GB, UB)[t % 2]
                        if t >= 2:
                            pe.wait_ge(v_lo, b * 4 + t - 1)
                        split_product(pe, bank[:, 0:D],
                                      [[xT[:, a, c2, ds(b * T + t * P, P)] for a in range(2)] for c2 in range(DC)],
                                      [[wqkv[:, a, c2, 2 * D:3 * D] for a in range(2)] for c2 in range(DC)],
                                      True, True).then_inc(v_mm, 1)

                def scores(n, j, h, par, first=False):
                    bank = SB[(par + j) % 2]
                    if not (first and j < 2):
                        pe.wait_ge(exp_done, n * 3 + j)
                    at_col = 0
                    for i in ((3,), (2,), (1, 0))[j]:
                        w = (i + 1) * P
                        o = bank[:, at_col:at_col + w]
                        pe.matmul(o, qs[:, ds(h, 1), i * P:(i + 1) * P].rearrange("p a t -> p (a t)"),
                                  ks[:, ds(h, 1), 0:w].rearrange("p a t -> p (a t)"), start=True, stop=False,
                                  skip_group_check=True)
                        mm = pe.matmul(bank[:, at_col + i * P:at_col + w], ident_b[:, :], causal[:, :], start=False,
                                       stop=True, skip_group_check=True)
                        at_col += w
                    mm.then_inc(s_mm, 1)

                def turn(n, j, par):
                    pe.wait_ge(t_ev, n * 3 + j + 1)
                    blocks, _, _ = TFILLS[j]
                    col = 0
                    for kb in blocks:
                        for a in range(2):
                            for i in range(kb, TPB):
                                src = PCOL[i] + kb * P
                                mm = pe.transpose(TB16[:, col:col + P], pn[:, par, a, src:src + P], ident[:, :])
                                col += P
                    mm.then_inc(t_mm, 1)

                def weighted(n, b, g, k):
                    if k == 0:
                        pe.wait_ge(ao_lo, b * 4 + g + 1)
                    for kb in range(TPB):
                        if kb < 3:
                            pe.wait_ge(t_ev, n * 3 + min(kb, 2) + 2)
                        for a in range(2):
                            c0, c1, w = KEYCOL[kb]
                            col = (c0, c1)[a]
                            mm = pe.matmul(AO[:, kb * P:T],
                                           vm[:, kb, ds(g, 1), k * P:(k + 1) * P].rearrange("p a t -> p (a t)"),
                                           pt[:, k % 2, col:col + w],
                                           start=(k == 0 and kb == 0 and a == 0), stop=(k == 3 and kb == 3 and a == 1),
                                           skip_group_check=True)
                    mm.then_inc(av_mm, 1)

                def down(n, ch, par):
                    pe.wait_ge(h_lo, n + 2)
                    for t in range(TPB):
                        mm = split_product(pe, FB[t // 2][:, (t % 2) * D:(t % 2 + 1) * D],
                                           [[hT[:, par, a, t * P:(t + 1) * P] for a in range(2)]],
                                           [[wdown[:, a, ds(ch, 1), :].rearrange("p a t -> p (a t)")
                                             for a in range(2)]], False, False)
                    mm.then_inc(d_mm, 1)

                project_qk(0, 0)
                pe.wait_ge(raw_lo, 4)
                for half in range(2):
                    pe.wait_ge(stacked[half], 96)
                for j in range(3):
                    scores(0, j, 0, 0, first=True)

                def batch(b, last):
                    pe.wait_ge(e_s, b * 2 + 2)
                    pe.wait_ge(e_b, b * 2 + 2)
                    project_v(b)
                    for f in range(2):
                        pe.matmul(FB[f][:, :], zeros[:, :], xT[:, 0, 0, 0:T], start=True, stop=False,
                                  skip_group_check=True)
                    if not last:
                        pe.wait_ge(raw_out, b * 128 + 128)
                        pe.wait_ge(v_lo, b * 4 + 3)
                        project_qk(b + 1, b + 1, after_v=b * 4 + 4)

                    def item(g, k, kind):
                        n = item_no(b, g, k)
                        par = (k + 1) % 2

                        def hidden(m):
                            bank, s = ((GB, g_mm), (UB, u_mm))[m]
                            if kind == "first":
                                if last:
                                    pe.wait_ge(v_lo, b * 4 + 4)
                                else:
                                    pe.wait_ge(raw_lo, b * 4 + 8)
                            pe.wait_ge((gb_r, gp_r)[m], n + 1)
                            split_product(pe, bank[:, :],
                                          [[wffn[m][:, a, c2, ds(g * 512 + k * P, P)] for a in range(2)] for c2 in range(DC)],
                                          [[xT[:, a, c2, ds(b * T, T)] for a in range(2)] for c2 in range(DC)],
                                          True, True).then_inc(s, 1)

                        have = kind != "end"
                        h = g * 4 + k + 1 if kind != "last" else 0
                        if kind == "last":
                            pe.wait_ge(stacked[0], b * 96 + 192)
                        if k == 3 and kind == "inner":
                            pe.wait_ge(stacked[1], b * 96 + 96)
                        if have:
                            scores(n + 1, 0, h, par)
                            scores(n + 1, 1, h, par)
                        pe.wait_ge(pn_lo, n * TPB + 2 * TPB)
                        turn(n, 0, k % 2)
                        hidden(0)
                        if have:
                            scores(n + 1, 2, h, par)
                        hidden(1)
                        turn(n, 1, k % 2)
                        if kind != "first":
                            down(n - 1, g * 4 + k - 1, 1 - k % 2)
                        turn(n, 2, k % 2)
                        weighted(n, b, g, k)

                    per_group(pe, b, last, item)
                    down(b * 16 + 15, 15, 1)
                    pe.wait_ge(gb_r, b * 16 + 17)
                    pe.wait_ge(gp_r, b * 16 + 17)
                    pe.wait_ge(ao_lo, b * 4 + 5)
                    for t in range(TPB):
                        mm = split_product(pe, (GB, UB)[t // 2][:, (t % 2) * D:(t % 2 + 1) * D],
                                           [[at[:, a, gg, t * P:(t + 1) * P] for a in range(2)] for gg in range(4)],
                                           [[wo[:, a, gg, :] for a in range(2)] for gg in range(4)], True, True)
                        if t % 2:
                            mm.then_inc(wo_mm, 1)

                per_batch(pe, batch)

            @block.scalar
            def _(act):
                def raw_parts(n):
                    for ch in range(4):
                        act.wait_ge(qk_mm, n * 4 + ch + 1)
                        act.activation(raw[:, 0, ch, :], (GB, UB)[ch % 2][:, :], ACT.Copy,
                                       scale=SC if ch < 2 else 1.0).then_inc(raw_hi, 1)

                def softmax_exp(n, par, js):
                    for j in js:
                        blocks = ((3,), (2,), (1, 0))[j]
                        col = 0
                        act.wait_ge(nmax_done, n * 3 + j + 1)
                        act.wait_ge(pn_lo, n * TPB + TPB - blocks[-1])
                        for i in blocks:
                            w = (i + 1) * P
                            ins = act.activation(ex[:, PCOL[i]:PCOL[i] + w], SB[(par + j) % 2][:, col:col + w], ACT.Exp,
                                                 bias=nmax[:, i:i + 1], accum_out=rsum[:, i:i + 1])
                            col += w
                        ins.then_inc(exp_done, 1)

                def probs_hi(n, par, blocks):
                    act.wait_ge(recip, n + 1)
                    act.wait_ge(exp_done, n * 3 + 4)
                    act.wait_ge(t_mm, n * 3 + 1)
                    for i in reversed(blocks):
                        act.activation(pn[:, par, 0, PCOL[i]:PCOL[i] + (i + 1) * P],
                                       ex[:, PCOL[i]:PCOL[i] + (i + 1) * P], ACT.Copy,
                                       scale=rinv[:, i:i + 1]).then_inc(pn_hi, 1)

                raw_parts(0)
                softmax_exp(0, 0, (0, 1, 2))
                probs_hi(0, 0, range(TPB))

                def batch(b, last):
                    for t in range(TPB):
                        act.wait_ge(v_mm, b * 4 + t + 1)
                        if t == 0:
                            act.wait_ge(av_mm, b * 16 + 2)
                            act.wait_ge(vm_zero, 1)
                        v4 = vm[:, t, :, :].rearrange("p g (k e) -> p g k e", e=160)
                        act.activation(v4[:, :, :, 0:16], (GB, UB)[t % 2][:, 0:D].rearrange("p (g k d) -> p g k d", g=4, k=4),
                                       ACT.Copy).then_inc(v_hi, 1)

                    if not last:
                        raw_parts(b + 1)

                    def item(g, k, kind):
                        n = item_no(b, g, k)
                        have = kind != "end"
                        if have:
                            softmax_exp(n + 1, (k + 1) % 2, (0, 1))
                        act.wait_ge(g_mm, n + 1)
                        if kind == "first":
                            act.wait_ge(e_x, b * 2 + 2)
                        act.activation(gsq, GB[:, :], ACT.Square).then_inc(sq_r, 1)
                        if have:
                            softmax_exp(n + 1, (k + 1) % 2, (2,))
                        act.wait_ge(ga_r, n + 1)
                        act.activation(gt, ga, ACT.Tanh, scale=GELU_K * GELU_C).then_inc(gt_r, 1)
                        if have:
                            probs_hi(n + 1, (k + 1) % 2, (2, 3))
                        turned(act, n, k % 2, 2)
                        if have:
                            probs_hi(n + 1, (k + 1) % 2, (0, 1))
                        act.wait_ge(gp_r, n + 2)
                        act.wait_ge(d_mm, n + 1)
                        act.activation(hT[:, k % 2, 0, :], gp[:, :], ACT.Copy).then_inc(h_hi, 1)
                        if k == 3:
                            act.wait_ge(av_mm, n + 3)
                            act.wait_ge(wo_mm, b * 2 + 2)
                            act.activation(at[:, 0, ds(g, 1), :].rearrange("p a t -> p (a t)"), AO[:, :],
                                           ACT.Copy).then_inc(ao_hi, 1)

                    per_group(act, b, last, item)
                    for i in range(2):
                        act.wait_ge(d_mm, b * 16 + 18)
                        act.activation(et[:, i, :], FB[i][:, :], ACT.Tanh, scale=0.5).then_inc(e_t, 1)

                per_batch(act, batch)

            @block.vector
            def _(dve):
                def raw_parts(n):
                    for ch in range(4):
                        dve.wait_ge(raw_hi, n * 4 + ch + 1)
                        dve.scalar_tensor_tensor(out=raw[:, 1, ch, :], in0=(GB, UB)[ch % 2][:, :],
                                                 scalar=SC if ch < 2 else 1.0, in1=raw[:, 0, ch, :],
                                                 op0=ALU.mult, op1=ALU.subtract).then_inc(raw_lo, 1)

                def maxima(n, par, j):
                    dve.wait_ge(s_mm, n * 3 + j + 1)
                    if j == 0:
                        dve.wait_ge(exp_done, n * 3 + 1)
                    blocks = ((3,), (2,), (1, 0))[j]
                    col = 0
                    for i in blocks:
                        w = (i + 1) * P
                        ins = dve.tensor_reduce(nmax[:, i:i + 1], SB[(par + j) % 2][:, col:col + w], axis=AX.X,
                                                op=ALU.max, negate=True)
                        col += w
                    ins.then_inc(nmax_done, 1)

                def reciprocals(n):
                    dve.wait_ge(exp_done, n * 3 + 4)
                    dve.reciprocal(rinv[:, :], rsum[:, :]).then_inc(recip, 1)

                def probs_lo(n, par, blocks):
                    dve.wait_ge(recip, n + 1)
                    for i in reversed(blocks):
                        dve.wait_ge(pn_hi, n * TPB + TPB - i)
                        s = slice(PCOL[i], PCOL[i] + (i + 1) * P)
                        dve.scalar_tensor_tensor(out=pn[:, par, 1, s], in0=ex[:, s], scalar=rinv[:, i:i + 1],
                                                 in1=pn[:, par, 0, s], op0=ALU.mult, op1=ALU.subtract).then_inc(pn_lo, 1)

                dve.memset(ks[:, :, :], 0.0).then_inc(stack_zero, 1)
                raw_parts(0)
                dve.memset(vm[:, :, :, :], 0.0).then_inc(vm_zero, 1)
                for j in range(3):
                    maxima(0, 0, j)
                reciprocals(0)
                probs_lo(0, 0, range(TPB))

                def batch(b, last):
                    for t in range(TPB):
                        dve.wait_ge(v_hi, b * 4 + t + 1)
                        v4 = vm[:, t, :, :].rearrange("p g (k e) -> p g k e", e=160)
                        dve.tensor_tensor(v4[:, :, :, 16:32], (GB, UB)[t % 2][:, 0:D].rearrange("p (g k d) -> p g k d", g=4, k=4),
                                          v4[:, :, :, 0:16], ALU.subtract).then_inc(v_lo, 1)

                    if not last:
                        raw_parts(b + 1)

                    def item(g, k, kind):
                        n = item_no(b, g, k)
                        have = kind != "end"
                        par = (k + 1) % 2
                        if have:
                            maxima(n + 1, par, 0)
                            maxima(n + 1, par, 1)
                        turned(dve, n, k % 2, 0)
                        if have:
                            maxima(n + 1, par, 2)
                        dve.wait_ge(sq_r, n + 1)
                        dve.scalar_tensor_tensor(out=ga, in0=gsq, scalar=1.0 / GELU_C, in1=GB[:, :],
                                                 op0=ALU.add, op1=ALU.mult).then_inc(ga_r, 1)
                        if have:
                            reciprocals(n + 1)
                        turned(dve, n, k % 2, 1)
                        dve.wait_ge(gt_r, n + 1)
                        dve.scalar_tensor_tensor(out=gb, in0=gt, scalar=1.0, in1=GB[:, :],
                                                 op0=ALU.add, op1=ALU.mult).then_inc(gb_r, 1)
                        if have:
                            probs_lo(n + 1, par, (3,))
                        dve.wait_ge(u_mm, n + 1)
                        dve.wait_ge(gb_r, n + 2)
                        dve.wait_ge(h_lo, n + 1)
                        dve.scalar_tensor_tensor(out=gp[:, :], in0=gb, scalar=0.5, in1=UB[:, :],
                                                 op0=ALU.mult, op1=ALU.mult).then_inc(gp_r, 1)
                        if have:
                            probs_lo(n + 1, par, (0, 1, 2))
                        if k == 3:
                            dve.wait_ge(ao_hi, b * 4 + g + 1)
                            dve.tensor_tensor(at[:, 1, ds(g, 1), :].rearrange("p a t -> p (a t)"), AO[:, :],
                                              at[:, 0, ds(g, 1), :].rearrange("p a t -> p (a t)"),
                                              ALU.subtract).then_inc(ao_lo, 1)

                    per_group(dve, b, last, item)
                    bo2 = bo[:, :].rearrange("p (a d) -> p a d", a=1).broadcast_to([P, 2, D])
                    for i in range(2):
                        dve.wait_ge(e_t, b * 2 + i + 1)
                        dve.wait_ge(e_x, b * 2 + i + 1)
                        dve.scalar_tensor_tensor(out=eb[:, i, :], in0=et[:, i, :], scalar=1.0, in1=FB[i][:, :],
                                                 op0=ALU.add, op1=ALU.mult).then_inc(e_b, 1)
                        dve.wait_ge(wo_mm, b * 2 + i + 3)
                        dve.wait_ge(e_b, b * 2 + i + 3)
                        dve.tensor_tensor(et[:, i, :].rearrange("p (a d) -> p a d", a=2),
                                          (GB, UB)[i][:, :].rearrange("p (a d) -> p a d", a=2), bo2,
                                          ALU.add).then_inc(e_s, 1)
                        dve.wait_ge(e_s, b * 2 + i + 3)
                        dve.scalar_tensor_tensor(out=eb[:, i, :], in0=et[:, i, :], scalar=0.5, in1=eb[:, i, :],
                                                 op0=ALU.mult, op1=ALU.mult).then_inc(e_q, 1)

                per_batch(dve, batch)


def experts(nc, A, xT, ident, zeros, gate, psum):
    with ExitStack() as c:
        sb = lambda n, s, d: c.enter_context(nc.sbuf_tensor("m_" + n, s, d))
        sem = lambda n: c.enter_context(nc.semaphore("m_" + n))
        w13 = [sb(f"w{m}", [P, 2, DC, HID1], F16) for m in range(2)]
        w2 = sb("w2", [P, 2, NCH1, D], F16)
        wg = sb("wg", [P, 2, DC, E], F16)
        sel = sb("sel", [E + 1, HID1], F16)
        share = sb("share", [E + 1, 2, TOK], F16)
        bias = sb("bias", [P, E], F32)
        with ExitStack() as c2:
            st = [c2.enter_context(nc.sbuf_tensor(f"m_stage{i}", [P, HID1], F32)) for i in range(2)]
            st2 = c2.enter_context(nc.sbuf_tensor("m_stage_w2", [P, 5, D], F32))
            stg = c2.enter_context(nc.sbuf_tensor("m_stage_gate", [P, DC, E], F32))
            extra = [(sel[:, :], A["sel"]), (bias[:, :], A["expert_bias"].broadcast_to([P, E]))]
            for m in range(2):
                split_weights(nc, [(A[f"w{m}"][cc * P:(cc + 1) * P, :], st[cc][:, :], w13[m][:, 0, cc, :],
                                    w13[m][:, 1, cc, :]) for cc in range(2)], f"moe{m}")
            for q in range(NCH1 // 5):
                jobs = [(A["w2"][q * 5 * P:(q + 1) * 5 * P, :].rearrange("(c p) d -> p c d", p=P), st2[:, :, :],
                         w2[:, 0, q * 5:(q + 1) * 5, :], w2[:, 1, q * 5:(q + 1) * 5, :])]
                if q == 0:
                    jobs.append((A["gate_w"].rearrange("(c p) e -> p c e", p=P), stg[:, :, :], wg[:, 0, :, :],
                                 wg[:, 1, :, :]))
                split_weights(nc, jobs, f"moe2{q}", extra if q == 0 else ())
        route(nc, xT, wg, bias, ident, share, psum)

        gt, gb, gp = (sb(n, [P, 2, T], F32) for n in ("gt", "gb", "gp"))
        hT = sb("hT", [P, 2, 2, T], F16)
        et, eb = sb("et", [P, 2, T], F32), sb("eb", [P, 2, T], F32)
        GB, UB, CB, FB = psum[0:2], psum[2:4], psum[4:6], psum[6:8]
        g_mm, u_mm, c_mm, gt_r, gb_r, gu_r, gp_r, h_hi, h_lo, d_mm, e_t, e_b, e_g = (
            sem(n) for n in ("g_mm", "u_mm", "c_mm", "tanh", "gb", "gu", "gp", "h_hi", "h_lo", "d_mm", "e_tanh",
                             "e_b", "e_gate"))

        def chunks(eng, b, item, tail=lambda: None):
            item(0, b * NCH1, 0, True)
            with eng.Fori(0, NCH1 // 2) as i:
                for k in range(2):
                    item(i * 2 + k + 1, b * NCH1 + i * 2 + k + 1, (k + 1) % 2, False)

        with nc.Block() as block:
            @block.tensor
            def _(pe):
                def down(ch, n, par):
                    pe.wait_ge(h_lo, n + 3)
                    for t in range(TPB):
                        mm = split_product(pe, FB[t // 2][:, (t % 2) * D:(t % 2 + 1) * D],
                                           [[hT[:, par, a, t * P:(t + 1) * P] for a in range(2)]],
                                           [[w2[:, a, ds(ch, 1), :].rearrange("p a t -> p (a t)")
                                             for a in range(2)]], False, False)
                    mm.then_inc(d_mm, 1)

                with pe.Fori(0, B) as b:
                    pe.wait_ge(e_b, b * 2 + 2)
                    for f in range(2):
                        pe.matmul(FB[f][:, :], zeros[:, :], xT[:, 0, 0, 0:T], start=True, stop=False,
                                  skip_group_check=True)

                    def item(ch, n, par, first):
                        pe.wait_ge(gp_r, n + 1)
                        for m, (banks, s) in enumerate(((GB, g_mm), (UB, u_mm))):
                            split_product(pe, banks[par][:, :],
                                          [[w13[m][:, a, c2, ds(ch * P, P)] for a in range(2)] for c2 in range(DC)],
                                          [[xT[:, a, c2, ds(b * T, T)] for a in range(2)] for c2 in range(DC)],
                                          True, True).then_inc(s, 1)
                        for a in range(2):
                            mm = pe.matmul(CB[par][:, :], sel[:, ds(ch * P, P)], share[:, a, ds(b * T, T)],
                                           start=a == 0, stop=a == 1, skip_group_check=True)
                        mm.then_inc(c_mm, 1)
                        if not first:
                            down(ch - 1, n - 1, 1 - par)

                    chunks(pe, b, item)
                    down(NCH1 - 1, b * NCH1 + NCH1 - 1, 0)

            @block.scalar
            def _(act):
                with act.Fori(0, B) as b:
                    def item(ch, n, par, first):
                        act.wait_ge(g_mm, n + 1)
                        act.activation(gt[:, par, :], GB[par][:, :], ACT.Tanh, scale=0.5).then_inc(gt_r, 1)
                        act.wait_ge(gp_r, n + 3)
                        act.wait_ge(d_mm, n + 1)
                        act.activation(hT[:, par, 0, :], gp[:, par, :], ACT.Copy).then_inc(h_hi, 1)

                    chunks(act, b, item)
                    act.wait_ge(d_mm, b * NCH1 + NCH1 + 2)
                    for i in range(2):
                        act.activation(et[:, i, :], FB[i][:, :], ACT.Tanh, scale=0.5).then_inc(e_t, 1)

            @block.gpsimd
            def _(pool):
                for s, credit in ((gp_r, 2), (h_lo, 2), (d_mm, 2), (e_b, 2)):
                    pool.sem_inc(s, credit)
                with pool.Fori(0, B) as b:
                    def item(ch, n, par, first):
                        pool.wait_ge(gp_r, n + 3)
                        pool.wait_ge(h_hi, n + 1)
                        pool.tensor_tensor(hT[:, par, 1, :], gp[:, par, :], hT[:, par, 0, :],
                                           ALU.subtract).then_inc(h_lo, 1)

                    chunks(pool, b, item)

            @block.vector
            def _(dve):
                with dve.Fori(0, B) as b:
                    def item(ch, n, par, first):
                        dve.wait_ge(gt_r, n + 1)
                        dve.scalar_tensor_tensor(out=gb[:, par, :], in0=gt[:, par, :], scalar=1.0, in1=GB[par][:, :],
                                                 op0=ALU.add, op1=ALU.mult).then_inc(gb_r, 1)
                        dve.wait_ge(u_mm, n + 1)
                        dve.wait_ge(gb_r, n + 1)
                        dve.scalar_tensor_tensor(out=gt[:, par, :], in0=gb[:, par, :], scalar=0.5, in1=UB[par][:, :],
                                                 op0=ALU.mult, op1=ALU.mult).then_inc(gu_r, 1)
                        dve.wait_ge(c_mm, n + 1)
                        dve.wait_ge(gu_r, n + 1)
                        dve.wait_ge(h_lo, n + 1)
                        dve.tensor_tensor(gp[:, par, :], gt[:, par, :], CB[par][:, :], ALU.mult).then_inc(gp_r, 1)

                    chunks(dve, b, item)
                    for i in range(2):
                        dve.wait_ge(e_t, b * 2 + i + 1)
                        dve.scalar_tensor_tensor(out=eb[:, i, :], in0=et[:, i, :], scalar=1.0, in1=FB[i][:, :],
                                                 op0=ALU.add, op1=ALU.mult).then_inc(e_b, 1)
                        dve.wait_ge(e_b, b * 2 + i + 3)
                        dve.tensor_scalar(gate[:, ds(b * TPB + 2 * i, 2), :].rearrange("p t d -> p (t d)"), eb[:, i, :],
                                          0.5, None, ALU.mult).then_inc(e_g, 1)


def route(nc, xT, wg, bias, ident, share, psum):
    with ExitStack() as c:
        sb = lambda n, s, d: c.enter_context(nc.sbuf_tensor("r_" + n, s, d))
        sem = lambda n: c.enter_context(nc.semaphore("r_" + n))
        score, biased, masked = sb("score", [P, NT, E], F32), sb("biased", [P, NT, E], F32), sb("masked", [P, NT, E], F32)
        gmax, grank, gsel = (sb(n, [P, NT, G], F32) for n in ("gmax", "grank", "gsel"))
        gcmp, geq = sb("gcmp", [P, NT, G, G], F32), sb("geq", [P, NT, G, G], F32)
        cmp_, eq = sb("cmp", [P, NT, E, E], F32), sb("eq", [P, NT, E, E], F32)
        lower_g, lower_e = sb("lower_g", [P, G, G], F32), sb("lower_e", [P, E, E], F32)
        rank, total = sb("rank", [P, NT, E], F32), sb("total", [P, NT], F32)
        parts = sb("parts", [P, 2, NT, E], F16)
        logits_done, tanh_done, low_made, chain = sem("logits"), sem("tanh"), sem("lower"), sem("chain")
        turned, hi_done, copied = sem("turned"), sem("hi"), sem("copied")
        LOG = psum[0]
        TQ = psum[1:5]

        with nc.Block() as block:
            @block.tensor
            def _(pe):
                for t in range(NT):
                    mm = split_product(pe, LOG[:, t * E:(t + 1) * E],
                                       [[xT[:, a, c2, t * P:(t + 1) * P] for a in range(2)] for c2 in range(DC)],
                                       [[wg[:, a, c2, :] for a in range(2)] for c2 in range(DC)], True, True)
                mm.then_inc(logits_done, 1)
                pe.wait_ge(copied, 1)
                for a in range(2):
                    for t in range(NT):
                        mm = pe.transpose(TQ[a * 2 + t // 8][:, :].bitcast(F16)[0:E, (t % 8) * P:(t % 8 + 1) * P],
                                          parts[:, a, t, :], ident[:, :])
                    mm.then_inc(turned, 1)

            @block.scalar
            def _(act):
                act.wait_ge(logits_done, 1)
                act.activation(score[:, :, :].rearrange("p t e -> p (t e)"), LOG[:, 0:NT * E], ACT.Tanh,
                               scale=0.5).then_inc(tanh_done, 1)

            @block.gpsimd
            def _(pool):
                for m, n in ((lower_g, G), (lower_e, E)):
                    pool.memset(m[:, :, :], 1.0).then_inc(low_made, 1)
                pool.wait_ge(low_made, 2)
                for m, n in ((lower_g, G), (lower_e, E)):
                    pool.affine_select(out=m[:, :, :], in_=m[:, :, :], compare_op=ALU.is_gt, fill=0.0, base=0,
                                       pattern=[[1, n], [-1, n]], channel_multiplier=0).then_inc(low_made, 1)
                pool.memset(share[:, 0, :], 1.0).then_inc(low_made, 1)
                pool.memset(share[:, 1, :], 0.0).then_inc(low_made, 1)

            @block.vector
            def _(dve):
                step = Count(chain)

                def do(ins):
                    step(ins)
                    step.wait(dve)

                dve.wait_ge(tanh_done, 1)
                dve.wait_ge(low_made, 6)
                do(dve.tensor_scalar(score[:, :, :], score[:, :, :], 1.0, 0.5, ALU.add, ALU.mult))
                bias_t = bias[:, :].rearrange("p (a e) -> p a e", a=1).broadcast_to([P, NT, E])
                do(dve.tensor_tensor(biased[:, :, :], score[:, :, :], bias_t, ALU.add))
                do(dve.tensor_reduce(gmax[:, :, :], biased[:, :, :].rearrange("p t (g e) -> p t g e", g=G),
                                     axis=AX.X, op=ALU.max))

                def ranks(value, n, lower, cmp_, eq, rank):
                    mine = value.rearrange("p t (e a) -> p t e a", a=1).broadcast_to([P, NT, n, n])
                    other = value.rearrange("p t (a e) -> p t a e", a=1).broadcast_to([P, NT, n, n])
                    low = lower[:, :, :].rearrange("p (a i) j -> p a i j", a=1).broadcast_to([P, NT, n, n])
                    do(dve.tensor_tensor(cmp_[:, :, :, :], other, mine, ALU.is_gt))
                    do(dve.tensor_tensor(eq[:, :, :, :], other, mine, ALU.is_equal))
                    do(dve.tensor_tensor(eq[:, :, :, :], eq[:, :, :, :], low, ALU.mult))
                    do(dve.tensor_tensor(cmp_[:, :, :, :], cmp_[:, :, :, :], eq[:, :, :, :], ALU.add))
                    do(dve.tensor_reduce(rank, cmp_[:, :, :, :], axis=AX.X, op=ALU.add))

                ranks(gmax[:, :, :], G, lower_g, gcmp, geq, grank[:, :, :])
                do(dve.tensor_scalar(gsel[:, :, :], grank[:, :, :], TOPK_G - 0.5, None, ALU.is_lt))
                sel_e = gsel[:, :, :].rearrange("p t (g a) -> p t g a", a=1).broadcast_to([P, NT, G, EG])
                as_groups = lambda ap: ap.rearrange("p t (g e) -> p t g e", g=G)
                do(dve.tensor_tensor(as_groups(masked[:, :, :]), as_groups(biased[:, :, :]), sel_e, ALU.mult))
                do(dve.tensor_scalar(gsel[:, :, :], gsel[:, :, :], 1.0, -MASKED, ALU.subtract, ALU.mult))
                do(dve.tensor_tensor(as_groups(masked[:, :, :]), as_groups(masked[:, :, :]), sel_e, ALU.add))
                ranks(masked[:, :, :], E, lower_e, cmp_, eq, rank[:, :, :])
                do(dve.tensor_scalar(rank[:, :, :], rank[:, :, :], TOPK - 0.5, None, ALU.is_lt))
                do(dve.tensor_tensor(score[:, :, :], score[:, :, :], rank[:, :, :], ALU.mult))
                do(dve.tensor_reduce(total[:, :], score[:, :, :], axis=AX.X, op=ALU.add))
                do(dve.reciprocal(total[:, :], total[:, :]))
                tot = total[:, :].rearrange("p (t a) -> p t a", a=1).broadcast_to([P, NT, E])
                do(dve.tensor_tensor(score[:, :, :], score[:, :, :], tot, ALU.mult))
                do(dve.tensor_copy(parts[:, 0, :, :], score[:, :, :]))
                dve.tensor_tensor(parts[:, 1, :, :], score[:, :, :], parts[:, 0, :, :], ALU.subtract).then_inc(copied, 1)
                for a in range(2):
                    dve.wait_ge(turned, a + 1)
                    for half in range(2):
                        dve.tensor_copy(share[0:E, a, half * 1024:(half + 1) * 1024],
                                        TQ[a * 2 + half][:, :].bitcast(F16)[0:E, :])


def attention1(nc, A, x, xT, ident, ident_b, causal, zeros, gate, psum):
    SC = HD1 ** -0.5
    NI = H1
    with ExitStack() as c:
        sb = lambda n, s, d: c.enter_context(nc.sbuf_tensor("a_" + n, s, d))
        sem = lambda n: c.enter_context(nc.semaphore("a_" + n))
        wq, wk, wv = (sb(n, [P, 2, DC, H1 * HD1], F16) for n in ("wq", "wk", "wv"))
        wo = sb("wo", [P, 2, H1, D], F16)
        bq, bk, bv = (sb(n, [P, H1], F32) for n in ("bq", "bk", "bv"))
        bo = sb("bo", [P, D], F32)
        with ExitStack() as c2:
            st = [c2.enter_context(nc.sbuf_tensor(f"a_stage{i}", [P, H1 * HD1], F32)) for i in range(2)]
            for m, (w, name) in enumerate(((wq, "wq1"), (wk, "wk1"), (wv, "wv1"))):
                split_weights(nc, [(A[name][cc * P:(cc + 1) * P, :], st[cc][:, :], w[:, 0, cc, :], w[:, 1, cc, :])
                                   for cc in range(2)], f"att{m}",
                              ((bq[:, :], A["bq1"]), (bk[:, :], A["bk1"]), (bv[:, :], A["bv1"]),
                               (bo[:, :], A["bo1"].broadcast_to([P, D]))) if m == 0 else ())
            split_weights(nc, [(A["wo1"][hh * 1024:(hh + 1) * 1024, :].rearrange("(h p) d -> p h d", p=P),
                                st[hh][:, :].rearrange("p (h d) -> p h d", d=D), wo[:, 0, hh * 8:hh * 8 + 8, :],
                                wo[:, 1, hh * 8:hh * 8 + 8, :]) for hh in range(2)], "att3")

        qk = sb("qk", [P, 2, 2, 2, T], F16)
        vv = sb("vv", [P, 2, 2, TPB * P], F16)
        ex = sb("ex", [P, PW], F32)
        pn = sb("pn", [P, 2, 2, PW], F16)
        pt = sb("pt", [P, 2, 2 * PW], F16)
        nmax, nbias = sb("nmax", [P, TPB], F32), sb("nbias", [P, TPB], F32)
        rsum, rinv = sb("rsum", [P, TPB], F32), sb("rinv", [P, TPB], F32)
        at = sb("at", [P, 2, 2, T], F16)
        fo = sb("fo", [P, 2, T], F32)
        SB, TB, JB, AO, FB = psum[0:2], psum[2], psum[3:5], psum[5], psum[6:8]
        TB16 = TB[:, :].bitcast(F16)
        p_mm = [sem(f"{n}_mm") for n in "qkv"]
        p_hi = [sem(f"{n}_hi") for n in "qkv"]
        p_lo = [sem(f"{n}_lo") for n in "qkv"]
        s_mm, bias_n, biased, exp_done = sem("s_mm"), sem("nmax_done"), sem("bias_ready"), sem("exp_done")
        recip, pn_hi, pn_lo = sem("recip"), sem("pn_hi"), sem("pn_lo")
        t_mm, t_ev, av_mm = sem("t_mm"), sem("t_evacuated"), sem("av_mm")
        ao_hi, ao_lo, wo_mm = sem("ao_hi"), sem("ao_lo"), sem("wo_mm")
        o_b, o_g, o_x, o_dma = sem("o_bias"), sem("o_gate"), sem("o_x"), sem("o_dma")

        def items(eng, b, last, item):
            def one(h, par, nxt, after):
                item(b, h, b * NI + h, par, nxt, after)

            one(0, 0, (b, 1), (b, 2))
            with eng.Fori(0, NI // 2 - 2) as i:
                for k in range(2):
                    h = i * 2 + k + 1
                    one(h, 1 - k, (b, h + 1), (b, h + 2))
            following = None if last else b + 1
            one(NI - 3, 1, (b, NI - 2), (b, NI - 1))
            one(NI - 2, 0, (b, NI - 1), None if last else (following, 0))
            one(NI - 1, 1, None if last else (following, 0), None if last else (following, 1))

        def turned(eng, n, par, j):
            _, col, w = TFILLS[j]
            eng.wait_ge(t_mm, n * 3 + j + 5)
            eng.wait_ge(av_mm, n + 1)
            if j < 2:
                eng.tensor_copy(pt[:, par, col:col + w], TB16[:, 0:w]).then_inc(t_ev, 1)
            else:
                eng.activation(pt[:, par, col:col + w], TB16[:, 0:w], ACT.Copy).then_inc(t_ev, 1)

        def per_batch(eng, body):
            with eng.Fori(0, B - 1) as b:
                body(b, False)
            body(B - 1, True)

        with nc.Block() as block:
            @block.gpsimd
            def _(pool):
                for s, credit in ((exp_done, 1), (pn_lo, 1), (t_mm, 4), (t_ev, 1), (av_mm, 2), (ao_lo, 1),
                                  (wo_mm, 2), (o_b, 2), (o_x, 2)):
                    pool.sem_inc(s, credit)
                with pool.Fori(0, B) as b:
                    for i in range(2):
                        pool.wait_ge(o_g, b * 2 + i + 1)
                        xv = x[:, ds(b * TPB + 2 * i, 2), :].rearrange("p t d -> p (t d)")
                        pool.tensor_tensor(xv, xv, fo[:, i, :], ALU.add).then_inc(o_x, 1)

            @block.sync
            def _(sp):
                with sp.Fori(0, B) as b:
                    for i in range(2):
                        sp.wait_ge(o_x, b * 2 + i + 3)
                        sp.dma_start(A["out"].rearrange("(t p) d -> p t d", p=P)[:, ds(b * TPB + 2 * i, 2), :],
                                     x[:, ds(b * TPB + 2 * i, 2), :]).then_inc(o_dma, 16)
                sp.wait_ge(o_dma, B * 2 * 16)

            @block.tensor
            def _(pe):
                def project(b, h, j, bank):
                    if j < 2:
                        w = (wq, wk)[j]
                        mm = split_product(pe, bank[:, :],
                                           [[w[:, a, c2, ds(h * P, P)] for a in range(2)] for c2 in range(DC)],
                                           [[xT[:, a, c2, ds(b * T, T)] for a in range(2)] for c2 in range(DC)],
                                           True, True)
                    else:
                        for t in range(TPB):
                            mm = split_product(pe, bank[:, t * P:(t + 1) * P],
                                               [[xT[:, a, c2, ds(b * T + t * P, P)] for a in range(2)] for c2 in range(DC)],
                                               [[wv[:, a, c2, ds(h * P, P)] for a in range(2)] for c2 in range(DC)],
                                               True, True)
                    mm.then_inc(p_mm[j], 1)

                def scores(n, j, par, first=False):
                    bank = SB[(par + j) % 2]
                    if not (first and j < 2):
                        pe.wait_ge(exp_done, n * 3 + j)
                    if j == 0:
                        pe.wait_ge(p_lo[0], n + 1)
                        pe.wait_ge(p_lo[1], n + 1)
                    at_col = 0
                    for i in ((3,), (2,), (1, 0))[j]:
                        w = (i + 1) * P
                        split_product(pe, bank[:, at_col:at_col + w],
                                      [[qk[:, par, 0, a, i * P:(i + 1) * P] for a in range(2)]],
                                      [[qk[:, par, 1, a, 0:w] for a in range(2)]], True, False)
                        mm = pe.matmul(bank[:, at_col + i * P:at_col + w], ident_b[:, :], causal[:, :], start=False,
                                       stop=True, skip_group_check=True)
                        at_col += w
                    mm.then_inc(s_mm, 1)

                def turn(n, j, par):
                    pe.wait_ge(t_ev, n * 3 + j + 1)
                    col = 0
                    for kb in TFILLS[j][0]:
                        for a in range(2):
                            for i in range(kb, TPB):
                                src = PCOL[i] + kb * P
                                mm = pe.transpose(TB16[:, col:col + P], pn[:, par, a, src:src + P], ident[:, :])
                                col += P
                    mm.then_inc(t_mm, 1)

                def weighted(n, par):
                    pe.wait_ge(ao_lo, n + 1)
                    pe.wait_ge(p_lo[2], n + 1)
                    for kb in range(TPB):
                        if kb < 3:
                            pe.wait_ge(t_ev, n * 3 + kb + 2)
                        c0, c1, w = KEYCOL[kb]
                        mm = split_product(pe, AO[:, kb * P:T], [[vv[:, par, a, kb * P:(kb + 1) * P] for a in range(2)]],
                                           [[pt[:, par, col:col + w] for col in (c0, c1)]], kb == 0, kb == 3)
                    mm.then_inc(av_mm, 1)

                def out_product(n, h, par):
                    pe.wait_ge(ao_lo, n + 2)
                    for t in range(TPB):
                        mm = split_product(pe, FB[t // 2][:, (t % 2) * D:(t % 2 + 1) * D],
                                           [[at[:, par, a, t * P:(t + 1) * P] for a in range(2)]],
                                           [[wo[:, a, ds(h, 1), :].rearrange("p a t -> p (a t)") for a in range(2)]],
                                           False, False)
                    mm.then_inc(wo_mm, 1)

                def item(b, h, n, par, nxt, after):
                    q = 1 - par
                    if nxt:
                        scores(n + 1, 0, q)
                        scores(n + 1, 1, q)
                    if after:
                        pe.wait_ge(p_lo[1], n + 2)
                        project(*after, 0, JB[q])
                    pe.wait_ge(pn_lo, n + 2)
                    pe.wait_ge(pn_hi, n * TPB + TPB)
                    turn(n, 0, par)
                    if after:
                        pe.wait_ge(p_lo[2], n + 1)
                        project(*after, 1, JB[par])
                    turn(n, 1, par)
                    if nxt:
                        scores(n + 1, 2, q)
                    if not (isinstance(h, int) and h == 0):
                        out_product(n - 1, h - 1, q)
                    turn(n, 2, par)
                    if nxt:
                        if after:
                            pe.wait_ge(p_lo[0], n + 3)
                        project(*nxt, 2, JB[q])
                    weighted(n, par)

                def batch(b, last):
                    pe.wait_ge(o_b, b * 2 + 2)
                    for f in range(2):
                        pe.matmul(FB[f][:, :], zeros[:, :], xT[:, 0, 0, 0:T], start=True, stop=False,
                                  skip_group_check=True)
                    items(pe, b, last, item)
                    out_product(b * NI + NI - 1, NI - 1, 1)

                for h in range(2):
                    for j in range(2):
                        if h:
                            pe.wait_ge(p_lo[j], 1)
                        project(0, h, j, JB[j])
                pe.wait_ge(p_lo[0], 2)
                project(0, 0, 2, JB[0])
                for j in range(3):
                    scores(0, j, 0, first=True)
                per_batch(pe, batch)

            def softmax_exp(act, n, par, js):
                for j in js:
                    col = 0
                    act.wait_ge(biased, n * 3 + j + 1)
                    if j == 0:
                        act.wait_ge(pn_lo, n + 1)
                    for i in ((3,), (2,), (1, 0))[j]:
                        w = (i + 1) * P
                        ins = act.activation(ex[:, PCOL[i]:PCOL[i] + w], SB[(par + j) % 2][:, col:col + w], ACT.Exp,
                                             bias=nbias[:, i:i + 1], scale=SC, accum_out=rsum[:, i:i + 1])
                        col += w
                    ins.then_inc(exp_done, 1)

            @block.scalar
            def _(act):
                def high(n, h, j, bank, par):
                    act.wait_ge(p_mm[j], n + 1)
                    if j < 2:
                        act.activation(qk[:, par, j, 0, :], bank[:, :], ACT.Identity,
                                       bias=(bq, bk)[j][:, ds(h, 1)]).then_inc(p_hi[j], 1)
                    else:
                        act.wait_ge(av_mm, n + 1)
                        act.activation(vv[:, par, 0, :], bank[:, :], ACT.Copy).then_inc(p_hi[j], 1)

                def probs_hi(n, par, blocks):
                    act.wait_ge(recip, n + 1)
                    act.wait_ge(exp_done, n * 3 + 4)
                    act.wait_ge(t_mm, n * 3 + 1)
                    for i in blocks:
                        act.activation(pn[:, par, 0, PCOL[i]:PCOL[i] + (i + 1) * P],
                                       ex[:, PCOL[i]:PCOL[i] + (i + 1) * P], ACT.Copy,
                                       scale=rinv[:, i:i + 1]).then_inc(pn_hi, 1)

                def item(b, h, n, par, nxt, after):
                    q = 1 - par
                    if nxt:
                        softmax_exp(act, n + 1, q, (0, 1))
                    if after:
                        high(n + 2, after[1], 0, JB[q], par)
                        high(n + 2, after[1], 1, JB[par], par)
                    if nxt:
                        softmax_exp(act, n + 1, q, (2,))
                    turned(act, n, par, 2)
                    if nxt:
                        probs_hi(n + 1, q, range(TPB))
                        high(n + 1, nxt[1], 2, JB[q], q)
                    act.wait_ge(av_mm, n + 3)
                    act.wait_ge(wo_mm, n + 1)
                    act.activation(at[:, par, 0, :], AO[:, :], ACT.Identity, bias=bv[:, ds(h, 1)]).then_inc(ao_hi, 1)

                for h in range(2):
                    for j in range(2):
                        high(h, h, j, JB[j], h)
                high(0, 0, 2, JB[0], 0)
                softmax_exp(act, 0, 0, (0, 1, 2))
                probs_hi(0, 0, range(TPB))
                per_batch(act, lambda b, last: items(act, b, last, item))

            @block.vector
            def _(dve):
                def low(n, h, j, bank, par):
                    dve.wait_ge(p_hi[j], n + 1)
                    if j < 2:
                        dve.scalar_tensor_tensor(out=qk[:, par, j, 1, :], in0=bank[:, :], scalar=(bq, bk)[j][:, ds(h, 1)],
                                                 in1=qk[:, par, j, 0, :], op0=ALU.add, op1=ALU.subtract).then_inc(p_lo[j], 1)
                    else:
                        dve.tensor_tensor(vv[:, par, 1, :], bank[:, :], vv[:, par, 0, :], ALU.subtract).then_inc(p_lo[j], 1)

                def maxima(n, par, j):
                    dve.wait_ge(s_mm, n * 3 + j + 1)
                    if j == 0:
                        dve.wait_ge(exp_done, n * 3 + 1)
                    blocks = ((3,), (2,), (1, 0))[j]
                    col = 0
                    for i in blocks:
                        w = (i + 1) * P
                        ins = dve.tensor_reduce(nmax[:, i:i + 1], SB[(par + j) % 2][:, col:col + w], axis=AX.X,
                                                op=ALU.max, negate=True)
                        col += w
                    ins.then_inc(bias_n, 1)
                    dve.wait_ge(bias_n, n * 3 + j + 1)
                    lo, hi = blocks[-1], blocks[0] + 1
                    dve.tensor_scalar(nbias[:, lo:hi], nmax[:, lo:hi], SC, None, ALU.mult).then_inc(biased, 1)

                def reciprocals(n):
                    dve.wait_ge(exp_done, n * 3 + 4)
                    dve.reciprocal(rinv[:, :], rsum[:, :]).then_inc(recip, 1)

                def probs_lo(n, par):
                    dve.wait_ge(recip, n + 1)
                    for i in range(TPB):
                        dve.wait_ge(pn_hi, n * TPB + i + 1)
                        s = slice(PCOL[i], PCOL[i] + (i + 1) * P)
                        ins = dve.scalar_tensor_tensor(out=pn[:, par, 1, s], in0=ex[:, s], scalar=rinv[:, i:i + 1],
                                                       in1=pn[:, par, 0, s], op0=ALU.mult, op1=ALU.subtract)
                    ins.then_inc(pn_lo, 1)

                def output_lo(n, h, par):
                    dve.wait_ge(ao_hi, n + 1)
                    dve.scalar_tensor_tensor(out=at[:, par, 1, :], in0=AO[:, :], scalar=bv[:, ds(h, 1)],
                                             in1=at[:, par, 0, :], op0=ALU.add, op1=ALU.subtract).then_inc(ao_lo, 1)

                def item(b, h, n, par, nxt, after):
                    q = 1 - par
                    if nxt:
                        maxima(n + 1, q, 0)
                        maxima(n + 1, q, 1)
                    if not (isinstance(h, int) and h == 0):
                        output_lo(n - 1, h - 1, q)
                    turned(dve, n, par, 0)
                    if after:
                        low(n + 2, after[1], 0, JB[q], par)
                    turned(dve, n, par, 1)
                    if after:
                        low(n + 2, after[1], 1, JB[par], par)
                    if nxt:
                        maxima(n + 1, q, 2)
                        reciprocals(n + 1)
                        probs_lo(n + 1, q)
                        low(n + 1, nxt[1], 2, JB[q], q)

                def batch(b, last):
                    items(dve, b, last, item)
                    output_lo(b * NI + NI - 1, NI - 1, 1)
                    bo2 = bo[:, :].rearrange("p (a d) -> p a d", a=1).broadcast_to([P, 2, D])
                    dve.wait_ge(wo_mm, b * NI + NI + 2)
                    for i in range(2):
                        f3 = fo[:, i, :].rearrange("p (a d) -> p a d", a=2)
                        dve.wait_ge(o_x, b * 2 + i + 1)
                        dve.tensor_tensor(f3, FB[i][:, :].rearrange("p (a d) -> p a d", a=2), bo2, ALU.add).then_inc(o_b, 1)
                        dve.wait_ge(o_b, b * 2 + i + 3)
                        dve.tensor_tensor(fo[:, i, :], fo[:, i, :],
                                          gate[:, ds(b * TPB + 2 * i, 2), :].rearrange("p t d -> p (t d)"),
                                          ALU.mult).then_inc(o_g, 1)

                for h in range(2):
                    for j in range(2):
                        low(h, h, j, JB[j], h)
                low(0, 0, 2, JB[0], 0)
                for j in range(3):
                    maxima(0, 0, j)
                reciprocals(0)
                probs_lo(0, 0)
                per_batch(dve, batch)


_OUT = (B, T, D)


def kernel(**inputs):
    import concourse.bacc as bacc
    from concourse.bass_utils import run_bass_kernel_spmd

    i = {k: np.asarray(v) for k, v in inputs.items()}

    def halves(w):
        return np.concatenate([w[0::2], w[1::2]], axis=0)

    def fp4(name):
        codes, scales = i[f"L0_ffn_{name}_W_packed"], i[f"L0_ffn_{name}_scales"]
        if name == "down":
            c = codes.T.reshape(8, P, D).transpose(1, 0, 2)
            s = np.repeat(scales.T.reshape(8, 8, D), 16, axis=1).transpose(1, 0, 2)
        else:
            order = np.arange(MLP).reshape(8, P, 2).transpose(0, 2, 1).reshape(-1)
            c = codes.T[:, order]
            s = np.repeat(scales.T[:, order], 16, axis=0)
        return c.reshape(P, MLP), s.reshape(P, MLP)

    host = {"x": i["L0_attn_x"].reshape(TOK, D)}
    host["wqkv0"] = halves(np.concatenate([i[f"L0_attn_W{n}"].T for n in "qkv"], axis=1))
    host["wo0"] = np.repeat(i["L0_attn_Wo"].T.reshape(4, 4, 1, HD0, D), 2, axis=2).reshape(4, P, D)
    host["bo0"] = i["L0_attn_bo"].reshape(1, D)
    for m, name in enumerate(("gate", "up", "down")):
        host[f"codes{m}"], host[f"scales{m}"] = fp4(name)
    for n in "qkv":
        host[f"w{n}1"] = i[f"L1_attn_w_{n}"]
        host[f"b{n}1"] = i[f"L1_attn_b_{n}"].reshape(H1, HD1).T
    host["wo1"] = i["L1_attn_w_o"]
    host["bo1"] = i["L1_attn_b_o"].reshape(1, D)
    host["gate_w"] = i["L1_ffn_gate_w"].T
    host["expert_bias"] = i["L1_ffn_expert_bias"].reshape(1, E)
    pad = HID1 - E * INTER - SHARED
    for m, (w, s) in enumerate((("w1", "sw1"), ("w3", "sw3"))):
        host[f"w{m}"] = np.concatenate([i[f"L1_ffn_{w}"].transpose(1, 0, 2).reshape(D, E * INTER), i[f"L1_ffn_{s}"],
                                        np.zeros((D, pad), np.float32)], axis=1)
    host["w2"] = np.concatenate([i["L1_ffn_w2"].reshape(E * INTER, D), i["L1_ffn_sw2"], np.zeros((pad, D), np.float32)])
    owner = np.minimum(np.arange(HID1) // INTER, E)
    host["sel"] = (owner[None, :] == np.arange(E + 1)[:, None]).astype(np.float16)

    nc = bacc.Bacc("TRN2", target_bir_lowering=False, num_devices=1)
    arrays, aps = {}, {}
    for name, a in host.items():
        arrays[f"in_{name}"] = np.ascontiguousarray(a)
        aps[name] = nc.dram_tensor(f"in_{name}", a.shape, mybir.dt.from_np(a.dtype), kind="ExternalInput").ap()
    aps["out"] = nc.dram_tensor("out_x", (TOK, D), F32, kind="ExternalOutput").ap()
    network(nc, aps)
    r = run_bass_kernel_spmd(nc, [arrays], core_ids=[0])
    return r.results[0]["out_x"].reshape(_OUT)
```

```python
from contextlib import ExitStack

import concourse.bass as bass
import numpy as np
from concourse import mybir

F32 = mybir.dt.float32
F16 = mybir.dt.float16
BF16 = mybir.dt.bfloat16
I32 = mybir.dt.int32
U16 = mybir.dt.uint16
U8 = mybir.dt.uint8
FP8 = mybir.dt.float8e3
ALU = mybir.AluOpType
ACT = mybir.ActivationFunctionType
AX = mybir.AxisListType
ds = bass.ds

P = 128
B, T, D = 4, 512, 256
TOK = B * T
NT = TOK // P
TPB = T // P
DC = D // P
H0, HD0 = 16, 16
H1, HD1 = 16, 128
MLP = 2048
NCH0 = MLP // P
E, TOPK, G, TOPK_G = 16, 4, 4, 2
EG = E // G
INTER, SHARED = 176, 352
HID1 = 3200
NCH1 = HID1 // P
EPS = 1e-5
MASKED = -1e30
GELU_C, GELU_K = 0.044715, 0.7978845608028654
HEADS = 4
VG = 640
SMAX = [(3, 0), (2, 512), (1, 896), (0, 1152)]
PW = 1280
TFILLS = [([0], 0, 1024), ([1], 1024, 768), ([2, 3], 1792, 768)]


def key_columns():
    where, at = {}, 0
    for blocks, _, _ in TFILLS:
        for kb in blocks:
            w = (TPB - kb) * P
            where[kb] = (at, at + w, w)
            at += 2 * w
    return where


KEYCOL = key_columns()
PCOL = dict(SMAX)


def starts_batch(head):
    return isinstance(head, int) and head == 0


class Count:

    def __init__(self, sem):
        self.sem, self.n = sem, 0

    def __call__(self, ins, by=1):
        ins.then_inc(self.sem, by)
        self.n += by
        return ins

    def wait(self, engine):
        engine.wait_ge(self.sem, self.n)


def split_product(pe, out, lhs, rhs, start, stop):
    mm = None
    n = len(lhs)
    for c in range(n):
        for i, (a, b) in enumerate(((0, 0), (0, 1), (1, 0))):
            mm = pe.matmul(out, lhs[c][a], rhs[c][b], start=start and c == 0 and i == 0,
                           stop=stop and c == n - 1 and i == 2, skip_group_check=True)
    return mm


def layer_norm(nc, ctx, tag, x, xT, ident, eps_tile, psum, interleaved, load=(), early=(), late=(), pool_low=(),
               zeroed=()):
    sb = lambda n, s, d: ctx.enter_context(nc.sbuf_tensor(f"{n}_{tag}", s, d))
    sem = lambda n: ctx.enter_context(nc.semaphore(f"{n}_{tag}"))
    stats = sb("stats", [P, NT, 6], F32)
    mv = sb("mv", [P, NT, 2], F32)
    std = sb("std", [P, NT], F32)
    rstd = sb("rstd", [P, NT], F32)
    xn = sb("xn", [P, 2, 2, D], F32)
    parts = sb("xn_parts", [P, 2, 2, 2, DC, P], F16)
    stats_done, std_done, rstd_done = sem("stats_done"), sem("std_done"), sem("rstd_done")
    xn_ready, hi_ready, lo_ready = sem("xn_ready"), sem("xn_hi_ready"), sem("xn_lo_ready")
    turned, copied = sem("xn_turned"), sem("xn_copied")
    xT4 = xT.rearrange("p a c t -> p (a c) t")
    NP = NT // 2

    def as_parts(k):
        v = xn[:, k, :, :].rearrange("p t d -> p (t d)")
        return (v.rearrange("p (t j c) -> p t c j", t=2, c=DC) if interleaved
                else v.rearrange("p (t c j) -> p t c j", t=2, c=DC))

    def pairs(eng, pair):
        pair(0, 0, True, False)
        with eng.Fori(0, NP // 2 - 1) as i:
            pair(i * 2 + 1, 1, False, False)
            pair(i * 2 + 2, 0, False, False)
        pair(NP - 1, 1, False, True)

    with nc.Block() as block:
        @block.sync
        def _(sp):
            for w in load:
                w.load(sp)

        @block.gpsimd
        def _(pool):
            for w in pool_low:
                w.low(pool)
            for buffer in zeroed:
                pool.memset(buffer, 0.0)

        @block.scalar
        def _(act):
            act.wait_ge(stats_done, 2 * NT)
            act.activation(std[:, :], mv[:, :, 1], ACT.Sqrt, bias=eps_tile[:, 0:1]).then_inc(std_done, 1)

            def pair(n, k, first, last):
                act.wait_ge(xn_ready, n * 2 + 2)
                act.wait_ge(turned, n + 1)
                act.activation(parts[:, k, 0], as_parts(k), ACT.Copy).then_inc(hi_ready, 1)
                if first:
                    for w in early:
                        w.high(act)

            pairs(act, pair)
            for w in late:
                w.high(act)

        @block.vector
        def _(dve):
            for t in range(NT):
                dve.bn_stats(stats[:, t, :], x[:, t, :]).then_inc(stats_done, 1)
            dve.wait_ge(stats_done, NT)
            for t in range(NT):
                dve.bn_aggr(mv[:, t, :], stats[:, t, :]).then_inc(stats_done, 1)
            dve.wait_ge(std_done, 1)
            dve.reciprocal(rstd[:, :], std[:, :]).then_inc(rstd_done, 1)
            dve.wait_ge(rstd_done, 1)
            dve.wait_ge(stats_done, 2 * NT)

            def normalise(n, k):
                for t in range(2):
                    tile = n * 2 + t
                    dve.tensor_scalar(xn[:, k, t, :], x[:, ds(tile, 1), :].rearrange("p a d -> p (a d)"),
                                      mv[:, ds(tile, 1), 0], rstd[:, ds(tile, 1)],
                                      ALU.subtract, ALU.mult).then_inc(xn_ready, 1)

            def copy_out(n, k):
                for t in range(2):
                    dve.wait_ge(turned, n + 3)
                    dve.tensor_copy(xT4[:, :, ds((n * 2 + t) * P, P)],
                                    psum[k * 2 + t][:, :].bitcast(F16)[:, 0:4 * P].rearrange("p (a t) -> p a t", a=4)
                                    ).then_inc(copied, 1)

            def pair(n, k, first, last):
                if not last:
                    if not first:
                        dve.wait_ge(lo_ready, n)
                    normalise(n + 1, 1 - k)
                dve.wait_ge(hi_ready, n + 1)
                dve.wait_ge(xn_ready, n * 2 + 2)
                dve.tensor_tensor(parts[:, k, 1], as_parts(k), parts[:, k, 0], ALU.subtract).then_inc(lo_ready, 1)
                if not first:
                    copy_out(n - 1, 1 - k)

            normalise(0, 0)
            pairs(dve, pair)
            copy_out(NP - 1, 1)
            for w in load:
                if w not in pool_low:
                    w.low(dve)

        @block.tensor
        def _(pe):
            pe.sem_inc(turned, 2)
            pe.sem_inc(copied, 4)

            def pair(n, k, first, last):
                pe.wait_ge(lo_ready, n + 1)
                pe.wait_ge(copied, n * 2 + 2)
                for t in range(2):
                    for a in range(2):
                        for c in range(DC):
                            q = (a * DC + c) * P
                            mm = pe.transpose(psum[k * 2 + t][:, :].bitcast(F16)[:, q:q + P], parts[:, k, a, t, c, :],
                                              ident[:, :])
                mm.then_inc(turned, 1)

            pairs(pe, pair)


def network(nc, A):
    ctx = ExitStack()
    with ctx:
        def sbp(name, shape, dt, c=ctx):
            return c.enter_context(nc.sbuf_tensor("s_" + name, shape, dt))

        x = sbp("x", [P, NT, D], F32)
        xT = sbp("xT", [P, 2, DC, TOK], F16)
        ident = sbp("ident", [P, P], F16)
        ident_b = sbp("ident_b", [P, P], BF16)
        causal = sbp("causal", [P, P], BF16)
        zeros = sbp("zeros", [P, P], F16)
        eps_tile = sbp("eps", [P, 1], F32)
        psum = [ctx.enter_context(nc.psum_tensor(f"bank{i}", [P, 512], F32)) for i in range(8)]

        ffn_ctx = ExitStack()
        ctx.enter_context(ffn_ctx)
        wffn = [sbp(f"wffn{m}", [P, 2, DC, MLP], F16, ffn_ctx) for m in range(2)]
        wdown = sbp("wdown", [P, 2, NCH0, D], F16, ffn_ctx)
        wqkv = sbp("wqkv", [P, 2, DC, 3 * D], F16, ffn_ctx)
        wo = sbp("wo", [P, 2, HEADS, D], F16, ffn_ctx)
        bo = sbp("bo", [P, D], F32, ffn_ctx)
        prepare_block0(nc, A, x, ident, ident_b, causal, zeros, eps_tile, wffn, wdown, wqkv, wo, bo)
        qs = sbp("qs", [P, H0, T], F16, ffn_ctx)
        ks = sbp("ks", [P, H0, T], F16, ffn_ctx)
        vm = sbp("vm", [P, TPB, HEADS, VG], F16, ffn_ctx)
        with ExitStack() as c:
            layer_norm(nc, c, "ln0", x, xT, ident, eps_tile, psum, True, zeroed=(qs[:, :, :], ks[:, :, :], vm[:, :, :, :]))
        block0(nc, A, x, xT, ident, ident_b, causal, zeros, wffn, wdown, wqkv, wo, bo, qs, ks, vm, psum)
        ffn_ctx.close()
        gate = sbp("gate", [P, NT, D], F32)
        wqk = sbp("wqk", [P, 2 * DC, 2, H1 * HD1], F16)
        experts(nc, A, x, xT, ident, zeros, eps_tile, gate, wqk, psum)
        attention1(nc, A, x, xT, ident, ident_b, causal, zeros, gate, wqk, psum)


class WeightSplit:

    def __init__(self, nc, ctx, name, src, stage, hi, lo, stage_of=None):
        self.src, self.stage, self.hi, self.lo, self.stage_of = src, stage, hi, lo, stage_of
        self.loaded, self.hi_done, self.lo_done = (
            ctx.enter_context(nc.semaphore(f"{name}_{n}")) for n in ("loaded", "hi", "lo"))

    def load(self, sp):
        if self.stage_of:
            sp.wait_ge(self.stage_of.lo_done, 1)
        sp.dma_start(self.stage, self.src).then_inc(self.loaded, 16)

    def high(self, act):
        act.wait_ge(self.loaded, 16)
        act.activation(self.hi, self.stage, ACT.Copy).then_inc(self.hi_done, 1)

    def low(self, eng):
        eng.wait_ge(self.loaded, 16)
        eng.wait_ge(self.hi_done, 1)
        eng.tensor_tensor(self.lo, self.stage, self.hi, ALU.subtract).then_inc(self.lo_done, 1)


def prepare_block0(nc, A, x, ident, ident_b, causal, zeros, eps_tile, wffn, wdown, wqkv, wo, bo):
    with ExitStack() as c:
        sb = lambda n, s, d: c.enter_context(nc.sbuf_tensor("p0_" + n, s, d))
        sem = lambda n: c.enter_context(nc.semaphore("p0_" + n))
        codes = [sb(f"codes{m}", [P, MLP], I32) for m in range(3)]
        scales = [sb(f"scales{m}", [P, MLP], F32) for m in range(3)]
        packed = [sb(f"packed{m}", [P, MLP // 2], U16) for m in range(3)]
        mag = sb("mag", [P, 2, MLP // 2], U16)
        sign = sb("sign", [P, 2, MLP // 2], U16)
        byte = sb("byte", [P, 2, MLP // 2], U16)
        high_w = sb("high_w", [P, 2, MLP], F32)
        qst = sb("qst", [P, DC, 3 * D], F32)
        ost = sb("ost", [P, HEADS, D], F32)
        loaded = [sem(f"fp4_loaded{m}") for m in range(3)]
        loaded_q, other, made = sem("qkvo_loaded"), sem("other_loaded"), sem("constants_made")
        pack_done, bits, w_ready, hi_ready = sem("packed"), sem("bits"), sem("w_ready"), sem("w_hi_ready")

        def target(m, nib):
            if m < 2:
                return wffn[m][:, 0, nib, :], wffn[m][:, 1, nib, :]
            v = wdown[:, :, :, :].rearrange("p a (j n) d -> p a n j d", n=2)
            return v[:, 0, nib, :, :], v[:, 1, nib, :, :]

        def weights(m, nib):
            return codes[m][:, :].bitcast(F32) if nib == 0 else high_w[:, m % 2, :]

        def low(eng, m, nib):
            eng.wait_ge(w_ready, 2 * m + nib + 1)
            eng.wait_ge(hi_ready, 2 * m + nib + 3)
            hi, lo = target(m, nib)
            eng.tensor_tensor(lo, shaped(m, weights(m, nib)), hi, ALU.subtract)

        def shaped(m, ap):
            return ap if m < 2 else ap.rearrange("p (j d) -> p j d", d=D)

        with nc.Block() as block:
            @block.sync
            def _(sp):
                for m in range(3):
                    sp.dma_start(codes[m][:, :], A[f"codes{m}"]).then_inc(loaded[m], 16)
                    sp.dma_start(scales[m][:, :], A[f"scales{m}"]).then_inc(loaded[m], 16)
                sp.dma_start(x[:, :, :], A["x"].rearrange("(t p) d -> p t d", p=P)).then_inc(other, 16)
                sp.dma_start(bo[:, :], A["bo0"].broadcast_to([P, D])).then_inc(other, 16)
                sp.wait_ge(other, 2 * 16)

            @block.scalar
            def _(act):
                act.dma_start(qst[:, :, :], A["wqkv0"].rearrange("(c p) n -> p c n", p=P)).then_inc(loaded_q, 16)
                act.dma_start(ost[:, :, :], A["wo0"].rearrange("g p n -> p g n")).then_inc(loaded_q, 16)
                def pack(m):
                    act.wait_ge(loaded[m], 32)
                    act.activation(packed[m][:, :].bitcast(U8), codes[m][:, :].bitcast(U8)[:, 0:4 * MLP:4],
                                   ACT.Copy).then_inc(pack_done, 1)

                pack(0)
                act.wait_ge(loaded_q, 32)
                act.activation(wqkv[:, 0, :, :], qst[:, :, :], ACT.Copy).then_inc(hi_ready, 1)
                act.activation(wo[:, 0, :, :], ost[:, :, :], ACT.Copy).then_inc(hi_ready, 1)
                for m in range(3):
                    if m < 2:
                        pack(m + 1)
                    for nib in range(2):
                        act.wait_ge(w_ready, 2 * m + nib + 1)
                        act.activation(target(m, nib)[0], shaped(m, weights(m, nib)), ACT.Copy).then_inc(hi_ready, 1)

            @block.gpsimd
            def _(pool):
                pool.memset(zeros[:, :], 0.0)
                pool.memset(eps_tile[:, :], EPS)
                for m in (ident, ident_b, causal):
                    pool.memset(m[:, :], 0.0).then_inc(made, 1)
                pool.wait_ge(made, 3)
                for m in (ident, ident_b):
                    pool.affine_select(out=m[:, :], in_=m[:, :], compare_op=ALU.not_equal, fill=1.0, base=0,
                                       pattern=[[-1, P]], channel_multiplier=1)
                pool.affine_select(out=causal[:, :], in_=causal[:, :], compare_op=ALU.is_ge, fill=MASKED, base=0,
                                   pattern=[[-1, P]], channel_multiplier=1)
                pool.wait_ge(loaded_q, 32)
                pool.wait_ge(hi_ready, 2)
                pool.tensor_tensor(wqkv[:, 1, :, :], qst[:, :, :], wqkv[:, 0, :, :], ALU.subtract)
                pool.tensor_tensor(wo[:, 1, :, :], ost[:, :, :], wo[:, 0, :, :], ALU.subtract)
                for m in range(3):
                    low(pool, m, 0)

            @block.vector
            def _(dve):
                done = Count(bits)
                for m in range(3):
                    cd = packed[m][:, :]
                    dve.wait_ge(loaded[m], 32)
                    dve.wait_ge(pack_done, m + 1)
                    if m:
                        dve.wait_ge(w_ready, 2 * m)
                    done(dve.tensor_scalar(mag[:, 0, :], cd, 0x0707, 3, ALU.bitwise_and, ALU.logical_shift_left))
                    done(dve.tensor_scalar(sign[:, 0, :], cd, 4, 0x8080, ALU.logical_shift_left, ALU.bitwise_and))
                    done(dve.tensor_scalar(mag[:, 1, :], cd, 1, 0x3838, ALU.logical_shift_right, ALU.bitwise_and))
                    done(dve.tensor_scalar(sign[:, 1, :], cd, 0x8080, None, ALU.bitwise_and))
                    done.wait(dve)
                    done(dve.tensor_tensor(byte[:, :, :], mag[:, :, :], sign[:, :, :], ALU.bitwise_or))
                    done.wait(dve)
                    if m:
                        low(dve, m - 1, 1)
                    for nib in range(2):
                        dve.scalar_tensor_tensor(out=weights(m, nib),
                                                 in0=byte[:, nib, :].bitcast(FP8), scalar=4.0,
                                                 in1=scales[m][:, :], op0=ALU.mult, op1=ALU.mult).then_inc(w_ready, 1)
                low(dve, 2, 1)

def block0(nc, A, x, xT, ident, ident_b, causal, zeros, wffn, wdown, wqkv, wo, bo, qs, ks, vm, psum):
    SC = HD0 ** -0.5
    with ExitStack() as c:
        sb = lambda n, s, d: c.enter_context(nc.sbuf_tensor("b0_" + n, s, d))
        sem = lambda n: c.enter_context(nc.semaphore("b0_" + n))
        raw = sb("raw", [P, 2, 4, T], F16)
        ex = sb("ex", [P, PW], F32)
        pn = sb("pn", [P, 2, 2, PW], F16)
        pt = sb("pt", [P, 2, 2 * PW], F16)
        nmax = sb("nmax", [P, TPB], F32)
        rsum, rinv = sb("rsum", [P, TPB], F32), sb("rinv", [P, TPB], F32)
        at = sb("at", [P, 2, HEADS, T], F16)
        g4 = sb("g4", [P, 4, T], F32)
        gsq, ga, gt, gb = (g4[:, i, :] for i in range(4))
        et, eb = g4[:, 0:2, :], g4[:, 2:4, :]
        gp = sb("gp", [P, T], F32)
        hT = sb("hT", [P, 2, 2, T], F16)
        scr = nc.dram_tensor("qk_parts", [2, 4, P, T], F16, kind="Internal").ap()

        SB, TB, GB, UB, AO, FB = psum[0:2], psum[2], psum[3], psum[4], psum[5], psum[6:8]
        TB16 = TB[:, :].bitcast(F16)

        raw_hi, raw_lo, raw_out = sem("raw_hi"), sem("raw_lo"), sem("raw_out")
        qk_mm, v_mm, v_hi, v_lo = sem("qk_mm"), sem("v_mm"), sem("v_hi"), sem("v_lo")
        stacked = [sem("stacked0"), sem("stacked1")]
        s_mm, nmax_done, exp_done = sem("s_mm"), sem("nmax_done"), sem("exp_done")
        recip, pn_hi, pn_lo = sem("recip"), sem("pn_hi"), sem("pn_lo")
        t_mm, t_ev, av_mm = sem("t_mm"), sem("t_evacuated"), sem("av_mm")
        ao_hi, ao_lo = sem("ao_hi"), sem("ao_lo")
        g_mm, u_mm, sq_r, ga_r, gt_r, gb_r, gp_r, h_hi, h_lo, d_mm = (
            sem(n) for n in ("g_mm", "u_mm", "sq", "ga", "gt", "gb", "gp", "h_hi", "h_lo", "d_mm"))
        wo_mm, e_t, e_b, e_s, e_q, e_x = (sem(n) for n in ("wo_mm", "e_tanh", "e_b", "e_s", "e_q", "e_x"))

        def per_batch(eng, body):
            with eng.Fori(0, B - 1) as b:
                body(b, False)
            body(B - 1, True)

        def per_group(last, eng, item):
            for k in range(HEADS):
                item(0, k, "first" if k == 0 else "inner")
            with eng.Fori(1, 3) as g:
                for k in range(HEADS):
                    item(g, k, "inner")
            for k in range(HEADS):
                item(3, k, "inner" if k < 3 else "end" if last else "last")

        def item_no(b, g, k):
            return b * 16 + g * 4 + k

        def turned(eng, n, par, j):
            _, col, w = TFILLS[j]
            eng.wait_ge(t_mm, n * 3 + j + 5)
            eng.wait_ge(av_mm, n + 1)
            if j < 2:
                eng.tensor_copy(pt[:, par, col:col + w], TB16[:, 0:w]).then_inc(t_ev, 1)
            else:
                eng.activation(pt[:, par, col:col + w], TB16[:, 0:w], ACT.Copy).then_inc(t_ev, 1)

        with nc.Block() as block:
            @block.sync
            def _(sp):
                def spill(n):
                    for ch in range(4):
                        sp.wait_ge(raw_hi, n * 4 + ch + 1)
                        sp.wait_ge(raw_lo, n * 4 + ch + 1)
                        for a in range(2):
                            sp.dma_start(scr[a, ch], raw[:, a, ch, :]).then_inc(raw_out, 16)
                    sp.wait_ge(raw_out, n * 128 + 128)

                def stack(half):
                    h = slice(half * 8, half * 8 + 8)
                    for row, a in enumerate((0, 1, 0)):
                        sp.dma_start(qs[16 * row:16 * row + 16, h, :],
                                     scr[a, half].rearrange("(h d) t -> d h t", d=HD0)).then_inc(stacked[half], 16)
                    for row, a in enumerate((0, 0, 1)):
                        sp.dma_start(ks[16 * row:16 * row + 16, h, :],
                                     scr[a, 2 + half].rearrange("(h d) t -> d h t", d=HD0)).then_inc(stacked[half], 16)

                spill(0)
                stack(0)
                stack(1)
                with sp.Fori(0, B - 1) as b:
                    for half in range(2):
                        sp.wait_ge(stacked[half], b * 96 + 96)
                    spill(b + 1)
                    sp.wait_ge(s_mm, b * 48 + 24)
                    stack(0)
                    sp.wait_ge(s_mm, b * 48 + 48)
                    stack(1)
                sp.wait_ge(stacked[0], 96 * B)
                sp.wait_ge(stacked[1], 96 * B)

            @block.gpsimd
            def _(pool):
                for s, credit in ((exp_done, 1), (pn_lo, TPB), (t_mm, 4), (t_ev, 1), (av_mm, 2), (ao_lo, 1), (gb_r, 1),
                                  (gp_r, 1), (h_lo, 1), (d_mm, 2), (wo_mm, 2), (e_s, 2), (e_b, 2), (e_x, 2)):
                    pool.sem_inc(s, credit)

                def item(b, g, k):
                    n = item_no(b, g, k)
                    pool.wait_ge(gp_r, n + 2)
                    pool.wait_ge(h_hi, n + 1)
                    pool.tensor_tensor(hT[:, k % 2, 1, :], gp[:, :], hT[:, k % 2, 0, :], ALU.subtract).then_inc(h_lo, 1)

                with pool.Fori(0, B) as b:
                    with pool.Fori(0, H0 // HEADS) as g:
                        for k in range(HEADS):
                            item(b, g, k)
                    for i in range(2):
                        pool.wait_ge(e_q, b * 2 + i + 1)
                        xv = x[:, ds(b * TPB + 2 * i, 2), :].rearrange("p t d -> p (t d)")
                        pool.tensor_tensor(xv, xv, eb[:, i, :], ALU.add).then_inc(e_x, 1)

            @block.tensor
            def _(pe):
                def project_qk(b, n, after_v=None):
                    for ch in range(4):
                        if ch == 1 and after_v is not None:
                            pe.wait_ge(v_lo, after_v)
                        bank = (GB, UB)[ch % 2]
                        if ch >= 2:
                            pe.wait_ge(raw_lo, n * 4 + ch - 1)
                        col = (ch // 2) * D + (ch % 2) * P
                        split_product(pe, bank[:, :],
                                      [[wqkv[:, a, c2, col:col + P] for a in range(2)] for c2 in range(DC)],
                                      [[xT[:, a, c2, ds(b * T, T)] for a in range(2)] for c2 in range(DC)],
                                      True, True).then_inc(qk_mm, 1)

                def project_v(b):
                    for t in range(TPB):
                        bank = (GB, UB)[t % 2]
                        if t >= 2:
                            pe.wait_ge(v_lo, b * 4 + t - 1)
                        split_product(pe, bank[:, 0:D],
                                      [[xT[:, a, c2, ds(b * T + t * P, P)] for a in range(2)] for c2 in range(DC)],
                                      [[wqkv[:, a, c2, 2 * D:3 * D] for a in range(2)] for c2 in range(DC)],
                                      True, True).then_inc(v_mm, 1)

                def scores(n, j, h, par, first=False):
                    bank = SB[(par + j) % 2]
                    if not (first and j < 2):
                        pe.wait_ge(exp_done, n * 3 + j)
                    at_col = 0
                    for i in ((3,), (2,), (1, 0))[j]:
                        w = (i + 1) * P
                        o = bank[:, at_col:at_col + w]
                        pe.matmul(o, qs[:, ds(h, 1), i * P:(i + 1) * P].rearrange("p a t -> p (a t)"),
                                  ks[:, ds(h, 1), 0:w].rearrange("p a t -> p (a t)"), start=True, stop=False,
                                  skip_group_check=True)
                        mm = pe.matmul(bank[:, at_col + i * P:at_col + w], ident_b[:, :], causal[:, :], start=False,
                                       stop=True, skip_group_check=True)
                        at_col += w
                    mm.then_inc(s_mm, 1)

                def turn(n, j, par):
                    pe.wait_ge(t_ev, n * 3 + j + 1)
                    blocks, _, _ = TFILLS[j]
                    col = 0
                    for kb in blocks:
                        for a in range(2):
                            for i in range(kb, TPB):
                                src = PCOL[i] + kb * P
                                mm = pe.transpose(TB16[:, col:col + P], pn[:, par, a, src:src + P], ident[:, :])
                                col += P
                    mm.then_inc(t_mm, 1)

                def weighted(n, b, g, k):
                    if k == 0:
                        pe.wait_ge(ao_lo, b * 4 + g + 1)
                    for kb in range(TPB):
                        if kb < 3:
                            pe.wait_ge(t_ev, n * 3 + min(kb, 2) + 2)
                        for a in range(2):
                            c0, c1, w = KEYCOL[kb]
                            col = (c0, c1)[a]
                            mm = pe.matmul(AO[:, kb * P:T],
                                           vm[:, kb, ds(g, 1), k * P:(k + 1) * P].rearrange("p a t -> p (a t)"),
                                           pt[:, k % 2, col:col + w],
                                           start=(k == 0 and kb == 0 and a == 0), stop=(k == 3 and kb == 3 and a == 1),
                                           skip_group_check=True)
                    mm.then_inc(av_mm, 1)

                def down(n, ch, par):
                    pe.wait_ge(h_lo, n + 2)
                    for t in range(TPB):
                        mm = split_product(pe, FB[t // 2][:, (t % 2) * D:(t % 2 + 1) * D],
                                           [[hT[:, par, a, t * P:(t + 1) * P] for a in range(2)]],
                                           [[wdown[:, a, ds(ch, 1), :].rearrange("p a t -> p (a t)")
                                             for a in range(2)]], False, False)
                    mm.then_inc(d_mm, 1)

                project_qk(0, 0)
                pe.wait_ge(raw_lo, 4)
                pe.wait_ge(stacked[0], 96)
                for j in range(3):
                    scores(0, j, 0, 0, first=True)

                def batch(b, last):
                    pe.wait_ge(e_s, b * 2 + 2)
                    pe.wait_ge(e_b, b * 2 + 2)
                    project_v(b)
                    for f in range(2):
                        pe.matmul(FB[f][:, :], zeros[:, :], xT[:, 0, 0, 0:T], start=True, stop=False,
                                  skip_group_check=True)
                    if not last:
                        pe.wait_ge(raw_out, b * 128 + 128)
                        pe.wait_ge(v_lo, b * 4 + 3)
                        project_qk(b + 1, b + 1, after_v=b * 4 + 4)

                    def item(g, k, kind):
                        n = item_no(b, g, k)
                        par = (k + 1) % 2

                        def hidden(m):
                            bank, s = ((GB, g_mm), (UB, u_mm))[m]
                            if kind == "first":
                                if last:
                                    pe.wait_ge(v_lo, b * 4 + 4)
                                else:
                                    pe.wait_ge(raw_lo, b * 4 + 8)
                            pe.wait_ge((gb_r, gp_r)[m], n + 1)
                            split_product(pe, bank[:, :],
                                          [[wffn[m][:, a, c2, ds(g * 512 + k * P, P)] for a in range(2)] for c2 in range(DC)],
                                          [[xT[:, a, c2, ds(b * T, T)] for a in range(2)] for c2 in range(DC)],
                                          True, True).then_inc(s, 1)

                        have = kind != "end"
                        h = g * 4 + k + 1 if kind != "last" else 0
                        if kind == "last":
                            pe.wait_ge(stacked[0], b * 96 + 192)
                        if k == 3 and kind == "inner":
                            pe.wait_ge(stacked[1], b * 96 + 96)
                        if have:
                            scores(n + 1, 0, h, par)
                            scores(n + 1, 1, h, par)
                        pe.wait_ge(pn_lo, n * TPB + 2 * TPB)
                        turn(n, 0, k % 2)
                        hidden(0)
                        if have:
                            scores(n + 1, 2, h, par)
                        turn(n, 1, k % 2)
                        hidden(1)
                        if kind != "first":
                            down(n - 1, g * 4 + k - 1, 1 - k % 2)
                        turn(n, 2, k % 2)
                        weighted(n, b, g, k)

                    per_group(last, pe, item)
                    down(b * 16 + 15, 15, 1)
                    pe.wait_ge(gb_r, b * 16 + 17)
                    pe.wait_ge(gp_r, b * 16 + 17)
                    pe.wait_ge(ao_lo, b * 4 + 5)
                    for t in range(TPB):
                        mm = split_product(pe, (GB, UB)[t // 2][:, (t % 2) * D:(t % 2 + 1) * D],
                                           [[at[:, a, gg, t * P:(t + 1) * P] for a in range(2)] for gg in range(4)],
                                           [[wo[:, a, gg, :] for a in range(2)] for gg in range(4)], True, True)
                        if t % 2:
                            mm.then_inc(wo_mm, 1)

                per_batch(pe, batch)

            @block.scalar
            def _(act):
                def raw_parts(n):
                    for ch in range(4):
                        act.wait_ge(qk_mm, n * 4 + ch + 1)
                        act.activation(raw[:, 0, ch, :], (GB, UB)[ch % 2][:, :], ACT.Copy,
                                       scale=SC if ch < 2 else 1.0).then_inc(raw_hi, 1)

                def softmax_exp(n, par, js):
                    for j in js:
                        blocks = ((3,), (2,), (1, 0))[j]
                        col = 0
                        act.wait_ge(nmax_done, n * 3 + j + 1)
                        act.wait_ge(pn_lo, n * TPB + TPB - blocks[-1])
                        for i in blocks:
                            w = (i + 1) * P
                            ins = act.activation(ex[:, PCOL[i]:PCOL[i] + w], SB[(par + j) % 2][:, col:col + w], ACT.Exp,
                                                 bias=nmax[:, i:i + 1], accum_out=rsum[:, i:i + 1])
                            col += w
                        ins.then_inc(exp_done, 1)

                def probs_hi(n, par, blocks):
                    act.wait_ge(recip, n + 1)
                    act.wait_ge(exp_done, n * 3 + 4)
                    act.wait_ge(t_mm, n * 3 + 1)
                    for i in reversed(blocks):
                        act.activation(pn[:, par, 0, PCOL[i]:PCOL[i] + (i + 1) * P],
                                       ex[:, PCOL[i]:PCOL[i] + (i + 1) * P], ACT.Copy,
                                       scale=rinv[:, i:i + 1]).then_inc(pn_hi, 1)

                raw_parts(0)
                softmax_exp(0, 0, (0, 1, 2))
                probs_hi(0, 0, range(TPB))

                def batch(b, last):
                    for t in range(TPB):
                        act.wait_ge(v_mm, b * 4 + t + 1)
                        if t == 0:
                            act.wait_ge(av_mm, b * 16 + 2)
                        v4 = vm[:, t, :, :].rearrange("p g (k e) -> p g k e", e=160)
                        act.activation(v4[:, :, :, 0:16], (GB, UB)[t % 2][:, 0:D].rearrange("p (g k d) -> p g k d", g=4, k=4),
                                       ACT.Copy).then_inc(v_hi, 1)

                    if not last:
                        raw_parts(b + 1)

                    def group_hi(g, n):
                        act.wait_ge(av_mm, n + 3)
                        act.wait_ge(wo_mm, b * 2 + 2)
                        act.activation(at[:, 0, ds(g, 1), :].rearrange("p a t -> p (a t)"), AO[:, :],
                                       ACT.Copy).then_inc(ao_hi, 1)

                    def item(g, k, kind):
                        n = item_no(b, g, k)
                        have = kind != "end"
                        if have:
                            softmax_exp(n + 1, (k + 1) % 2, (0,))
                        if k == 0 and kind != "first":
                            group_hi(g - 1, n - 1)
                        act.wait_ge(g_mm, n + 1)
                        if kind == "first":
                            act.wait_ge(e_x, b * 2 + 2)
                        act.activation(gsq, GB[:, :], ACT.Square).then_inc(sq_r, 1)
                        if have:
                            softmax_exp(n + 1, (k + 1) % 2, (1,))
                            softmax_exp(n + 1, (k + 1) % 2, (2,))
                        act.wait_ge(ga_r, n + 1)
                        act.activation(gt, ga, ACT.Tanh, scale=GELU_K * GELU_C).then_inc(gt_r, 1)
                        if have:
                            probs_hi(n + 1, (k + 1) % 2, (2, 3))
                        turned(act, n, k % 2, 2)
                        if have:
                            probs_hi(n + 1, (k + 1) % 2, (0, 1))
                        act.wait_ge(gp_r, n + 2)
                        act.wait_ge(d_mm, n + 1)
                        act.activation(hT[:, k % 2, 0, :], gp[:, :], ACT.Copy).then_inc(h_hi, 1)

                    per_group(last, act, item)
                    group_hi(3, b * 16 + 15)
                    for i in range(2):
                        act.wait_ge(d_mm, b * 16 + 18)
                        act.activation(et[:, i, :], FB[i][:, :], ACT.Tanh, scale=0.5).then_inc(e_t, 1)

                per_batch(act, batch)

            @block.vector
            def _(dve):
                def raw_parts(n):
                    for ch in range(4):
                        dve.wait_ge(raw_hi, n * 4 + ch + 1)
                        dve.scalar_tensor_tensor(out=raw[:, 1, ch, :], in0=(GB, UB)[ch % 2][:, :],
                                                 scalar=SC if ch < 2 else 1.0, in1=raw[:, 0, ch, :],
                                                 op0=ALU.mult, op1=ALU.subtract).then_inc(raw_lo, 1)

                def maxima(n, par, j):
                    dve.wait_ge(s_mm, n * 3 + j + 1)
                    if j == 0:
                        dve.wait_ge(exp_done, n * 3 + 1)
                    blocks = ((3,), (2,), (1, 0))[j]
                    col = 0
                    for i in blocks:
                        w = (i + 1) * P
                        ins = dve.tensor_reduce(nmax[:, i:i + 1], SB[(par + j) % 2][:, col:col + w], axis=AX.X,
                                                op=ALU.max, negate=True)
                        col += w
                    ins.then_inc(nmax_done, 1)

                def reciprocals(n):
                    dve.wait_ge(exp_done, n * 3 + 4)
                    dve.reciprocal(rinv[:, :], rsum[:, :]).then_inc(recip, 1)

                def probs_lo(n, par, blocks):
                    dve.wait_ge(recip, n + 1)
                    for i in reversed(blocks):
                        dve.wait_ge(pn_hi, n * TPB + TPB - i)
                        s = slice(PCOL[i], PCOL[i] + (i + 1) * P)
                        dve.scalar_tensor_tensor(out=pn[:, par, 1, s], in0=ex[:, s], scalar=rinv[:, i:i + 1],
                                                 in1=pn[:, par, 0, s], op0=ALU.mult, op1=ALU.subtract).then_inc(pn_lo, 1)

                raw_parts(0)
                for j in range(3):
                    maxima(0, 0, j)
                reciprocals(0)
                probs_lo(0, 0, range(TPB))

                def batch(b, last):
                    for t in range(TPB):
                        dve.wait_ge(v_hi, b * 4 + t + 1)
                        v4 = vm[:, t, :, :].rearrange("p g (k e) -> p g k e", e=160)
                        dve.tensor_tensor(v4[:, :, :, 16:32], (GB, UB)[t % 2][:, 0:D].rearrange("p (g k d) -> p g k d", g=4, k=4),
                                          v4[:, :, :, 0:16], ALU.subtract).then_inc(v_lo, 1)

                    if not last:
                        raw_parts(b + 1)

                    def group_lo(g):
                        dve.wait_ge(ao_hi, b * 4 + g + 1)
                        dve.tensor_tensor(at[:, 1, ds(g, 1), :].rearrange("p a t -> p (a t)"), AO[:, :],
                                          at[:, 0, ds(g, 1), :].rearrange("p a t -> p (a t)"),
                                          ALU.subtract).then_inc(ao_lo, 1)

                    def item(g, k, kind):
                        n = item_no(b, g, k)
                        have = kind != "end"
                        par = (k + 1) % 2
                        if have:
                            maxima(n + 1, par, 0)
                            maxima(n + 1, par, 1)
                        turned(dve, n, k % 2, 0)
                        if k == 0 and kind != "first":
                            group_lo(g - 1)
                        if have:
                            maxima(n + 1, par, 2)
                        dve.wait_ge(sq_r, n + 1)
                        dve.scalar_tensor_tensor(out=ga, in0=gsq, scalar=1.0 / GELU_C, in1=GB[:, :],
                                                 op0=ALU.add, op1=ALU.mult).then_inc(ga_r, 1)
                        if have:
                            reciprocals(n + 1)
                        turned(dve, n, k % 2, 1)
                        dve.wait_ge(gt_r, n + 1)
                        dve.scalar_tensor_tensor(out=gb, in0=gt, scalar=1.0, in1=GB[:, :],
                                                 op0=ALU.add, op1=ALU.mult).then_inc(gb_r, 1)
                        if have:
                            probs_lo(n + 1, par, (3,))
                        dve.wait_ge(u_mm, n + 1)
                        dve.wait_ge(gb_r, n + 2)
                        dve.wait_ge(h_lo, n + 1)
                        dve.scalar_tensor_tensor(out=gp[:, :], in0=gb, scalar=0.5, in1=UB[:, :],
                                                 op0=ALU.mult, op1=ALU.mult).then_inc(gp_r, 1)
                        if have:
                            probs_lo(n + 1, par, (2,))
                            probs_lo(n + 1, par, (0, 1))

                    per_group(last, dve, item)
                    group_lo(3)
                    bo2 = bo[:, :].rearrange("p (a d) -> p a d", a=1).broadcast_to([P, 2, D])
                    for i in range(2):
                        dve.wait_ge(e_t, b * 2 + i + 1)
                        dve.wait_ge(e_x, b * 2 + i + 1)
                        dve.scalar_tensor_tensor(out=eb[:, i, :], in0=et[:, i, :], scalar=1.0, in1=FB[i][:, :],
                                                 op0=ALU.add, op1=ALU.mult).then_inc(e_b, 1)
                        dve.wait_ge(wo_mm, b * 2 + i + 3)
                        dve.wait_ge(e_b, b * 2 + i + 3)
                        dve.tensor_tensor(et[:, i, :].rearrange("p (a d) -> p a d", a=2),
                                          (GB, UB)[i][:, :].rearrange("p (a d) -> p a d", a=2), bo2,
                                          ALU.add).then_inc(e_s, 1)
                        dve.wait_ge(e_s, b * 2 + i + 3)
                        dve.scalar_tensor_tensor(out=eb[:, i, :], in0=et[:, i, :], scalar=0.5, in1=eb[:, i, :],
                                                 op0=ALU.mult, op1=ALU.mult).then_inc(e_q, 1)

                per_batch(dve, batch)


def experts(nc, A, x, xT, ident, zeros, eps_tile, gate, wqk, psum):
    with ExitStack() as c:
        sb = lambda n, s, d: c.enter_context(nc.sbuf_tensor("m_" + n, s, d))
        sem = lambda n: c.enter_context(nc.semaphore("m_" + n))
        w13 = [sb(f"w{m}", [P, 2, DC, HID1], F16) for m in range(2)]
        w2 = sb("w2", [P, 2, NCH1, D], F16)
        wg = sb("wg", [P, 2, DC, E], F16)
        sel = sb("sel", [E + 1, HID1], F16)
        share = sb("share", [E + 1, 2, TOK], F16)
        bias = sb("bias", [P, E], F32)
        with ExitStack() as c2:
            c3 = c2.enter_context(ExitStack())
            stg = c2.enter_context(nc.sbuf_tensor("m_stage_gate", [P, DC, E], F32))
            W2C = NCH1 // 5
            own2 = c2.enter_context(nc.sbuf_tensor("m_stage_w2", [P, W2C, D], F32))
            own = c3.enter_context(nc.sbuf_tensor("m_stage_w13", [P, HID1], F32))
            wqk32 = wqk.rearrange("p m a n -> p (m a n)").bitcast(F32)
            stages = [own[:, :], gate.rearrange("p t d -> p (t d)")[:, 0:HID1], wqk32[:, 0:HID1],
                      wqk32[:, HID1:2 * HID1]]
            stages2 = [own2[:, :, :],
                       wqk32[:, 2 * HID1:2 * HID1 + W2C * D].rearrange("p (c d) -> p c d", d=D)]
            first = [WeightSplit(nc, c2, f"w{m}_{cc}", A[f"w{m}"][cc * P:(cc + 1) * P, :], stages[m * 2 + cc],
                                 w13[m][:, 0, cc, :], w13[m][:, 1, cc, :]) for m in range(2) for cc in range(DC)]
            first.insert(0, WeightSplit(nc, c2, "wg", A["gate_w"].rearrange("(c p) e -> p c e", p=P), stg[:, :, :],
                                        wg[:, 0, :, :], wg[:, 1, :, :]))
            second = []
            for q in range(5):
                r = slice(q * W2C, (q + 1) * W2C)
                second.append(WeightSplit(
                    nc, c2, f"w2_{q}", A["w2"][q * W2C * P:(q + 1) * W2C * P, :].rearrange("(c p) d -> p c d", p=P),
                    stages2[q % 2], w2[:, 0, r, :], w2[:, 1, r, :], second[q - 2] if q >= 2 else None))
            layer_norm(nc, c3, "ln1", x, xT, ident, eps_tile, psum, False, load=first, early=first[0:2],
                       late=first[2:], pool_low=first[1:3])
            c3.close()
            route(nc, A, xT, wg, bias, sel, ident, share, psum, second)

        gt, gb, gp = (sb(n, [P, 2, T], F32) for n in ("gt", "gb", "gp"))
        hT = sb("hT", [P, 2, 2, T], F16)
        et, eb = gt, gb
        stage = sb("stage_qk", [P, H1 * HD1], F32)
        qk_loaded, qk_hi, qk_lo = sem("qk_loaded"), sem("qk_hi"), sem("qk_lo")
        GB, UB, CB, FB = psum[0:2], psum[2:4], psum[4:6], psum[6:8]
        g_mm, u_mm, c_mm, gt_r, gb_r, gu_r, gp_r, h_hi, h_lo, d_mm, e_t, e_b, e_g = (
            sem(n) for n in ("g_mm", "u_mm", "c_mm", "tanh", "gb", "gu", "gp", "h_hi", "h_lo", "d_mm", "e_tanh",
                             "e_b", "e_gate"))

        def chunks(eng, b, item, aside=lambda q: None):
            item(0, b * NCH1, 0, True)
            with eng.Fori(0, 4) as q:
                with eng.Fori(0, NCH1 // 8) as i:
                    for k in range(2):
                        ch = q * (NCH1 // 4) + i * 2 + k + 1
                        item(ch, b * NCH1 + ch, (k + 1) % 2, False)
                aside(q)

        with nc.Block() as block:
            @block.sync
            def _(sp):
                with sp.Fori(0, B) as b:
                    sp.wait_ge(qk_lo, b * 4 + 1)
                    sp.dma_start(stage[:, :], A["wqk1"][ds(b * P, P), :]).then_inc(qk_loaded, 16)
                sp.wait_ge(qk_loaded, 16 * B)

            @block.tensor
            def _(pe):
                def down(ch, n, par):
                    pe.wait_ge(h_lo, n + 3)
                    for t in range(TPB):
                        mm = split_product(pe, FB[t // 2][:, (t % 2) * D:(t % 2 + 1) * D],
                                           [[hT[:, par, a, t * P:(t + 1) * P] for a in range(2)]],
                                           [[w2[:, a, ds(ch, 1), :].rearrange("p a t -> p (a t)")
                                             for a in range(2)]], False, False)
                    mm.then_inc(d_mm, 1)

                with pe.Fori(0, B) as b:
                    pe.wait_ge(e_b, b * 2 + 2)
                    for f in range(2):
                        pe.matmul(FB[f][:, :], zeros[:, :], xT[:, 0, 0, 0:T], start=True, stop=False,
                                  skip_group_check=True)

                    def item(ch, n, par, first):
                        pe.wait_ge(gp_r, n + 1)
                        for m, (banks, s) in enumerate(((GB, g_mm), (UB, u_mm))):
                            split_product(pe, banks[par][:, :],
                                          [[w13[m][:, a, c2, ds(ch * P, P)] for a in range(2)] for c2 in range(DC)],
                                          [[xT[:, a, c2, ds(b * T, T)] for a in range(2)] for c2 in range(DC)],
                                          True, True).then_inc(s, 1)
                        for a in range(2):
                            mm = pe.matmul(CB[par][:, :], sel[:, ds(ch * P, P)], share[:, a, ds(b * T, T)],
                                           start=a == 0, stop=a == 1, skip_group_check=True)
                        mm.then_inc(c_mm, 1)
                        if not first:
                            down(ch - 1, n - 1, 1 - par)

                    chunks(pe, b, item)
                    down(NCH1 - 1, b * NCH1 + NCH1 - 1, 0)

            @block.scalar
            def _(act):
                with act.Fori(0, B) as b:
                    def item(ch, n, par, first):
                        if first:
                            act.wait_ge(e_b, b * 2 + 2)
                        act.wait_ge(g_mm, n + 1)
                        act.activation(gt[:, par, :], GB[par][:, :], ACT.Tanh, scale=0.5).then_inc(gt_r, 1)
                        act.wait_ge(gp_r, n + 3)
                        act.wait_ge(d_mm, n + 1)
                        act.activation(hT[:, par, 0, :], gp[:, par, :], ACT.Copy).then_inc(h_hi, 1)

                    def qk_high(q):
                        act.wait_ge(qk_loaded, b * 16 + 16)
                        act.activation(wqk[:, ds(b, 1), 0, ds(q * T, T)].rearrange("p m n -> p (m n)"),
                                       stage[:, ds(q * T, T)], ACT.Copy).then_inc(qk_hi, 1)

                    chunks(act, b, item, qk_high)
                    act.wait_ge(d_mm, b * NCH1 + NCH1 + 2)
                    for i in range(2):
                        act.activation(et[:, i, :], FB[i][:, :], ACT.Tanh, scale=0.5).then_inc(e_t, 1)
            @block.gpsimd
            def _(pool):
                for s, credit in ((gp_r, 2), (h_lo, 2), (d_mm, 2), (e_b, 2), (qk_lo, 1)):
                    pool.sem_inc(s, credit)
                with pool.Fori(0, B) as b:
                    def item(ch, n, par, first):
                        pool.wait_ge(gp_r, n + 3)
                        pool.wait_ge(h_hi, n + 1)
                        pool.tensor_tensor(hT[:, par, 1, :], gp[:, par, :], hT[:, par, 0, :],
                                           ALU.subtract).then_inc(h_lo, 1)

                    chunks(pool, b, item)

            @block.vector
            def _(dve):
                with dve.Fori(0, B) as b:
                    def item(ch, n, par, first):
                        dve.wait_ge(gt_r, n + 1)
                        dve.scalar_tensor_tensor(out=gb[:, par, :], in0=gt[:, par, :], scalar=1.0, in1=GB[par][:, :],
                                                 op0=ALU.add, op1=ALU.mult).then_inc(gb_r, 1)
                        dve.wait_ge(u_mm, n + 1)
                        dve.wait_ge(gb_r, n + 1)
                        dve.scalar_tensor_tensor(out=gt[:, par, :], in0=gb[:, par, :], scalar=0.5, in1=UB[par][:, :],
                                                 op0=ALU.mult, op1=ALU.mult).then_inc(gu_r, 1)
                        dve.wait_ge(c_mm, n + 1)
                        dve.wait_ge(gu_r, n + 1)
                        dve.wait_ge(h_lo, n + 1)
                        dve.tensor_tensor(gp[:, par, :], gt[:, par, :], CB[par][:, :], ALU.mult).then_inc(gp_r, 1)

                    def qk_low(q):
                        dve.wait_ge(qk_hi, b * 4 + q + 1)
                        part = [wqk[:, ds(b, 1), a, ds(q * T, T)].rearrange("p m n -> p (m n)") for a in range(2)]
                        dve.tensor_tensor(part[1], stage[:, ds(q * T, T)], part[0], ALU.subtract).then_inc(qk_lo, 1)

                    chunks(dve, b, item, qk_low)
                    for i in range(2):
                        dve.wait_ge(e_t, b * 2 + i + 1)
                        dve.scalar_tensor_tensor(out=eb[:, i, :], in0=et[:, i, :], scalar=1.0, in1=FB[i][:, :],
                                                 op0=ALU.add, op1=ALU.mult).then_inc(e_b, 1)
                        dve.wait_ge(e_b, b * 2 + i + 3)
                        dve.tensor_scalar(gate[:, ds(b * TPB + 2 * i, 2), :].rearrange("p t d -> p (t d)"), eb[:, i, :],
                                          0.5, None, ALU.mult).then_inc(e_g, 1)


def route(nc, A, xT, wg, bias, sel, ident, share, psum, second):
    with ExitStack() as c:
        sb = lambda n, s, d: c.enter_context(nc.sbuf_tensor("r_" + n, s, d))
        sem = lambda n: c.enter_context(nc.semaphore("r_" + n))
        score, biased, masked = sb("score", [P, NT, E], F32), sb("biased", [P, NT, E], F32), sb("masked", [P, NT, E], F32)
        gmax, grank, gsel = (sb(n, [P, NT, G], F32) for n in ("gmax", "grank", "gsel"))
        gcmp, geq = sb("gcmp", [P, NT, G, G], F16), sb("geq", [P, NT, G, G], F16)
        cmp_, eq = sb("cmp", [P, NT, E, E], F16), sb("eq", [P, NT, E, E], F16)
        lower_g, lower_e = sb("lower_g", [P, G, G], F16), sb("lower_e", [P, E, E], F16)
        rank, total = sb("rank", [P, NT, E], F32), sb("total", [P, NT], F32)
        parts = sb("parts", [P, 2, NT, E], F16)
        logits_done, tanh_done, low_made, chain = sem("logits"), sem("tanh"), sem("lower"), sem("chain")
        turned, copied, other = sem("turned"), sem("copied"), sem("other")
        LOG = psum[0]
        TQ = psum[1:5]

        with nc.Block() as block:
            @block.sync
            def _(sp):
                sp.dma_start(bias[:, :], A["expert_bias"].broadcast_to([P, E])).then_inc(other, 16)
                sp.dma_start(sel[:, :], A["sel"]).then_inc(other, 16)
                for w in second:
                    w.load(sp)

            @block.tensor
            def _(pe):
                for t in range(NT):
                    mm = split_product(pe, LOG[:, t * E:(t + 1) * E],
                                       [[xT[:, a, c2, t * P:(t + 1) * P] for a in range(2)] for c2 in range(DC)],
                                       [[wg[:, a, c2, :] for a in range(2)] for c2 in range(DC)], True, True)
                mm.then_inc(logits_done, 1)
                pe.wait_ge(copied, 1)
                for a in range(2):
                    for t in range(NT):
                        mm = pe.transpose(TQ[a * 2 + t // 8][:, :].bitcast(F16)[0:E, (t % 8) * P:(t % 8 + 1) * P],
                                          parts[:, a, t, :], ident[:, :])
                    mm.then_inc(turned, 1)

            @block.scalar
            def _(act):
                act.wait_ge(logits_done, 1)
                act.activation(score[:, :, :].rearrange("p t e -> p (t e)"), LOG[:, 0:NT * E], ACT.Tanh,
                               scale=0.5).then_inc(tanh_done, 1)
                for w in second:
                    w.high(act)

            @block.gpsimd
            def _(pool):
                for m, n in ((lower_g, G), (lower_e, E)):
                    pool.memset(m[:, :, :], 1.0).then_inc(low_made, 1)
                pool.wait_ge(low_made, 2)
                for m, n in ((lower_g, G), (lower_e, E)):
                    pool.affine_select(out=m[:, :, :], in_=m[:, :, :], compare_op=ALU.is_gt, fill=0.0, base=0,
                                       pattern=[[1, n], [-1, n]], channel_multiplier=0).then_inc(low_made, 1)
                pool.memset(share[:, 0, :], 1.0).then_inc(low_made, 1)
                pool.memset(share[:, 1, :], 0.0).then_inc(low_made, 1)
                for w in second:
                    w.low(pool)

            @block.vector
            def _(dve):
                step = Count(chain)

                def do(ins):
                    step(ins)
                    step.wait(dve)

                dve.wait_ge(tanh_done, 1)
                dve.wait_ge(low_made, 6)
                dve.wait_ge(other, 32)
                do(dve.tensor_scalar(score[:, :, :], score[:, :, :], 1.0, 0.5, ALU.add, ALU.mult))
                bias_t = bias[:, :].rearrange("p (a e) -> p a e", a=1).broadcast_to([P, NT, E])
                do(dve.tensor_tensor(biased[:, :, :], score[:, :, :], bias_t, ALU.add))
                do(dve.tensor_reduce(gmax[:, :, :], biased[:, :, :].rearrange("p t (g e) -> p t g e", g=G),
                                     axis=AX.X, op=ALU.max))

                def ranks(value, n, lower, cmp_, eq, rank):
                    mine = value.rearrange("p t (e a) -> p t e a", a=1).broadcast_to([P, NT, n, n])
                    other = value.rearrange("p t (a e) -> p t a e", a=1).broadcast_to([P, NT, n, n])
                    low = lower[:, :, :].rearrange("p (a i) j -> p a i j", a=1).broadcast_to([P, NT, n, n])
                    do(dve.tensor_tensor(cmp_[:, :, :, :], other, mine, ALU.is_gt))
                    do(dve.tensor_tensor(eq[:, :, :, :], other, mine, ALU.is_equal))
                    do(dve.tensor_tensor(eq[:, :, :, :], eq[:, :, :, :], low, ALU.mult))
                    do(dve.tensor_tensor(cmp_[:, :, :, :], cmp_[:, :, :, :], eq[:, :, :, :], ALU.add))
                    do(dve.tensor_reduce(rank, cmp_[:, :, :, :], axis=AX.X, op=ALU.add))

                ranks(gmax[:, :, :], G, lower_g, gcmp, geq, grank[:, :, :])
                do(dve.tensor_scalar(gsel[:, :, :], grank[:, :, :], TOPK_G - 0.5, None, ALU.is_lt))
                sel_e = gsel[:, :, :].rearrange("p t (g a) -> p t g a", a=1).broadcast_to([P, NT, G, EG])
                as_groups = lambda ap: ap.rearrange("p t (g e) -> p t g e", g=G)
                do(dve.tensor_tensor(as_groups(masked[:, :, :]), as_groups(biased[:, :, :]), sel_e, ALU.mult))
                do(dve.tensor_scalar(gsel[:, :, :], gsel[:, :, :], 1.0, -MASKED, ALU.subtract, ALU.mult))
                do(dve.tensor_tensor(as_groups(masked[:, :, :]), as_groups(masked[:, :, :]), sel_e, ALU.add))
                ranks(masked[:, :, :], E, lower_e, cmp_, eq, rank[:, :, :])
                do(dve.tensor_scalar(rank[:, :, :], rank[:, :, :], TOPK - 0.5, None, ALU.is_lt))
                do(dve.tensor_tensor(score[:, :, :], score[:, :, :], rank[:, :, :], ALU.mult))
                do(dve.tensor_reduce(total[:, :], score[:, :, :], axis=AX.X, op=ALU.add))
                do(dve.reciprocal(total[:, :], total[:, :]))
                tot = total[:, :].rearrange("p (t a) -> p t a", a=1).broadcast_to([P, NT, E])
                do(dve.tensor_tensor(score[:, :, :], score[:, :, :], tot, ALU.mult))
                do(dve.tensor_copy(parts[:, 0, :, :], score[:, :, :]))
                dve.tensor_tensor(parts[:, 1, :, :], score[:, :, :], parts[:, 0, :, :], ALU.subtract).then_inc(copied, 1)
                for a in range(2):
                    dve.wait_ge(turned, a + 1)
                    for half in range(2):
                        dve.tensor_copy(share[0:E, a, half * 1024:(half + 1) * 1024],
                                        TQ[a * 2 + half][:, :].bitcast(F16)[0:E, :])


def attention1(nc, A, x, xT, ident, ident_b, causal, zeros, gate, wqk, psum):
    SC = HD1 ** -0.5
    NI = H1
    with ExitStack() as c:
        sb = lambda n, s, d: c.enter_context(nc.sbuf_tensor("a_" + n, s, d))
        sem = lambda n: c.enter_context(nc.semaphore("a_" + n))
        wv = sb("wv", [P, 2, DC, H1 * HD1], F16)
        wo = sb("wo", [P, 2, H1, D], F16)
        bq, bk, bv = (sb(n, [P, H1], F32) for n in ("bq", "bk", "bv"))
        bo = sb("bo", [P, D], F32)
        stages = [sb(f"stage{i}", [P, H1 * HD1], F32) for i in range(4)]
        v_split = [WeightSplit(nc, c, f"wv{cc}", A["wv1"][cc * P:(cc + 1) * P, :], stages[cc][:, :], wv[:, 0, cc, :],
                               wv[:, 1, cc, :]) for cc in range(DC)]
        o_split = [WeightSplit(nc, c, f"wo{hh}",
                               A["wo1"][hh * 1024:(hh + 1) * 1024, :].rearrange("(h p) d -> p h d", p=P),
                               stages[2 + hh][:, :].rearrange("p (h d) -> p h d", d=D),
                               wo[:, 0, hh * 8:hh * 8 + 8, :], wo[:, 1, hh * 8:hh * 8 + 8, :]) for hh in range(2)]

        qk = sb("qk", [P, 2, 2, 2, T], F16)
        vv = sb("vv", [P, 2, 2, TPB * P], F16)
        ex = sb("ex", [P, PW], F32)
        pn = sb("pn", [P, 2, 2, PW], F16)
        pt = sb("pt", [P, 2, 2 * PW], F16)
        nmax, nbias = sb("nmax", [P, TPB], F32), sb("nbias", [P, TPB], F32)
        rsum, rinv = sb("rsum", [P, TPB], F32), sb("rinv", [P, TPB], F32)
        xb = sb("xb", [P, 2, DC, T], F16)
        at = sb("at", [P, 2, 2, T], F16)
        fo = sb("fo", [P, 2, T], F32)
        SB, TB, JB, AO, FB = psum[0:2], psum[2], psum[3:5], psum[5], psum[6:8]
        TB16 = TB[:, :].bitcast(F16)
        p_mm = [sem(f"{n}_mm") for n in "qkv"]
        p_hi = [sem(f"{n}_hi") for n in "qkv"]
        p_lo = [sem(f"{n}_lo") for n in "qkv"]
        s_mm, bias_n, biased, exp_done = sem("s_mm"), sem("nmax_done"), sem("bias_ready"), sem("exp_done")
        recip, pn_hi, pn_lo = sem("recip"), sem("pn_hi"), sem("pn_lo")
        t_mm, t_ev, av_mm = sem("t_mm"), sem("t_evacuated"), sem("av_mm")
        ao_hi, ao_lo, wo_mm = sem("ao_hi"), sem("ao_lo"), sem("wo_mm")
        xb_ready = sem("xb_ready")
        biases = sem("biases_loaded")
        o_b, o_g, o_x, o_dma = sem("o_bias"), sem("o_gate"), sem("o_x"), sem("o_dma")

        def items(eng, b, last, item):
            def one(h, par, nxt, after):
                item(h, b * NI + h, par, h - 1, nxt, after)

            with eng.Fori(0, NI // 2 - 2) as i:
                for k in range(2):
                    h = i * 2 + k + 1
                    one(h, 1 - k, (b, h + 1), (b, h + 2))
            following = None if last else b + 1
            one(NI - 3, 1, (b, NI - 2), (b, NI - 1))
            one(NI - 2, 0, (b, NI - 1), None if last else (following, 0))
            one(NI - 1, 1, None if last else (following, 0), None if last else (following, 1))
            if not last:
                item(0, (b + 1) * NI, 0, NI - 1, (following, 1), (following, 2), ended=b)

        def turned(eng, n, par, j):
            _, col, w = TFILLS[j]
            eng.wait_ge(t_mm, n * 3 + j + 5)
            eng.wait_ge(av_mm, n + 1)
            if j < 2:
                eng.tensor_copy(pt[:, par, col:col + w], TB16[:, 0:w]).then_inc(t_ev, 1)
            else:
                eng.activation(pt[:, par, col:col + w], TB16[:, 0:w], ACT.Copy).then_inc(t_ev, 1)

        def per_batch(eng, item, body):
            item(0, 0, 0, None, (0, 1), (0, 2))
            with eng.Fori(0, B - 1) as b:
                body(b, False)
            body(B - 1, True)

        with nc.Block() as block:
            @block.gpsimd
            def _(pool):
                for s, credit in ((exp_done, 1), (pn_lo, 1), (t_mm, 4), (t_ev, 1), (av_mm, 2), (ao_lo, 1),
                                  (wo_mm, 2), (o_b, 2), (o_x, 2)):
                    pool.sem_inc(s, credit)
                with pool.Fori(0, B) as b:
                    for i in range(2):
                        pool.wait_ge(o_b, b * 2 + i + 3)
                        pool.tensor_tensor(fo[:, i, :], fo[:, i, :],
                                           gate[:, ds(b * TPB + 2 * i, 2), :].rearrange("p t d -> p (t d)"),
                                           ALU.mult).then_inc(o_g, 1)
                        pool.wait_ge(o_g, b * 2 + i + 1)
                        xv = x[:, ds(b * TPB + 2 * i, 2), :].rearrange("p t d -> p (t d)")
                        pool.tensor_tensor(xv, xv, fo[:, i, :], ALU.add).then_inc(o_x, 1)

            @block.sync
            def _(sp):
                for dst, name in ((bq, "bq1"), (bk, "bk1"), (bv, "bv1")):
                    sp.dma_start(dst[:, :], A[name]).then_inc(biases, 16)
                sp.dma_start(bo[:, :], A["bo1"].broadcast_to([P, D])).then_inc(biases, 16)
                for w in v_split:
                    w.load(sp)
                for w in v_split:
                    sp.wait_ge(w.loaded, 16)
                for w in o_split:
                    w.load(sp)
                with sp.Fori(0, B) as b:
                    for i in range(2):
                        sp.wait_ge(o_x, b * 2 + i + 3)
                        sp.dma_start(A["out"].rearrange("(t p) d -> p t d", p=P)[:, ds(b * TPB + 2 * i, 2), :],
                                     x[:, ds(b * TPB + 2 * i, 2), :]).then_inc(o_dma, 16)
                sp.wait_ge(o_dma, B * 2 * 16)

            @block.tensor
            def _(pe):
                def project(b, h, j, bank):
                    if j < 2:
                        mm = split_product(pe, bank[:, :],
                                           [[wqk[:, j * DC + c2, a, ds(h * P, P)] for a in range(2)] for c2 in range(DC)],
                                           [[xT[:, a, c2, ds(b * T, T)] for a in range(2)] for c2 in range(DC)],
                                           True, True)
                    else:
                        if starts_batch(h):
                            pe.wait_ge(xb_ready, b + 1)
                        for t in range(TPB):
                            mm = split_product(pe, bank[:, t * P:(t + 1) * P],
                                               [[xb[:, a, c2, t * P:(t + 1) * P] for a in range(2)] for c2 in range(DC)],
                                               [[wv[:, a, c2, ds(h * P, P)] for a in range(2)] for c2 in range(DC)],
                                               True, True)
                    mm.then_inc(p_mm[j], 1)

                def scores(n, j, par, first=False):
                    bank = SB[(par + j) % 2]
                    if not (first and j < 2):
                        pe.wait_ge(exp_done, n * 3 + j)
                    if j == 0:
                        pe.wait_ge(p_lo[0], n + 1)
                        pe.wait_ge(p_lo[1], n + 1)
                    at_col = 0
                    for i in ((3,), (2,), (1, 0))[j]:
                        w = (i + 1) * P
                        split_product(pe, bank[:, at_col:at_col + w],
                                      [[qk[:, par, 0, a, i * P:(i + 1) * P] for a in range(2)]],
                                      [[qk[:, par, 1, a, 0:w] for a in range(2)]], True, False)
                        mm = pe.matmul(bank[:, at_col + i * P:at_col + w], ident_b[:, :], causal[:, :], start=False,
                                       stop=True, skip_group_check=True)
                        at_col += w
                    mm.then_inc(s_mm, 1)

                def turn(n, j, par):
                    pe.wait_ge(t_ev, n * 3 + j + 1)
                    col = 0
                    for kb in TFILLS[j][0]:
                        for a in range(2):
                            for i in range(kb, TPB):
                                src = PCOL[i] + kb * P
                                mm = pe.transpose(TB16[:, col:col + P], pn[:, par, a, src:src + P], ident[:, :])
                                col += P
                    mm.then_inc(t_mm, 1)

                def weighted(n, par):
                    pe.wait_ge(ao_lo, n + 1)
                    pe.wait_ge(p_lo[2], n + 1)
                    for kb in range(TPB):
                        if kb < 3:
                            pe.wait_ge(t_ev, n * 3 + kb + 2)
                        c0, c1, w = KEYCOL[kb]
                        mm = split_product(pe, AO[:, kb * P:T], [[vv[:, par, a, kb * P:(kb + 1) * P] for a in range(2)]],
                                           [[pt[:, par, col:col + w] for col in (c0, c1)]], kb == 0, kb == 3)
                    mm.then_inc(av_mm, 1)

                def out_product(n, h, par):
                    pe.wait_ge(ao_lo, n + 2)
                    for t in range(TPB):
                        mm = split_product(pe, FB[t // 2][:, (t % 2) * D:(t % 2 + 1) * D],
                                           [[at[:, par, a, t * P:(t + 1) * P] for a in range(2)]],
                                           [[wo[:, a, ds(h, 1), :].rearrange("p a t -> p (a t)") for a in range(2)]],
                                           False, False)
                    mm.then_inc(wo_mm, 1)

                def item(h, n, par, before, nxt, after, ended=None):
                    q = 1 - par
                    if nxt:
                        scores(n + 1, 0, q)
                        scores(n + 1, 1, q)
                    if after:
                        pe.wait_ge(p_lo[1], n + 2)
                        project(*after, 0, JB[q])
                    pe.wait_ge(pn_lo, n + 2)
                    turn(n, 0, par)
                    if after:
                        pe.wait_ge(p_lo[2], n + 1)
                        project(*after, 1, JB[par])
                    turn(n, 1, par)
                    if nxt:
                        scores(n + 1, 2, q)
                    if before is not None:
                        out_product(n - 1, before, q)
                    turn(n, 2, par)
                    if nxt:
                        if after:
                            pe.wait_ge(p_lo[0], n + 3)
                        project(*nxt, 2, JB[q])
                    weighted(n, par)

                def batch(b, last):
                    pe.wait_ge(o_b, b * 2 + 2)
                    for f in range(2):
                        pe.matmul(FB[f][:, :], zeros[:, :], xT[:, 0, 0, 0:T], start=True, stop=False,
                                  skip_group_check=True)
                    items(pe, b, last, item)
                    if last:
                        out_product(b * NI + NI - 1, NI - 1, 1)

                for h in range(2):
                    for j in range(2):
                        if h:
                            pe.wait_ge(p_lo[j], 1)
                        project(0, h, j, JB[j])
                for j in range(3):
                    scores(0, j, 0, first=True)
                pe.wait_ge(p_lo[0], 2)
                for w in v_split:
                    pe.wait_ge(w.lo_done, 1)
                project(0, 0, 2, JB[0])
                for w in o_split:
                    pe.wait_ge(w.lo_done, 1)
                per_batch(pe, item, batch)

            def softmax_exp(act, n, par, js):
                for j in js:
                    col = 0
                    act.wait_ge(biased, n * 3 + j + 1)
                    if j == 0:
                        act.wait_ge(pn_lo, n + 1)
                    for i in ((3,), (2,), (1, 0))[j]:
                        w = (i + 1) * P
                        ins = act.activation(ex[:, PCOL[i]:PCOL[i] + w], SB[(par + j) % 2][:, col:col + w], ACT.Exp,
                                             bias=nbias[:, i:i + 1], scale=SC, accum_out=rsum[:, i:i + 1])
                        col += w
                    ins.then_inc(exp_done, 1)

            @block.scalar
            def _(act):
                def high(n, h, j, bank, par):
                    act.wait_ge(p_mm[j], n + 1)
                    if j < 2:
                        act.activation(qk[:, par, j, 0, :], bank[:, :], ACT.Identity,
                                       bias=(bq, bk)[j][:, ds(h, 1)]).then_inc(p_hi[j], 1)
                    else:
                        act.wait_ge(av_mm, n + 1)
                        act.activation(vv[:, par, 0, :], bank[:, :], ACT.Copy).then_inc(p_hi[j], 1)

                def probs_hi(n, par, blocks):
                    act.wait_ge(recip, n + 1)
                    act.wait_ge(exp_done, n * 3 + 4)
                    act.wait_ge(t_mm, n * 3 + 1)
                    for i in blocks:
                        act.activation(pn[:, par, 0, PCOL[i]:PCOL[i] + (i + 1) * P],
                                       ex[:, PCOL[i]:PCOL[i] + (i + 1) * P], ACT.Copy,
                                       scale=rinv[:, i:i + 1]).then_inc(pn_hi, 1)

                def item(h, n, par, before, nxt, after, ended=None):
                    q = 1 - par
                    if nxt:
                        softmax_exp(act, n + 1, q, (0,))
                        softmax_exp(act, n + 1, q, (1,))
                    if after:
                        high(n + 2, after[1], 0, JB[q], par)
                        high(n + 2, after[1], 1, JB[par], par)
                    if nxt:
                        softmax_exp(act, n + 1, q, (2,))
                    turned(act, n, par, 2)
                    if nxt:
                        probs_hi(n + 1, q, range(TPB))
                        high(n + 1, nxt[1], 2, JB[q], q)
                    act.wait_ge(av_mm, n + 3)
                    act.wait_ge(wo_mm, n + 1)
                    act.activation(at[:, par, 0, :], AO[:, :], ACT.Identity, bias=bv[:, ds(h, 1)]).then_inc(ao_hi, 1)

                act.wait_ge(biases, 64)
                for h in range(2):
                    for j in range(2):
                        high(h, h, j, JB[j], h)
                softmax_exp(act, 0, 0, (0, 1, 2))
                for w in v_split:
                    w.high(act)
                probs_hi(0, 0, range(TPB))
                high(0, 0, 2, JB[0], 0)
                for w in o_split:
                    w.high(act)
                per_batch(act, item, lambda b, last: items(act, b, last, item))

            @block.vector
            def _(dve):
                def low(n, h, j, bank, par):
                    dve.wait_ge(p_hi[j], n + 1)
                    if j < 2:
                        dve.scalar_tensor_tensor(out=qk[:, par, j, 1, :], in0=bank[:, :], scalar=(bq, bk)[j][:, ds(h, 1)],
                                                 in1=qk[:, par, j, 0, :], op0=ALU.add, op1=ALU.subtract).then_inc(p_lo[j], 1)
                    else:
                        dve.tensor_tensor(vv[:, par, 1, :], bank[:, :], vv[:, par, 0, :], ALU.subtract).then_inc(p_lo[j], 1)

                def maxima(n, par, j):
                    dve.wait_ge(s_mm, n * 3 + j + 1)
                    if j == 0:
                        dve.wait_ge(exp_done, n * 3 + 1)
                    blocks = ((3,), (2,), (1, 0))[j]
                    col = 0
                    for i in blocks:
                        w = (i + 1) * P
                        ins = dve.tensor_reduce(nmax[:, i:i + 1], SB[(par + j) % 2][:, col:col + w], axis=AX.X,
                                                op=ALU.max, negate=True)
                        col += w
                    ins.then_inc(bias_n, 1)
                    dve.wait_ge(bias_n, n * 3 + j + 1)
                    lo, hi = blocks[-1], blocks[0] + 1
                    dve.tensor_scalar(nbias[:, lo:hi], nmax[:, lo:hi], SC, None, ALU.mult).then_inc(biased, 1)

                def reciprocals(n):
                    dve.wait_ge(exp_done, n * 3 + 4)
                    dve.reciprocal(rinv[:, :], rsum[:, :]).then_inc(recip, 1)

                def probs_lo(n, par):
                    dve.wait_ge(recip, n + 1)
                    for i in range(TPB):
                        dve.wait_ge(pn_hi, n * TPB + i + 1)
                        s = slice(PCOL[i], PCOL[i] + (i + 1) * P)
                        ins = dve.scalar_tensor_tensor(out=pn[:, par, 1, s], in0=ex[:, s], scalar=rinv[:, i:i + 1],
                                                       in1=pn[:, par, 0, s], op0=ALU.mult, op1=ALU.subtract)
                    ins.then_inc(pn_lo, 1)

                def batch_rows(b):
                    bo2 = bo[:, :].rearrange("p (a d) -> p a d", a=1).broadcast_to([P, 2, D])
                    dve.wait_ge(wo_mm, b * NI + NI + 2)
                    for i in range(2):
                        dve.wait_ge(o_x, b * 2 + i + 1)
                        dve.tensor_tensor(fo[:, i, :].rearrange("p (a d) -> p a d", a=2),
                                          FB[i][:, :].rearrange("p (a d) -> p a d", a=2), bo2, ALU.add).then_inc(o_b, 1)

                def output_lo(n, h, par):
                    dve.wait_ge(ao_hi, n + 1)
                    dve.scalar_tensor_tensor(out=at[:, par, 1, :], in0=AO[:, :], scalar=bv[:, ds(h, 1)],
                                             in1=at[:, par, 0, :], op0=ALU.add, op1=ALU.subtract).then_inc(ao_lo, 1)

                def batch_tokens(b, n):
                    if n is not None:
                        dve.wait_ge(p_mm[2], n + 1)
                    dve.tensor_copy(xb[:, :, :, :], xT[:, :, :, ds(b * T, T)]).then_inc(xb_ready, 1)

                def item(h, n, par, before, nxt, after, ended=None):
                    q = 1 - par
                    if nxt and starts_batch(nxt[1]):
                        batch_tokens(nxt[0], n)
                    if nxt:
                        maxima(n + 1, q, 0)
                        maxima(n + 1, q, 1)
                    turned(dve, n, par, 0)
                    if before is not None:
                        output_lo(n - 1, before, q)
                    if after:
                        low(n + 2, after[1], 0, JB[q], par)
                    turned(dve, n, par, 1)
                    if nxt:
                        maxima(n + 1, q, 2)
                    if after:
                        low(n + 2, after[1], 1, JB[par], par)
                    if nxt:
                        reciprocals(n + 1)
                    if ended is not None:
                        batch_rows(ended)
                    if nxt:
                        probs_lo(n + 1, q)
                        low(n + 1, nxt[1], 2, JB[q], q)

                def batch(b, last):
                    items(dve, b, last, item)
                    if last:
                        output_lo(b * NI + NI - 1, NI - 1, 1)
                        batch_rows(b)

                batch_tokens(0, None)
                dve.wait_ge(biases, 64)
                for h in range(2):
                    for j in range(2):
                        low(h, h, j, JB[j], h)
                for j in range(3):
                    maxima(0, 0, j)
                for w in v_split:
                    w.low(dve)
                reciprocals(0)
                probs_lo(0, 0)
                low(0, 0, 2, JB[0], 0)
                for w in o_split:
                    w.low(dve)
                per_batch(dve, item, batch)


_OUT = (B, T, D)


def kernel(**inputs):
    import concourse.bacc as bacc
    from concourse.bass_utils import run_bass_kernel_spmd

    i = {k: np.asarray(v) for k, v in inputs.items()}

    def halves(w):
        return np.concatenate([w[0::2], w[1::2]], axis=0)

    def fp4(name):
        codes, scales = i[f"L0_ffn_{name}_W_packed"], i[f"L0_ffn_{name}_scales"]
        if name == "down":
            c = codes.T.reshape(8, P, D).transpose(1, 0, 2)
            s = np.repeat(scales.T.reshape(8, 8, D), 16, axis=1).transpose(1, 0, 2)
        else:
            order = np.arange(MLP).reshape(8, P, 2).transpose(0, 2, 1).reshape(-1)
            c = codes.T[:, order]
            s = np.repeat(scales.T[:, order], 16, axis=0)
        return c.reshape(P, MLP), s.reshape(P, MLP)

    host = {"x": i["L0_attn_x"].reshape(TOK, D)}
    host["wqkv0"] = halves(np.concatenate([i[f"L0_attn_W{n}"].T for n in "qkv"], axis=1))
    host["wo0"] = np.repeat(i["L0_attn_Wo"].T.reshape(4, 4, 1, HD0, D), 2, axis=2).reshape(4, P, D)
    host["bo0"] = i["L0_attn_bo"].reshape(1, D)
    for m, name in enumerate(("gate", "up", "down")):
        host[f"codes{m}"], host[f"scales{m}"] = fp4(name)
    host["wqk1"] = np.concatenate([i["L1_attn_w_q"], i["L1_attn_w_k"]])
    host["wv1"] = i["L1_attn_w_v"]
    for n in "qkv":
        host[f"b{n}1"] = i[f"L1_attn_b_{n}"].reshape(H1, HD1).T
    host["wo1"] = i["L1_attn_w_o"]
    host["bo1"] = i["L1_attn_b_o"].reshape(1, D)
    host["gate_w"] = i["L1_ffn_gate_w"].T
    host["expert_bias"] = i["L1_ffn_expert_bias"].reshape(1, E)
    pad = HID1 - E * INTER - SHARED
    for m, (w, s) in enumerate((("w1", "sw1"), ("w3", "sw3"))):
        host[f"w{m}"] = np.concatenate([i[f"L1_ffn_{w}"].transpose(1, 0, 2).reshape(D, E * INTER), i[f"L1_ffn_{s}"],
                                        np.zeros((D, pad), np.float32)], axis=1)
    host["w2"] = np.concatenate([i["L1_ffn_w2"].reshape(E * INTER, D), i["L1_ffn_sw2"], np.zeros((pad, D), np.float32)])
    owner = np.minimum(np.arange(HID1) // INTER, E)
    host["sel"] = (owner[None, :] == np.arange(E + 1)[:, None]).astype(np.float16)

    nc = bacc.Bacc("TRN2", target_bir_lowering=False, num_devices=1)
    arrays, aps = {}, {}
    for name, a in host.items():
        arrays[f"in_{name}"] = np.ascontiguousarray(a)
        aps[name] = nc.dram_tensor(f"in_{name}", a.shape, mybir.dt.from_np(a.dtype), kind="ExternalInput").ap()
    aps["out"] = nc.dram_tensor("out_x", (TOK, D), F32, kind="ExternalOutput").ap()
    network(nc, aps)
    r = run_bass_kernel_spmd(nc, [arrays], core_ids=[0])
    return r.results[0]["out_x"].reshape(_OUT)
```
